# Optimizing a Trainium2 kernel written in Bass

```python
import numpy as np
import jax
import jax.numpy as jnp

def _softmax(x, axis=-1):
    return jax.nn.softmax(x, axis=axis)

def _gelu(x):
    return jax.nn.gelu(x, approximate=True)

def _silu(x):
    return jax.nn.silu(x)

def _sigmoid(x):
    return jax.nn.sigmoid(x)

def _layernorm(x, axis=-1, eps=1e-05):
    m = jnp.mean(x, axis=axis, keepdims=True)
    v = jnp.var(x, axis=axis, keepdims=True)
    return (x - m) / jnp.sqrt(v + eps)

def _scatter_add(tgt, idx, src, axis=0):
    return tgt.at[idx].add(src)

def _segment_sum(src, seg, n):
    return jax.ops.segment_sum(src, seg, n)
kernel_name = 'mk_flamingo_gated_d2_seqx_r4_9e074a'

def setup_inputs(seed: int=0):
    np.random.seed(seed)
    _w = jnp.asarray

    def _rec_inputs():
        import jax
        import jax.numpy as jnp
        _rk = jax.random.key(seed)
        x = -0.0002928 + 1 * jax.random.normal(jax.random.fold_in(_rk, 1), (8, 256, 256), jnp.float32)
        _lenS = 256 - jax.random.randint(jax.random.fold_in(_rk, 7), (8,), 0, max(1, 256 // 4) + 1, jnp.int32)
        _lenS2 = 256 - jax.random.randint(jax.random.fold_in(_rk, 8), (8,), 0, max(1, 256 // 4) + 1, jnp.int32)
        _ctx_1024P = jax.random.normal(jax.random.fold_in(_rk, 11), (8, 16, 256), jnp.float32)
        _ctx_1024c = jax.random.dirichlet(jax.random.fold_in(_rk, 511), 0.3 * jnp.ones((16,), jnp.float32), (8, 256))
        _ctx_1024t = jnp.einsum('bsk,bkd->bsd', _ctx_1024c, _ctx_1024P)
        _ctx_1024t = _ctx_1024t * jax.lax.rsqrt(jnp.mean(jnp.square(_ctx_1024t)) + 1e-12) * 0.953939
        ctx_1024 = -1.39393e-06 + 0.999914 * (_ctx_1024t + 0.3 * jax.random.normal(jax.random.fold_in(_rk, 611), (8, 256, 256), jnp.float32))
        _validS = jnp.arange(256)[None, :] < _lenS[:, None]
        _validS2 = jnp.arange(256)[None, :] < _lenS2[:, None]
        _causal = jnp.tril(jnp.ones((256, 256), dtype=bool))
        mask_BxS2_ik0 = jnp.where(jnp.broadcast_to(_validS2[:, :], (8, 256)), 0, 1).astype(jnp.int32)
        _g = jax.random.normal(jax.random.fold_in(_rk, 9001), (2, 2), jnp.float32)
        _g = jnp.sign(_g) * jnp.maximum(jnp.abs(_g), 1.0) + (_g == 0) * 1.0
        g_xattn = _g[0]
        g_ffn = _g[1]
        return (x, ctx_1024, mask_BxS2_ik0, g_xattn, g_ffn)
    x, ctx_1024, mask_BxS2_ik0, g_xattn, g_ffn = _rec_inputs()

    def _L0_xattn_setup():
        import jax, jax.numpy as jnp
        import numpy as np
        B, SQ, SKV, D, H = (2, 512, 512, 256, 16)
        W = D // H

        def _heads(x):
            b, s, _ = x.shape
            return x.reshape(b, s, H, W).transpose(0, 2, 1, 3)
        key = jax.random.key(seed)
        ks = jax.random.split(key, 10)
        s = 1.0 / np.sqrt(D)
        return {'x_q': jax.random.normal(ks[0], (B, SQ, D), jnp.float32), 'x_k': jax.random.normal(ks[1], (B, SKV, D), jnp.float32), 'x_v': jax.random.normal(ks[2], (B, SKV, D), jnp.float32), 'mask': jax.random.randint(ks[3], (B, SKV), 0, 2, jnp.int32), 'Wq': jax.random.normal(ks[4], (D, D), jnp.float32) * s, 'bq': jnp.zeros((D,), jnp.float32), 'Wk': jax.random.normal(ks[5], (D, D), jnp.float32) * s, 'bk': jnp.zeros((D,), jnp.float32), 'Wv': jax.random.normal(ks[6], (D, D), jnp.float32) * s, 'bv': jnp.zeros((D,), jnp.float32)}
    _L0_xattn_all = _L0_xattn_setup()
    _L0_xattn_in = {k: v for k, v in _L0_xattn_all.items() if k in ('Wq', 'bq', 'Wk', 'bk', 'Wv', 'bv')}
    del _L0_xattn_all

    def _L0_ffn_setup():
        import jax, jax.numpy as jnp
        import numpy as np
        CAPACITY = 2
        B, S, D, E, I = (4, 1024, 256, 8, 1024)
        key = jax.random.key(seed)
        k0, k1, k2, k3, k4 = jax.random.split(key, 5)
        x = jax.random.normal(k0, (B, S, D), dtype=jnp.float32)
        gate_w = jax.random.normal(k1, (E, D), dtype=jnp.float32) * 0.006
        w_gate = jax.random.normal(k2, (E, I, D), dtype=jnp.float32) * (1.0 / np.sqrt(D))
        w_up = jax.random.normal(k3, (E, I, D), dtype=jnp.float32) * (1.0 / np.sqrt(D))
        w_down = jax.random.normal(k4, (E, D, I), dtype=jnp.float32) * (1.0 / np.sqrt(I))
        return {'x': x, 'gate_w': gate_w, 'w_gate': w_gate, 'w_up': w_up, 'w_down': w_down}
    _L0_ffn_all = _L0_ffn_setup()
    _L0_ffn_in = {k: v for k, v in _L0_ffn_all.items() if k in ('gate_w', 'w_gate', 'w_up', 'w_down')}
    del _L0_ffn_all

    def _L1_xattn_setup():
        import jax, jax.numpy as jnp
        import numpy as np
        NUM_HEADS = 16
        key = jax.random.key(seed)
        kq, kk, kv = jax.random.split(key, 3)
        B, S, E = (4, 512, 256)
        Q = jax.random.normal(kq, (B, S, E), dtype=jnp.float32)
        K = jax.random.normal(kk, (B, S, E), dtype=jnp.float32)
        V = jax.random.normal(kv, (B, S, E), dtype=jnp.float32)
        return {'Q': Q, 'K': K, 'V': V}
    _L1_xattn_all = _L1_xattn_setup()
    _L1_xattn_in = {k: v for k, v in _L1_xattn_all.items() if k in ()}
    del _L1_xattn_all

    def _L1_ffn_setup():
        import jax, jax.numpy as jnp
        import numpy as np
        B, T, C, H, E, K = (4, 256, 256, 256, 8, 2)

        def _swiglu(x):
            a, b = jnp.split(x, 2, axis=-1)
            return jax.nn.silu(a) * b
        key = jax.random.key(seed)
        ks = jax.random.split(key, 6)
        s = 0.02
        x = jax.random.normal(ks[0], (B, T, C), jnp.float32)
        w_shared_in = jax.random.normal(ks[1], (C, 2 * H), jnp.float32) * s
        w_shared_out = jax.random.normal(ks[2], (H, C), jnp.float32) * s
        w1_shared = jax.random.normal(ks[3], (C, 2 * H), jnp.float32) * s
        w2 = jax.random.normal(ks[4], (E, H, C), jnp.float32) * s
        w_gate = jax.random.normal(ks[5], (C, E), jnp.float32) * s
        gate_bias = jnp.zeros((E,), jnp.float32)
        return {'x': x, 'w_shared_in': w_shared_in, 'w_shared_out': w_shared_out, 'w1_shared': w1_shared, 'w2': w2, 'w_gate': w_gate, 'gate_bias': gate_bias}
    _L1_ffn_all = _L1_ffn_setup()
    _L1_ffn_in = {k: v for k, v in _L1_ffn_all.items() if k in ('w_shared_in', 'w_shared_out', 'w1_shared', 'w2', 'w_gate', 'gate_bias')}
    del _L1_ffn_all
    return {'x': x, 'ctx_1024': ctx_1024, 'mask_BxS2_ik0': mask_BxS2_ik0, 'g_xattn': g_xattn, 'g_ffn': g_ffn, 'L0_xattn_Wq': _L0_xattn_in['Wq'], 'L0_xattn_bq': _L0_xattn_in['bq'], 'L0_xattn_Wk': _L0_xattn_in['Wk'], 'L0_xattn_bk': _L0_xattn_in['bk'], 'L0_xattn_Wv': _L0_xattn_in['Wv'], 'L0_xattn_bv': _L0_xattn_in['bv'], 'L0_ffn_gate_w': _L0_ffn_in['gate_w'], 'L0_ffn_w_gate': _L0_ffn_in['w_gate'], 'L0_ffn_w_up': _L0_ffn_in['w_up'], 'L0_ffn_w_down': _L0_ffn_in['w_down'], 'L1_ffn_w_shared_in': _L1_ffn_in['w_shared_in'], 'L1_ffn_w_shared_out': _L1_ffn_in['w_shared_out'], 'L1_ffn_w1_shared': _L1_ffn_in['w1_shared'], 'L1_ffn_w2': _L1_ffn_in['w2'], 'L1_ffn_w_gate': _L1_ffn_in['w_gate'], 'L1_ffn_gate_bias': _L1_ffn_in['gate_bias']}

def reference(x, ctx_1024, mask_BxS2_ik0, g_xattn, g_ffn, L0_xattn_Wq, L0_xattn_bq, L0_xattn_Wk, L0_xattn_bk, L0_xattn_Wv, L0_xattn_bv, L0_ffn_gate_w, L0_ffn_w_gate, L0_ffn_w_up, L0_ffn_w_down, L1_ffn_w_shared_in, L1_ffn_w_shared_out, L1_ffn_w1_shared, L1_ffn_w2, L1_ffn_w_gate, L1_ffn_gate_bias):
    import jax
    import jax.numpy as jnp

    def _L0_xattn_ref(x_q, x_k, x_v, mask, Wq, bq, Wk, bk, Wv, bv):
        import jax, jax.numpy as jnp
        import numpy as np
        B, SQ, SKV, D, H = (2, 512, 512, 256, 16)
        W = D // H

        def _heads(x):
            b, s, _ = x.shape
            return x.reshape(b, s, H, W).transpose(0, 2, 1, 3)
        q = _heads(x_q @ Wq.T + bq)
        k = _heads(x_k @ Wk.T + bk)
        v = _heads(x_v @ Wv.T + bv)
        scores = jnp.einsum('bhqw,bhkw->bhqk', q, k) / np.sqrt(W).astype(np.float32)
        m = mask[:, None, None, :].astype(scores.dtype)
        scores = scores - 10000.0 * (1.0 - m)
        p = jax.nn.softmax(scores, axis=-1)
        h = jnp.einsum('bhqk,bhkw->bhqw', p, v)
        return h.transpose(0, 2, 1, 3).reshape(x_q.shape[0], x_q.shape[1], D)

    def _L0_ffn_ref(x, gate_w, w_gate, w_up, w_down):
        import jax, jax.numpy as jnp
        import numpy as np
        CAPACITY = 2
        B, S, D = x.shape
        E = gate_w.shape[0]
        k = S // E * CAPACITY
        logits = jnp.einsum('bsd,ed->bse', x, gate_w)
        affinity = jax.nn.softmax(logits, axis=-1)
        affinity = jnp.transpose(affinity, (0, 2, 1))
        gating, idx = jax.lax.top_k(affinity, k)
        bidx = jnp.arange(B)[:, None, None]
        x_in = x[bidx, idx]
        h = jax.nn.silu(jnp.einsum('bekd,eid->beki', x_in, w_gate)) * jnp.einsum('bekd,eid->beki', x_in, w_up)
        x_e = jnp.einsum('beki,edi->bekd', h, w_down)
        out = jnp.zeros_like(x).at[bidx, idx].add(gating[..., None] * x_e)
        return out

    def _L1_xattn_ref(Q, K, V):
        import jax, jax.numpy as jnp
        import numpy as np
        NUM_HEADS = 16
        B, S, E = Q.shape
        H = NUM_HEADS
        d_k = E // H
        q = Q.reshape(B, S, H, d_k).transpose(0, 2, 1, 3)
        k = K.reshape(B, S, H, d_k).transpose(0, 2, 1, 3)
        v = V.reshape(B, S, H, d_k).transpose(0, 2, 1, 3)
        scale = 1.0 / np.sqrt(d_k).astype(np.float32)
        scores = jnp.einsum('bhqd,bhkd->bhqk', q, k) * scale
        causal_mask = jnp.tril(jnp.ones((S, S), dtype=bool))
        scores = jnp.where(causal_mask, scores, jnp.finfo(scores.dtype).min)
        attn = jax.nn.softmax(scores, axis=-1)
        out = jnp.einsum('bhqk,bhkd->bhqd', attn, v)
        return out.transpose(0, 2, 1, 3).reshape(B, S, E)

    def _L1_ffn_ref(x, w_shared_in, w_shared_out, w1_shared, w2, w_gate, gate_bias):
        import jax, jax.numpy as jnp
        import numpy as np
        B, T, C, H, E, K = (4, 256, 256, 256, 8, 2)

        def _swiglu(x):
            a, b = jnp.split(x, 2, axis=-1)
            return jax.nn.silu(a) * b
        Bx, Tx, Cx = x.shape
        S = Bx * Tx
        fx = x.reshape(S, Cx)
        shared_out = _swiglu(fx @ w_shared_in) @ w_shared_out
        logits = fx @ w_gate + gate_bias
        probs = jax.nn.softmax(logits, axis=-1)
        top_val, top_idx = jax.lax.top_k(probs, K)
        wdense = jnp.zeros((S, E), probs.dtype).at[jnp.arange(S)[:, None], top_idx].add(top_val)
        hid = _swiglu(fx @ w1_shared)
        routed_out = jnp.zeros_like(shared_out)
        for e in range(E):
            routed_out = routed_out + wdense[:, e:e + 1] * (hid @ w2[e])
        return (shared_out + routed_out).reshape(Bx, Tx, Cx)
    x = x + jnp.tanh(g_xattn[0]) * _L0_xattn_ref(_layernorm(x, axis=-1), ctx_1024, ctx_1024, mask_BxS2_ik0, L0_xattn_Wq, L0_xattn_bq, L0_xattn_Wk, L0_xattn_bk, L0_xattn_Wv, L0_xattn_bv)
    x = x + jnp.tanh(g_ffn[0]) * _L0_ffn_ref(_layernorm(x, axis=-1), L0_ffn_gate_w, L0_ffn_w_gate, L0_ffn_w_up, L0_ffn_w_down)
    x = x + jnp.tanh(g_xattn[1]) * _L1_xattn_ref(_layernorm(x, axis=-1), ctx_1024, ctx_1024)
    x = x + jnp.tanh(g_ffn[1]) * _L1_ffn_ref(_layernorm(x, axis=-1), L1_ffn_w_shared_in, L1_ffn_w_shared_out, L1_ffn_w1_shared, L1_ffn_w2, L1_ffn_w_gate, L1_ffn_gate_bias)
    return x

_drawn_inputs = setup_inputs


def setup_inputs(seed=0):
    import zlib

    import numpy as np

    out = dict(_drawn_inputs(seed))
    spreads = {'g_ffn': (-1.0, 0.6),
     'L0_xattn_bq': (0.0, 0.389),
     'L0_xattn_bk': (0.0, 0.8),
     'L0_xattn_bv': (0.0, 0.1),
     'L1_ffn_gate_bias': (0.0, 0.8)}
    factors = {'L1_ffn_w_shared_in': 4.374,
     'L1_ffn_w_shared_out': 4.386,
     'L1_ffn_w1_shared': 8.0,
     'L1_ffn_w2': 8.0,
     'L1_ffn_w_gate': 8.0}
    for name, (base, spread) in spreads.items():
        noise = np.random.default_rng([zlib.crc32(name.encode()), seed]).standard_normal(out[name].shape)
        drawn = base * np.exp(spread * noise) if base else spread * noise
        out[name] = jnp.asarray(drawn.astype(out[name].dtype))
    for name, factor in factors.items():
        out[name] = (out[name] * factor).astype(out[name].dtype)
    return out
```

```python
from contextlib import ExitStack

import concourse.bass as bass
from concourse import mybir

ALU = mybir.AluOpType
ACT = mybir.ActivationFunctionType
F32 = mybir.dt.float32
BF16 = mybir.dt.bfloat16
I32 = mybir.dt.int32
AX = mybir.AxisListType.X

P = 128
NB, S, D = 8, 256, 256
NH, W = 16, 16
TT = S // P
DT = D // P
NT = NB * TT
NE, I = 8, 1024
IT = I // P
CAP = S // NE * 2
SLOTS = NB * CAP
NPAIR = NE // 2
H1 = 256
NE1 = 8
EPS = 1e-5
SCALE = 0.25
NEG = -1.0e30

MASK0 = 6 * W
NMAX0 = MASK0 + 3
ROWS_A = NMAX0
ROWS_B = NMAX0 + 3


class Count:

    def __init__(self, sem, per, base=0):
        self.sem, self.per, self.base = sem, per, base

    def at(self, b, j=0):
        return b * self.per + (self.base + j + 1)


class Batch:

    def __init__(self, offset, turn=None, stride=2):
        self.offset, self.turn, self.stride = offset, turn, stride
        self.parity = offset % 2
        self.half = offset // 2 if turn is None else turn + offset // 2
        self.n = offset if turn is None else turn * stride + offset

    def back(self, n):
        return Batch(self.offset - n, self.turn, self.stride)


def wait(eng, count, b, j=0):
    if b.turn is not None or count.at(b.n, j) > 0:
        eng.wait_ge(count.sem, count.at(b.n, j))


def bcast(ap, dim, n):
    ap = ap.unsqueeze(dim)
    shape = list(ap.shape)
    shape[dim] = n
    return ap.broadcast_to(shape)


def build_program(nc, x, ctx, ctxT, mask, g_xattn, g_ffn, wq, wkv, bq, bk, bv, gate0, w_gate, w_up, w_down,
                  ws_in, ws_out, w1s, w2, wg1, gbias, out):
    with ExitStack() as keep:
        def sem(name):
            return keep.enter_context(nc.semaphore(name))

        def sb(name, shape, dt=F32, where=keep):
            return where.enter_context(nc.sbuf_tensor(name, shape, dt))

        xs = sb("xs", [P, NT, D])
        ident = sb("ident", [P, P])
        identb = sb("identb", [P, P], BF16)
        upper = sb("upper", [P, P], BF16)
        onesb = sb("onesb", [P, P], BF16)
        causal_q = sb("causal_q", [P, P], BF16)
        causal_k = sb("causal_k", [P, P], BF16)
        half = sb("half", [P, 3 * TT])
        zeros = sb("zeros", [P, TT, D])
        iota64 = sb("iota64", [P, CAP])
        tg = sb("tg", [P, 4])
        graw = sb("graw", [P, 4])
        gw0 = sb("gw0", [P, DT, NE])
        gw1 = sb("gw1", [P, DT, NE1])
        gb1 = sb("gb1", [P, NE1])
        maski = sb("maski", [P, NT], I32)
        maskr = sb("maskr", [P, 3, NT])
        maskp = sb("maskp", [P, NT, 3], BF16)
        lg = sb("lg", [P, TT, NB, NE])
        lgt = sb("lgt", [P, TT, NB, NE])
        lgs = sb("lgs", [P, TT * NB])
        sel = sb("sel", [P, TT, NB * NE], BF16)
        slot = sb("slot", [P, TT, NB * NE])
        onehot = sb("onehot", [P, TT, NB, NE * CAP], BF16)

        ye = nc.dram_tensor("ye", [NB, NE * CAP, D], F32, kind="Internal").ap()
        gates = nc.dram_tensor("gates", [NB, P, NPAIR, S], F32, kind="Internal").ap()

        with ExitStack() as att:
            def ab(name, shape, dt=F32):
                return sb(name, shape, dt, att)

            xn2s = ab("xn2s", [P, NT, 3, D], BF16)
            xnT_all = xn2s[:, :, :, :].rearrange("p a b c -> p (a b c)")[:, 0:2 * DT * NB * S].bitcast(F32)\
                .rearrange("p (a b) -> p a b", a=DT)
            q_nat = ab("q_nat", [P, TT, NH, P], BF16)
            k_nat = ab("k_nat", [P, TT, NH, P], BF16)
            q_t = ab("q_t", [P, NH, S], BF16)
            q_tm = ab("q_tm", [P, NH, S], BF16)
            k_t = [ab(f"k_t{i}", [P, NH, S], BF16) for i in range(2)]
            v_aug = [ab(f"v_aug{i}", [P, TT, NH, 2 * W]) for i in range(2)]
            probs = [ab(f"probs{i}", [P, 4, TT * S]) for i in range(2)]
            o_t = ab("o_t", [P, 4, S])
            xn = ab("xn", [P, TT, D])
            xn_post = ab("xn_post", [P, TT, D])
            xnT = ab("xnT", [P, DT, S])
            xnT_post = ab("xnT_post", [P, DT, S])
            q32 = ab("q32", [P, TT, D])
            k32 = ab("k32", [P, TT, D])
            rq = ab("rq", [P, TT, D])
            rk = ab("rk", [P, TT, D])
            rx = ab("rx", [P, TT, D])
            o_nat = ab("o_nat", [P, TT, D])
            wq_s = ab("wq_s", [P, DT, D])
            wkv_s = ab("wkv_s", [P, DT, 2 * D])
            bq_s, bk_s, bv_s = (ab(n, [P, D]) for n in ("bq_s", "bk_s", "bv_s"))
            ctx_s = [ab(f"ctx_s{i}", [P, 2, 256]) for i in range(2)]
            ye_s = [ab(f"ye_s{i}", [P, NPAIR, D]) for i in range(2)]
            gates_s = [ab(f"gates_s{i}", [P, NPAIR, S]) for i in range(2)]
            st, st2 = ab("st", [P, TT, 6]), ab("st2", [P, TT, 6])
            mv, mv2 = ab("mv", [P, TT, 2]), ab("mv2", [P, TT, 2])
            rs, rs2 = ab("rs", [P, 2, TT]), ab("rs2", [P, 2, TT])
            mx = ab("mx", [P, TT, NH])
            mr = ab("mr", [P, TT, NH])
            rden = ab("rden", [P, 2, TT, NH])

        with ExitStack() as ffn:
            def fb(name, shape, dt=F32):
                return sb(name, shape, dt, ffn)

            fb("xn2s_place", [P, NT, 3, D], BF16)
            xin = fb("xin", [P, DT, NE, SLOTS])
            wg_s = [fb(f"wg_s{i}", [P, DT, I]) for i in range(2)]
            wu_s = [fb(f"wu_s{i}", [P, DT, I]) for i in range(2)]
            wd_s = [fb(f"wd_s{i}", [P, IT, D]) for i in range(2)]
            silu = fb("silu", [P, 2, SLOTS])
            hT = fb("hT", [P, IT, SLOTS])
            y_s = fb("y_s", [P, 2, 2, D])
            gated = fb("gated", [P, TT, NE * CAP])
            gt_s = fb("gt_s", [P, TT, NPAIR, P])
            top = [fb(f"top{i}", [NB * NE, S]) for i in range(2)]
            top8 = fb("top8", [NB * NE, 8])
            selT = fb("selT", [NB * NE, S], BF16)

        with ExitStack() as last:
            def lb(name, shape, dt=F32):
                return sb(name, shape, dt, last)

            lb("xnT_all_place", [P, NT, 3, D], BF16)
            wsi_s = lb("wsi_s", [P, DT, 2 * H1])
            w1_s = lb("w1_s", [P, DT, 2 * H1])
            wso_s = lb("wso_s", [P, DT, D])
            w2_s = lb("w2_s", [P, DT, NE1, D])
            sact = lb("sact", [P, 2, 512])
            hsT = lb("hsT", [P, 2, 512])
            hrT = lb("hrT", [P, 2, 512])
            lg1 = lb("lg1", [P, NT, NE1])
            e1 = lb("e1", [P, NT, NE1])
            sm1 = lb("sm1", [P, NT])
            top1 = lb("tops_1", [P, NT, 2 * NE1])
            top1r = lb("tops_1r", [P, NT, 2 * NE1])
            best = lb("best", [P, NT, 8])
            find = lb("find", [P, NT, 8])
            wd1 = lb("wd1", [P, NT, NE1])

        pA, pB, pM = [keep.enter_context(nc.psum_tensor(n, [P, k, 512], F32)) for n, k in (("pA", 2), ("pB", 2), ("pM", 3))]
        pO = keep.enter_context(nc.psum_tensor("pO", [P, 2, S], F32))
        pMb = pM[:, :, :].bitcast(BF16)

        loaded = {n: sem(f"loaded_{n}") for n in ("x", "small", "wqkv", "wl1")}
        const_pool, const_dve, const_act = sem("const_pool"), sem("const_dve"), sem("const_act")
        const_l1 = sem("const_l1")
        settled = sem("settled")
        phase_end = sem("phase_end")
        ctx_in = [[sem(f"ctx_in{l}{i}") for i in range(2)] for l in range(2)]
        gates_in = [sem(f"gates_in{i}") for i in range(2)]
        ye_in = [sem(f"ye_in{i}") for i in range(2)]
        N_SMALL = 10
        N_CONST_POOL, N_CONST_DVE, N_CONST_ACT = 19, 11, 1

        both = dict(stat=2, mv=2, rs=2, xn=2, v=2, q1=1, qr=1, q2=1, q3=1, k1=1, kr=1, k2=1, k3=1, qt_ps=4, qt=4,
                    kt_ps=4, kt=4, a_ps=NH, mx=NH, m1=1, mr=1, m2=1, m3=1, qtm_ps=4, qtm=2, qtm_a=2, b_ps=NH, p=NH,
                    pv=4, ot=4, ott=1, rden=2, o=1, xres=1, stat2=2, mv2=2, rs2=2, xn2=2, x2T_ps=1, x2T=1)
        only0 = dict(xnT_ps=1, xnT=1, q_ps=1, kv_ps=2, q32=1, k32=2, kmask=1, s1=1, sr=1, s2=1, s3=1, lg_ps=1, lg=1)
        only1 = dict(sc_ps=1, x2=1)
        C = [{n: Count(sem(n), per) for n, per in (both | only0).items()}, {}]
        C[1] = {n: Count(C[0][n].sem, per + (n == "rs"), NB * per) for n, per in both.items()}
        C[1] |= {n: Count(sem(n), per) for n, per in only1.items()}

        def barrier(eng, n):
            eng.drain().then_inc(phase_end, 1)
            eng.wait_ge(phase_end, 5 * n)

        def settle(eng):
            eng.sem_inc(settled, 1)

        def tile_of(n):
            return xs[:, bass.ds(n, 1), :].rearrange("p o d -> p (o d)")

        def stack(nat):
            return nat[:, :, :, 0:MASK0].rearrange("p t h (n w) -> p (t h) n w", w=W)

        def rep(nat, first, n):
            return stack(nat)[:, :, first:first + n, :]

        def rep_of(src, n):
            return bcast(src[:].rearrange("p t (h w) -> p (t h) w", w=W), 2, n)

        def part_of(nat, n):
            return nat[:, :, :, n * W:(n + 1) * W]

        def by_head(src):
            return src[:].rearrange("p t (h w) -> p t h w", w=W)

        def turned(bank, rows):
            return pMb[0:rows, bank, :].rearrange("p (h s) -> p h s", h=4)

        def out_bank(q):
            return pM[:, q, :] if q < 3 else pO[:].rearrange("p a b -> p (a b)")

        w_in = [[sem(f"w_in{p}{i}") for i in range(3)] for p in range(2)]
        y_ready = Count(sem("y_ready"), 2)
        gates_out = [sem("gates_out0"), sem("gates_out1")]
        y_out = [sem("y_out0"), sem("y_out1")]
        stored, out_ready = sem("stored"), sem("out_ready")
        g_ps, u_ps = Count(sem("g_ps"), IT), Count(sem("u_ps"), IT)
        silu_ok, h_ok = Count(sem("silu_ok"), IT), Count(sem("h_ok"), IT)
        down_ps = Count(sem("down_ps"), 2)
        gated_ok, gt_ps, gt_ok = Count(sem("gated_ok"), 2), Count(sem("gt_ps"), 2), Count(sem("gt_ok"), 2)
        onehot_ok, gather_ps = Count(sem("onehot_ok"), 2), Count(sem("gather_ps"), 2)
        route, route_act, route_pe = sem("route"), sem("route_act"), sem("route_pe")
        xin_ok, xin_act = Count(sem("xin_ok"), 1), Count(sem("xin_act"), 1)
        const_v1 = sem("const_v1")
        f1_ps, f1_act, f1_h = Count(sem("f1_ps"), 8), Count(sem("f1_act"), 4), Count(sem("f1_h"), 4)
        r1, r1_act, r1_pe = sem("r1"), sem("r1_act"), sem("r1_pe")
        o1_ps, o1_acc = Count(sem("o1_ps"), 20), Count(sem("o1_acc"), 36)

        block = keep.enter_context(nc.Block())

        def pairs(eng, body, n):
            body(Batch(0))
            body(Batch(1))
            with eng.Fori(1, n // 2) as j:
                body(Batch(0, j))
                body(Batch(1, j))

        def slots(eng, slot_of):
            slot_of(Batch(0), None, None)
            slot_of(Batch(1), Batch(0), None)
            with eng.Fori(0, 3) as j:
                slot_of(Batch(2, j), Batch(1, j), Batch(0, j))
                slot_of(Batch(3, j), Batch(2, j), Batch(1, j))
            slot_of(None, Batch(7), Batch(6))
            slot_of(None, None, Batch(7))

        @block.sync
        def _(sp):
            for i, (dst, src) in enumerate(((maski[:], mask), (graw[:, 0:2], g_xattn.partition_broadcast(P)),
                                            (graw[:, 2:4], g_ffn.partition_broadcast(P)),
                                            (gw0[:], gate0), (gw1[:], wg1), (gb1[:], gbias.partition_broadcast(P)),
                                            (bq_s[:], bq.partition_broadcast(P)), (bk_s[:], bk.partition_broadcast(P)),
                                            (bv_s[:], bv.partition_broadcast(P)))):
                sp.dma_start(dst, src).then_inc(loaded["small"], 16)
            sp.dma_start(xs[:, 0:4, :], x[:, 0:4, :]).then_inc(loaded["small"], 16)
            sp.dma_start(wq_s[:], wq).then_inc(loaded["wqkv"], 16)
            sp.dma_start(ctx_s[0][:], ctxT[0]).then_inc(ctx_in[0][0], 16)
            sp.dma_start(wkv_s[:], wkv).then_inc(loaded["wqkv"], 16)
            sp.dma_start(ctx_s[1][:], ctxT[1]).then_inc(ctx_in[0][1], 16)
            sp.dma_start(xs[:, 4:NT, :], x[:, 4:NT, :]).then_inc(loaded["x"], 16)

            def ctx_loads(layer):
                src = (ctxT, ctx)[layer]
                c = C[layer]
                with sp.Fori(0, 3) as j:
                    for b in (Batch(2, j), Batch(3, j)):
                        if layer == 0:
                            wait(sp, c["kv_ps"], b.back(2), 1)
                        else:
                            wait(sp, c["k3"], b.back(2))
                            settle(sp)
                            wait(sp, c["v"], b.back(2), 1)
                            settle(sp)
                            wait(sp, c["sc_ps"], b.back(2))
                        settle(sp)
                        sp.dma_start(ctx_s[b.parity][:], src[bass.ds(b.n, 1)].rearrange("o p t d -> (o p) t d"))\
                          .then_inc(ctx_in[layer][b.parity], 16)
                        if layer == 1:
                            sp.dma_start(ye_s[b.parity][:], ye[bass.ds(b.n, 1)].rearrange("o (q p) d -> (o p) q d", p=P))\
                              .then_inc(ye_in[b.parity], 16)
                            sp.dma_start(gates_s[b.parity][:], gates[bass.ds(b.n, 1)].rearrange("o p q s -> (o p) q s"))\
                              .then_inc(gates_in[b.parity], 16)

            ctx_loads(0)
            barrier(sp, 1)

            def load_expert(e, n):
                for i, (dst, src) in enumerate(((wg_s, w_gate), (wu_s, w_up), (wd_s, w_down))):
                    s = src[bass.ds(n, 1)].rearrange("o p a b -> (o p) a b")
                    sp.dma_start(dst[e.parity][:], s).then_inc(w_in[e.parity][i], 16)

            load_expert(Batch(0), 0)
            load_expert(Batch(1), 1)

            def store_y(e):
                for t in range(TT):
                    wait(sp, gt_ok, e, t)
                    settle(sp)
                    sp.dma_start(gates[bass.ds(e.n, 1), :, :, t * P:(t + 1) * P].rearrange("o p q s -> (o p) q s"),
                                 gt_s[:, t, :, :]).then_inc(gates_out[t], 16)
                for h in range(2):
                    wait(sp, y_ready, e, h)
                    settle(sp)
                    for q in range(2):
                        tt = 2 * h + q
                        for b2 in range(2):
                            sp.dma_start(ye[2 * tt + b2, bass.ds(e.n * CAP, CAP), :],
                                         y_s[b2 * CAP:(b2 + 1) * CAP, h, q, :]).then_inc(y_out[h], 16)

            with sp.Fori(0, 3) as j:
                for e in (Batch(0, j), Batch(1, j)):
                    store_y(e)
                    wait(sp, down_ps, e, 1)
                    settle(sp)
                    load_expert(e, e.n + 2)
            for e in (Batch(6), Batch(7)):
                store_y(e)
            for h in range(2):
                sp.wait_ge(y_out[h], 16 * 4 * NE)
                sp.wait_ge(gates_out[h], 16 * NB)
            barrier(sp, 2)
            for b in range(2):
                sp.dma_start(ctx_s[b][:], ctx[b]).then_inc(ctx_in[1][b], 16)
                sp.dma_start(ye_s[b][:], ye[b].rearrange("(q p) d -> p q d", p=P)).then_inc(ye_in[b], 16)
                sp.dma_start(gates_s[b][:], gates[b]).then_inc(gates_in[b], 16)
            ctx_loads(1)
            barrier(sp, 3)
            for dst, src in ((wsi_s, ws_in), (w1_s, w1s), (wso_s, ws_out), (w2_s, w2)):
                sp.dma_start(dst[:], src).then_inc(loaded["wl1"], 16)
            with sp.Fori(0, NT) as n:
                sp.wait_ge(out_ready, n + 1)
                settle(sp)
                sp.dma_start(out[:, bass.ds(n, 1), :], xs[:, bass.ds(n, 1), :]).then_inc(stored, 16)
            sp.wait_ge(stored, 16 * NT)

        @block.gpsimd
        def _(pool):
            done = [0]

            def const(ins):
                done[0] += 1
                ins.then_inc(const_pool, 1)

            const(pool.memset(ident[:], 0.0))
            const(pool.memset(identb[:], 0.0))
            const(pool.memset(upper[:], 1.0))
            const(pool.memset(onesb[:], 1.0))
            const(pool.memset(causal_q[:], 0.0))
            const(pool.memset(causal_k[:], 0.0))
            const(pool.memset(half[:, 0:TT], -0.5))
            const(pool.memset(half[:, TT:2 * TT], EPS))
            const(pool.memset(half[:, 2 * TT:], SCALE))
            const(pool.memset(zeros[:], 0.0))
            const(pool.iota(iota64[:], pattern=[[1, CAP]], base=0, channel_multiplier=0,
                            allow_small_or_imprecise_dtypes=True))
            pool.wait_ge(const_pool, done[0])
            for m in (ident, identb):
                const(pool.affine_select(out=m[:], in_=m[:], compare_op=ALU.not_equal, fill=1.0, base=0,
                                         pattern=[[-1, P]], channel_multiplier=1))
            const(pool.affine_select(out=upper[:], in_=upper[:], compare_op=ALU.is_ge, fill=0.0, base=0,
                                     pattern=[[1, P]], channel_multiplier=-1))
            const(pool.affine_select(out=causal_q[:], in_=causal_q[:], compare_op=ALU.is_ge, fill=NEG, base=0,
                                     pattern=[[-1, P]], channel_multiplier=1))
            const(pool.affine_select(out=causal_k[:], in_=causal_k[:], compare_op=ALU.is_ge, fill=NEG, base=0,
                                     pattern=[[1, P]], channel_multiplier=-1))
            const(pool.memset(q_nat[:, :, :, MASK0:NMAX0], 1.0))
            const(pool.memset(q_nat[:, :, :, NMAX0:ROWS_B], 0.0))
            const(pool.memset(k_nat[:, :, :, NMAX0:ROWS_B], 1.0))
            assert done[0] == N_CONST_POOL

            def rstd(c, b, mvs, rss, mv_name, rs_name, used_name):
                wait(pool, c[mv_name], b, 1)
                wait(pool, c[used_name], b.back(1), 1)
                pool.tensor_tensor(rss[:, 0, :], mvs[:, :, 1], half[:, TT:2 * TT], ALU.add).then_inc(c[rs_name].sem, 1)
                wait(pool, c[rs_name], b, 0)
                pool.tensor_tensor(rss[:, 1, :], rss[:, 0, :], half[:, 0:TT], ALU.pow).then_inc(c[rs_name].sem, 1)

            def slot_of(layer):
                c = C[layer]

                def go(a, b, z):
                    if a is not None:
                        rstd(c, a, mv, rs, "mv", "rs", "xn")
                        if layer == 1:
                            wait(pool, c["rs"], a, 1)
                            pool.tensor_tensor(rs[:, 1, :], rs[:, 1, :], half[:, 2 * TT:], ALU.mult).then_inc(c["rs"].sem, 1)
                    if a is not None and layer == 1:
                        pool.wait_ge(ctx_in[1][a.parity], 16 * (a.half + 1))
                        wait(pool, c["pv"], a.back(2), 3)
                        for t in range(TT):
                            settle(pool)
                            pool.tensor_tensor(v_aug[a.parity][:, t, :, 0:W], by_head(ctx_s[a.parity])[:, t],
                                               by_head(zeros)[:, t], ALU.add).then_inc(c["v"].sem, 1)
                    if z is not None:
                        rstd(c, z, mv2, rs2, "mv2", "rs2", "xn2")
                    if z is not None and layer == 0:
                        part = [xn2s[:, bass.ds(z.n * TT, TT), i, :] for i in range(3)]
                        wait(pool, c["xn2"], z, 1)
                        wait(pool, c["s3"], z.back(1))
                        settle(pool)
                        pool.tensor_tensor(part[0], xn_post[:], zeros[:], ALU.add).then_inc(c["s1"].sem, 1)
                        wait(pool, c["s1"], z)
                        settle(pool)
                        pool.tensor_tensor(rx[:], xn_post[:], part[0], ALU.subtract).then_inc(c["sr"].sem, 1)
                        wait(pool, c["sr"], z)
                        settle(pool)
                        pool.tensor_tensor(part[1], rx[:], zeros[:], ALU.add).then_inc(c["s2"].sem, 1)
                        wait(pool, c["s2"], z)
                        settle(pool)
                        pool.tensor_tensor(part[2], rx[:], part[1], ALU.subtract).then_inc(c["s3"].sem, 1)
                return go

            slots(pool, slot_of(0))
            barrier(pool, 1)
            barrier(pool, 2)
            pool.memset(q_nat[:, :, :, MASK0:NMAX0], 1.0).then_inc(const_l1, 1)
            pool.memset(q_nat[:, :, :, NMAX0:ROWS_B], 0.0).then_inc(const_l1, 1)
            pool.memset(k_nat[:, :, :, NMAX0:ROWS_B], 1.0).then_inc(const_l1, 1)
            pool.memset(k_nat[:, :, :, MASK0:NMAX0], 0.0).then_inc(const_l1, 1)
            slots(pool, slot_of(1))
            barrier(pool, 3)

        @block.scalar
        def _(act):
            act.wait_ge(loaded["small"], 16 * N_SMALL)
            act.activation(tg[:], graw[:], ACT.Tanh).then_inc(const_act, 1)

            def slot_of(layer):
                c = C[layer]
                width = 2 * S if layer == 0 else S + P

                def go(a, b, z):
                    for h in range(NH):
                        if b is not None:
                            wait(act, c["b_ps"], b, h)
                            wait(act, c["pv"], b, h // 4 - 2)
                            act.activation(probs[h // 4 % 2][:, h % 4, 0:width], pB[:, h % 2, 0:width], ACT.Exp)\
                               .then_inc(c["p"].sem, 1)
                        if h == 1 and a is not None and layer == 0:
                            wait(act, c["xnT_ps"], a)
                            wait(act, c["kv_ps"], a, -1)
                            act.activation(xnT[:], pM[:, 2, :].rearrange("p (a b) -> p a b", a=DT), ACT.Copy)\
                               .then_inc(c["xnT"].sem, 1)
                        if h == 5 and z is not None:
                            wait(act, c["x2T_ps"], z)
                            src = pM[:, 0, :].rearrange("p (a b) -> p a b", a=DT)
                            if layer == 0:
                                wait(act, c["lg_ps"], z, -1)
                                act.activation(xnT_post[:], src, ACT.Copy).then_inc(c["x2T"].sem, 1)
                            else:
                                settle(act)
                                act.activation(xnT_all[:, :, bass.ds(z.n * S, S)], src, ACT.Copy).then_inc(c["x2T"].sem, 1)
                        if a is None:
                            continue
                        if h == 5:
                            wait(act, c["xn" if layer else "q32"], a, layer)
                            wait(act, c["qtm_ps"], a, -1)
                            act.activation(rep(q_nat, 0, 3), rep_of(q32, 3), ACT.Copy).then_inc(c["q1"].sem, 1)
                        if h == 7:
                            wait(act, c["qr"], a)
                            act.activation(rep(q_nat, 4, 2), rep_of(rq, 2), ACT.Copy).then_inc(c["q2"].sem, 1)
                        if h == 9:
                            if layer == 0:
                                wait(act, c["k32"], a, 1)
                                src = k32
                            else:
                                act.wait_ge(ctx_in[1][a.parity], 16 * (a.half + 1))
                                src = ctx_s[a.parity]
                            wait(act, c["kt_ps"], a, -1)
                            act.activation(rep(k_nat, 2, 3), rep_of(src, 3), ACT.Copy).then_inc(c["k1"].sem, 1)
                        if h == 11:
                            wait(act, c["kr"], a)
                            act.activation(stack(k_nat)[:, :, 0:6:5, :], rep_of(rk, 2), ACT.Copy).then_inc(c["k2"].sem, 1)
                        if 8 <= h < 12:
                            i = h - 8
                            wait(act, c["qt_ps"], a, i)
                            wait(act, c["a_ps"], a, -1)
                            act.activation(q_t[0:ROWS_A, 4 * i:4 * i + 4, :], turned((2, 1, 0, 2)[i], ROWS_A), ACT.Copy)\
                               .then_inc(c["qt"].sem, 1)
                    if a is not None:
                        for i in (1, 3):
                            wait(act, c["qtm_ps"], a, i)
                            wait(act, c["b_ps"], a.back(1), 4 * i + 3)
                            act.activation(q_tm[0:ROWS_B, 4 * i:4 * i + 4, :], turned((0, 2, 1, 0)[i], ROWS_B), ACT.Copy)\
                               .then_inc(c["qtm_a"].sem, 1)
                return go

            slots(act, slot_of(0))
            barrier(act, 1)
            act.wait_ge(route, 2)
            act.activation(lg[:], lgt[:], ACT.Exp).then_inc(route_act, 1)

            def gather(b):
                wait(act, gather_ps, b, 1)
                settle(act)
                act.activation(xin[:, 1, :, bass.ds(b.n * CAP, CAP)], pB[:, b.parity, :].rearrange("p (e s) -> p e s", e=NE),
                               ACT.Copy).then_inc(xin_act.sem, 1)

            pairs(act, gather, NB)

            def expert(e):
                for it in range(IT):
                    wait(act, g_ps, e, it)
                    wait(act, h_ok, e, it - 2)
                    act.activation(silu[:, it % 2, :], pA[:, it % 2, :], ACT.Silu).then_inc(silu_ok.sem, 1)

            pairs(act, expert, NE)
            barrier(act, 2)
            slots(act, slot_of(1))
            barrier(act, 3)
            act.wait_ge(r1, 3)
            act.activation(e1[:], lg1[:], ACT.Exp).then_inc(r1_act, 1)

            def chunk(c):
                for i in range(4):
                    wait(act, f1_ps, c, 2 * i)
                    wait(act, f1_h, c, i - 2)
                    act.activation(sact[:, i % 2, :], pA[:, i % 2, :], ACT.Silu).then_inc(f1_act.sem, 1)

            chunk(Batch(0))
            with act.Fori(1, 4) as j:
                chunk(Batch(0, j, 1))

        @block.vector
        def _(dve):
            n_const = [0]

            def const(ins):
                n_const[0] += 1
                ins.then_inc(const_dve, 1)

            def v_const(count):
                for v in v_aug:
                    count(dve.memset(v[:, :, :, W:W + 1], 1.0))
                    count(dve.memset(v[:, :, :, W + 1:2 * W], 0.0))

            v_const(const)
            dve.wait_ge(loaded["small"], 16 * N_SMALL)
            const(dve.tensor_scalar(bq_s[:], bq_s[:], SCALE, None, ALU.mult))
            const(dve.tensor_copy(maskr[:, 0, :], maski[:]))
            dve.wait_ge(const_dve, n_const[0])
            const(dve.tensor_scalar(maskr[:, 1, :], maskr[:, 0, :], 10000.0, -10000.0, ALU.mult, ALU.add))
            dve.wait_ge(const_dve, n_const[0])
            const(dve.tensor_copy(maskp[:, :, 0], maskr[:, 1, :]))
            dve.wait_ge(const_dve, n_const[0])
            const(dve.tensor_tensor(maskr[:, 2, :], maskr[:, 1, :], maskp[:, :, 0], ALU.subtract))
            dve.wait_ge(const_dve, n_const[0])
            const(dve.tensor_copy(maskp[:, :, 1], maskr[:, 2, :]))
            dve.wait_ge(const_dve, n_const[0])
            const(dve.tensor_tensor(maskp[:, :, 2], maskr[:, 2, :], maskp[:, :, 1], ALU.subtract))
            assert n_const[0] == N_CONST_DVE
            dve.wait_ge(const_dve, N_CONST_DVE)
            dve.wait_ge(const_pool, N_CONST_POOL)
            dve.wait_ge(const_act, N_CONST_ACT)

            def slot_of(layer):
                c = C[layer]

                def inc(name):
                    return c[name].sem, 1

                def x_of(b):
                    return xs[:, bass.ds(b.n * TT, TT), :]

                def statistics(b, stt, mvv, stat, mv_name):
                    settle(dve)
                    for t in range(TT):
                        dve.bn_stats(stt[:, t, :], tile_of(b.n * TT + t)).then_inc(*inc(stat))
                    for t in range(TT):
                        wait(dve, c[stat], b, t)
                        settle(dve)
                        dve.bn_aggr(mvv[:, t, :], stt[:, t, :]).then_inc(*inc(mv_name))

                def normalise(b, dst, mvv, rss, name):
                    for t in range(TT):
                        dve.tensor_scalar(dst[:, t, :], tile_of(b.n * TT + t), mvv[:, t, 0:1],
                                          rss[:, 1, t:t + 1], ALU.subtract, ALU.mult).then_inc(*inc(name))

                def take_o(b, g):
                    wait(dve, c["pv"], b, g)
                    wait(dve, c["ott"], b.back(1))
                    dve.tensor_copy(o_t[:, g, :], pO[:, g % 2, :]).then_inc(*inc("ot"))

                def take_k(a, i):
                    wait(dve, c["kt_ps"], a, i)
                    wait(dve, c["b_ps"], a.back(2), NH - 1)
                    dve.tensor_copy(k_t[a.parity][0:ROWS_B, 4 * i:4 * i + 4, :], turned((1, 0, 2, 1)[i], ROWS_B))\
                       .then_inc(*inc("kt"))

                def go(a, b, z):
                    if a is not None:
                        if layer == 1:
                            wait(dve, c["sc_ps"], a)
                            settle(dve)
                            dve.tensor_tensor(x_of(a), x_of(a), pM[:, 2, :].rearrange("p (t d) -> p t d", t=TT), ALU.add)\
                               .then_inc(*inc("x2"))
                            wait(dve, c["x2"], a)
                        elif a.turn is None and a.offset == 1:
                            dve.wait_ge(loaded["x"], 16)
                        statistics(a, st, mv, "stat", "mv")
                    if z is not None:
                        o_ps = pM[:, 0:TT, :].rearrange("p t (h w) -> p t h w", w=2 * W)
                        wait(dve, c["ott"], z)
                        dve.reciprocal(rden[:, 0, :, :], o_ps[:, :, :, W]).then_inc(*inc("rden"))
                        wait(dve, c["rden"], z, 0)
                        dve.tensor_scalar(rden[:, 1, :, :], rden[:, 0, :, :], tg[:, layer:layer + 1], None, ALU.mult)\
                           .then_inc(*inc("rden"))
                        wait(dve, c["rden"], z, 1)
                        dve.tensor_tensor(o_nat[:].rearrange("p t (h w) -> p t h w", w=W), o_ps[:, :, :, 0:W],
                                          bcast(rden[:, 1, :, :], 3, W), ALU.mult).then_inc(*inc("o"))
                        wait(dve, c["o"], z)
                        settle(dve)
                        dve.tensor_tensor(x_of(z), x_of(z), o_nat[:], ALU.add).then_inc(*inc("xres"))
                        wait(dve, c["xres"], z)
                        statistics(z, st2, mv2, "stat2", "mv2")
                    if a is not None:
                        wait(dve, c["rs"], a, 1 + layer)
                        if layer == 0:
                            wait(dve, c["xnT_ps"], a, -1)
                        normalise(a, (xn, q32)[layer], mv, rs, "xn")
                        if layer == 0:
                            wait(dve, c["q_ps"], a)
                            dve.scalar_tensor_tensor(out=q32[:], in0=pM[:, 0, :].rearrange("p (t d) -> p t d", t=TT),
                                                     scalar=SCALE, in1=bcast(bq_s[:], 1, TT), op0=ALU.mult, op1=ALU.add)\
                               .then_inc(*inc("q32"))
                            for t in range(TT):
                                wait(dve, c["kv_ps"], a, t)
                                dve.tensor_tensor(k32[:, t, :], pM[:, 1 + t, 0:D], bk_s[:], ALU.add).then_inc(*inc("k32"))
                                wait(dve, c["pv"], a.back(2), 3)
                                dve.tensor_tensor(v_aug[a.parity][:, t, :, 0:W],
                                                  pM[:, 1 + t, D:2 * D].rearrange("p (h w) -> p h w", w=W),
                                                  bv_s[:].rearrange("p (h w) -> p h w", w=W), ALU.add).then_inc(*inc("v"))
                    if z is not None:
                        wait(dve, c["rs2"], z, 1)
                        wait(dve, c["x2T_ps"], z, -1)
                        if layer == 0:
                            wait(dve, c["sr"], z, -1)
                        normalise(z, xn_post, mv2, rs2, "xn2")
                    if b is not None:
                        take_o(b, 0)
                    if z is not None and layer == 0:
                        wait(dve, c["lg_ps"], z)
                        settle(dve)
                        dve.tensor_copy(lg[:, :, bass.ds(z.n, 1), :], pM[:, 1, 0:TT * NE].rearrange("p (t e) -> p t e", t=TT))\
                           .then_inc(*inc("lg"))
                    if a is not None:
                        wait(dve, c["q1"], a)
                        dve.tensor_tensor(by_head(rq), by_head(q32), part_of(q_nat, 0), ALU.subtract).then_inc(*inc("qr"))
                        wait(dve, c["q2"], a)
                        dve.tensor_tensor(part_of(q_nat, 3), by_head(rq), part_of(q_nat, 4), ALU.subtract).then_inc(*inc("q3"))
                    if b is not None:
                        take_o(b, 1)
                    if a is not None:
                        src = k32 if layer == 0 else ctx_s[a.parity]
                        wait(dve, c["k1"], a)
                        dve.tensor_tensor(by_head(rk), by_head(src), part_of(k_nat, 2), ALU.subtract).then_inc(*inc("kr"))
                        wait(dve, c["k2"], a)
                        dve.tensor_tensor(part_of(k_nat, 1), by_head(rk), part_of(k_nat, 0), ALU.subtract).then_inc(*inc("k3"))
                        if layer == 0:
                            settle(dve)
                            dve.tensor_copy(k_nat[:, :, :, MASK0:NMAX0], bcast(maskp[:, bass.ds(a.n * TT, TT), :], 2, NH))\
                               .then_inc(*inc("kmask"))
                        take_k(a, 0)
                    if b is not None:
                        take_o(b, 2)
                    if a is not None:
                        for i in range(1, 4):
                            take_k(a, i)
                    if b is not None:
                        take_o(b, 3)
                    if a is None:
                        return
                    for h in range(NH):
                        wait(dve, c["a_ps"], a, h)
                        if layer == 0:
                            dve.tensor_reduce(mx[:, :, h], pA[:, h % 2, :].rearrange("p (t k) -> p t k", t=TT), AX, ALU.max)\
                               .then_inc(*inc("mx"))
                        else:
                            dve.tensor_reduce(mx[:, 0, h:h + 1], pA[:, h % 2, 0:P], AX, ALU.max)
                            dve.tensor_reduce(mx[:, 1, h:h + 1], pA[:, h % 2, P:P + S], AX, ALU.max).then_inc(*inc("mx"))
                    part = [q_nat[:, :, :, NMAX0 + i] for i in range(3)]
                    wait(dve, c["mx"], a, NH - 1)
                    dve.tensor_scalar(part[0], mx[:], -1.0, None, ALU.mult).then_inc(*inc("m1"))
                    wait(dve, c["m1"], a)
                    dve.scalar_tensor_tensor(out=mr[:], in0=mx[:], scalar=-1.0, in1=part[0], op0=ALU.mult, op1=ALU.subtract)\
                       .then_inc(*inc("mr"))
                    wait(dve, c["mr"], a)
                    dve.tensor_copy(part[1], mr[:]).then_inc(*inc("m2"))
                    wait(dve, c["m2"], a)
                    dve.tensor_tensor(part[2], mr[:], part[1], ALU.subtract).then_inc(*inc("m3"))
                    for i in (0, 2):
                        wait(dve, c["qtm_ps"], a, i)
                        wait(dve, c["b_ps"], a.back(1), 4 * i + 3)
                        dve.tensor_copy(q_tm[0:ROWS_B, 4 * i:4 * i + 4, :], turned((0, 2, 1, 0)[i], ROWS_B))\
                           .then_inc(*inc("qtm"))
                return go

            slots(dve, slot_of(0))
            barrier(dve, 1)

            step = [0]

            def then(ins, sem_=route):
                step[0] += 1
                ins.then_inc(sem_, 1)
                dve.wait_ge(sem_, step[0])

            lg3 = lg[:].rearrange("p t b e -> p (t b) e")
            lgt3 = lgt[:].rearrange("p t b e -> p (t b) e")
            then(dve.tensor_reduce(lgs[:], lg3, AX, ALU.max))
            then(dve.tensor_tensor(lgt3, lg3, bcast(lgs[:], 2, NE), ALU.subtract))
            dve.wait_ge(route_act, 1)
            then(dve.tensor_reduce(lgs[:], lg3, AX, ALU.add))
            then(dve.reciprocal(lgs[:], lgs[:]))
            then(dve.tensor_tensor(lg3, lg3, bcast(lgs[:], 2, NE), ALU.mult))
            assert step[0] == 5
            dve.wait_ge(route_pe, 1)
            then(dve.tensor_copy(top[0][:], pA[0:NB * NE, 0, 0:S]))
            for r in range(CAP // 8):
                then(dve.max(top8[:], top[r % 2][:]))
                then(dve.match_replace(top[1 - r % 2][:], top8[:], top[r % 2][:], -1.0))
            then(dve.tensor_scalar(selT[:], top[0][:], 0.0, None, ALU.is_lt))
            assert step[0] == 7 + CAP // 4
            dve.wait_ge(route_pe, 2)
            then(dve.tensor_copy(sel[:], pA[:, 1, 0:TT * NB * NE // 2].bitcast(BF16).rearrange("p (t n) -> p t n", t=TT)))
            dve.wait_ge(route_pe, 3)
            then(dve.tensor_tensor(slot[:], pB[:, 0, 0:TT * NB * NE].rearrange("p (t n) -> p t n", t=TT), sel[:], ALU.mult))
            then(dve.tensor_scalar(slot[:], slot[:], -1.0, None, ALU.add))
            then(dve.tensor_scalar(lg3, lg3, tg[:, 2:3], None, ALU.mult))

            def gather(b):
                for t in range(TT):
                    dve.tensor_tensor(onehot[:, t, bass.ds(b.n, 1), :].rearrange("p o (e s) -> p (o e) s", e=NE),
                                      bcast(iota64[:], 1, NE), bcast(slot[:, t, bass.ds(b.n * NE, NE)], 2, CAP),
                                      ALU.is_equal).then_inc(onehot_ok.sem, 1)
                wait(dve, gather_ps, b, 0)
                settle(dve)
                dve.tensor_copy(xin[:, 0, :, bass.ds(b.n * CAP, CAP)], pA[:, b.parity, :].rearrange("p (e s) -> p e s", e=NE))\
                   .then_inc(xin_ok.sem, 1)

            pairs(dve, gather, NB)

            def expert(e):
                for t in range(TT):
                    wait(dve, gt_ps, e.back(1), t)
                    settle(dve)
                    dve.tensor_tensor(gated[:, t, :].rearrange("p (e s) -> p e s", e=NE),
                                      onehot[:, t, bass.ds(e.n, 1), :].rearrange("p o (e s) -> p (o e) s", e=NE),
                                      bcast(lg[:, t, bass.ds(e.n, 1), :].rearrange("p o e -> p (o e)"), 2, CAP),
                                      ALU.mult).then_inc(gated_ok.sem, 1)
                for it in range(IT):
                    wait(dve, silu_ok, e, it)
                    wait(dve, u_ps, e, it)
                    if it == 0:
                        wait(dve, down_ps, e.back(1), 1)
                    dve.tensor_tensor(hT[:, it, :], silu[:, it % 2, :], pB[:, it % 2, :], ALU.mult).then_inc(h_ok.sem, 1)
                for t in range(TT):
                    wait(dve, gt_ps, e, t)
                    settle(dve)
                    bank = pM[:, 2, :] if t == 0 else pO[:].rearrange("p a b -> p (a b)")
                    if e.turn is not None or e.offset > 0:
                        dve.wait_ge(gates_out[t], e.n * 16)
                    dve.tensor_copy(gt_s[:, t, :, :], bank.rearrange("p (q s) -> p q s", q=NPAIR)).then_inc(gt_ok.sem, 1)
                for h in range(2):
                    wait(dve, down_ps, e, h)
                    if e.turn is not None or e.offset > 0:
                        dve.wait_ge(y_out[h], e.n * 64)
                    dve.tensor_copy(y_s[:, h, :, :], pM[:, h, :].rearrange("p (q d) -> p q d", q=2)).then_inc(y_ready.sem, 1)

            pairs(dve, expert, NE)
            barrier(dve, 2)
            v_const(lambda ins: ins.then_inc(const_v1, 1))
            dve.wait_ge(const_v1, 4)
            slots(dve, slot_of(1))
            barrier(dve, 3)

            step[0] = 0

            def then1(ins):
                then(ins, r1)

            dve.wait_ge(r1_pe, 1)
            then1(dve.tensor_tensor(lg1[:], pA[:, 0, 0:NT * NE1].rearrange("p (n e) -> p n e", n=NT), bcast(gb1[:], 1, NT), ALU.add))
            then1(dve.tensor_reduce(sm1[:], lg1[:], AX, ALU.max))
            then1(dve.tensor_tensor(lg1[:], lg1[:], bcast(sm1[:], 2, NE1), ALU.subtract))
            dve.wait_ge(r1_act, 1)
            then1(dve.tensor_reduce(sm1[:], e1[:], AX, ALU.add))
            then1(dve.reciprocal(sm1[:], sm1[:]))
            then1(dve.tensor_tensor(top1[:, :, 0:NE1], e1[:], bcast(sm1[:], 2, NE1), ALU.mult))
            then1(dve.memset(top1[:, :, NE1:2 * NE1], -2.0))
            then1(dve.memset(find[:, :, 2:8], -2.0))
            for n in range(NT):
                then1(dve.max(best[:, n, :], top1[:, n, 0:NE1]))
            then1(dve.tensor_copy(find[:, :, 0:2], best[:, :, 0:2]))
            for n in range(NT):
                then1(dve.match_replace(top1r[:, n, :], find[:, n, :], top1[:, n, :], -2.0))
            then1(dve.scalar_tensor_tensor(out=wd1[:], in0=top1r[:, :, 0:NE1], scalar=-1.0, in1=top1[:, :, 0:NE1],
                                           op0=ALU.is_lt, op1=ALU.mult))
            then1(dve.tensor_scalar(wd1[:], wd1[:], tg[:, 3:4], None, ALU.mult))

            def chunk(c):
                for i in range(4):
                    wait(dve, f1_act, c, i)
                    wait(dve, f1_ps, c, 2 * i + 1)
                    dst = hsT[:, i, :] if i < 2 else hrT[:, i - 2, :]
                    dve.tensor_tensor(dst, sact[:, i % 2, :], pB[:, i % 2, :], ALU.mult).then_inc(f1_h.sem, 1)
                for t in range(4):
                    n = c.n * 4 + t
                    x_n = tile_of(n)
                    wait(dve, o1_ps, c, 5 * t)
                    settle(dve)
                    dve.scalar_tensor_tensor(out=x_n, in0=pA[:, t % 2, 0:D], scalar=tg[:, 3:4], in1=x_n, op0=ALU.mult, op1=ALU.add)\
                       .then_inc(o1_acc.sem, 1)
                    for e in range(NE1):
                        if e % 2 == 0:
                            wait(dve, o1_ps, c, 5 * t + 1 + e // 2)
                        wait(dve, o1_acc, c, 9 * t + e)
                        settle(dve)
                        ins = dve.scalar_tensor_tensor(out=x_n, in0=out_bank(e // 2)[:, e % 2 * D:(e % 2 + 1) * D],
                                                       scalar=wd1[:, bass.ds(n, 1), e:e + 1].rearrange("p o e -> p (o e)"), in1=x_n,
                                                       op0=ALU.mult, op1=ALU.add)
                        ins.then_inc(o1_acc.sem, 1)
                    wait(dve, o1_acc, c, 9 * t + 8)
                    dve.sem_inc(out_ready, 1)

            chunk(Batch(0))
            with dve.Fori(1, 4) as j:
                chunk(Batch(0, j, 1))

        @block.tensor
        def _(pe):
            pe.wait_ge(const_pool, N_CONST_POOL)

            def slot_of(layer):
                c = C[layer]

                def turn_in(dst, src, ps_name):
                    for t in range(TT):
                        for d in range(DT):
                            last = pe.transpose(dst[:, d * S + t * P:d * S + (t + 1) * P], src[:, t, d * P:(d + 1) * P], ident[:])
                    last.then_inc(c[ps_name].sem, 1)

                def turn_stack(src, rows, i, bank, ps_name):
                    for hh in range(4):
                        for t in range(TT):
                            last = pe.transpose(pMb[0:rows, bank, hh * S + t * P:hh * S + (t + 1) * P],
                                                src[:, t, 4 * i + hh, 0:rows], identb[:])
                    last.then_inc(c[ps_name].sem, 1)

                def scores_q(a, h):
                    if h % 4 == 0:
                        wait(pe, c["qt"], a, h // 4)
                        wait(pe, c["kt"], a, h // 4)
                    wait(pe, c["mx"], a, h - 2)
                    kt = k_t[a.parity][0:ROWS_A, h, :]
                    if layer == 0:
                        for t in range(TT):
                            last = pe.matmul(pA[:, h % 2, t * S:(t + 1) * S], q_t[0:ROWS_A, h, t * P:(t + 1) * P], kt,
                                             start=True, stop=True)
                    else:
                        for t, lo in ((0, 0), (1, P)):
                            pe.matmul(pA[:, h % 2, lo:lo + (t + 1) * P], q_t[0:ROWS_A, h, t * P:(t + 1) * P],
                                      kt[:, 0:(t + 1) * P], start=True, stop=False, skip_group_check=True)
                            last = pe.matmul(pA[:, h % 2, lo + t * P:lo + (t + 1) * P], identb[:], causal_q[:],
                                             start=False, stop=True, skip_group_check=True)
                    last.then_inc(c["a_ps"].sem, 1)

                def scores_k(b, h):
                    if h % 4 == 0:
                        wait(pe, c["qtm_a" if h // 4 % 2 else "qtm"], b, h // 8)
                    wait(pe, c["p"], b, h - 2)
                    q = q_tm[0:ROWS_B, h, :]
                    if layer == 0:
                        for t in range(TT):
                            last = pe.matmul(pB[:, h % 2, t * S:(t + 1) * S], k_t[b.parity][0:ROWS_B, h, t * P:(t + 1) * P], q,
                                             start=True, stop=True)
                    else:
                        for t, lo in ((0, 0), (1, S)):
                            pe.matmul(pB[:, h % 2, lo:lo + S - t * P], k_t[b.parity][0:ROWS_B, h, t * P:(t + 1) * P],
                                      q[:, t * P:S], start=True, stop=False, skip_group_check=True)
                            last = pe.matmul(pB[:, h % 2, lo:lo + P], identb[:], causal_k[:],
                                             start=False, stop=True, skip_group_check=True)
                    last.then_inc(c["b_ps"].sem, 1)

                def values(b, g):
                    if g == 0:
                        wait(pe, c["v"], b, 1)
                    wait(pe, c["p"], b, 4 * g + 3)
                    wait(pe, c["ot"], b, g - 1)
                    for t in range(TT):
                        lo = 0 if layer == 0 else t * P
                        for hh in range(4):
                            last = pe.matmul(pO[32 * hh:32 * hh + 32, g % 2, lo:S], v_aug[b.parity][:, t, 4 * g + hh, :],
                                             probs[g % 2][:, hh, t * S:t * S + S - lo], start=(t == 0), stop=(t == TT - 1),
                                             skip_group_check=True)
                    last.then_inc(c["pv"].sem, 1)

                def go(a, b, z):
                    if z is not None:
                        wait(pe, c["ot"], z, 3)
                        if b is not None:
                            wait(pe, c["qtm"], b, 1)
                            wait(pe, c["qtm_a"], b, 1)
                        for t in range(TT):
                            for g in range(4):
                                last = pe.transpose(pM[:, t, g * P:(g + 1) * P], o_t[:, g, t * P:(t + 1) * P], ident[:])
                        last.then_inc(c["ott"].sem, 1)
                    if a is not None:
                        wait(pe, c["qtm_a"], a.back(1), 0)
                        if layer == 0:
                            wait(pe, c["xn"], a, 1)
                            turn_in(pM[:, 2, :], xn, "xnT_ps")
                        else:
                            pe.wait_ge(ye_in[a.parity], 16 * (a.half + 1))
                            pe.wait_ge(gates_in[a.parity], 16 * (a.half + 1))
                            for t in range(TT):
                                for q in range(NPAIR):
                                    last = pe.matmul(pM[:, 2, t * D:(t + 1) * D], gates_s[a.parity][:, q, t * P:(t + 1) * P], ye_s[a.parity][:, q, :],
                                                     start=(q == 0), stop=(q == NPAIR - 1))
                            last.then_inc(c["sc_ps"].sem, 1)
                    for h in range(NH):
                        if b is not None:
                            scores_k(b, h)
                        if a is not None and layer == 0 and h == 2:
                            if z is None:
                                wait(pe, c["qtm_a"], a.back(1), 1)
                            else:
                                wait(pe, c["o"], z)
                            if a.turn is None and a.offset == 0:
                                pe.wait_ge(loaded["wqkv"], 32)
                            wait(pe, c["xnT"], a)
                            for t in range(TT):
                                for d in range(DT):
                                    last = pe.matmul(pM[:, 0, t * D:(t + 1) * D], xnT[:, d, t * P:(t + 1) * P], wq_s[:, d, :],
                                                     start=(d == 0), stop=(d == DT - 1))
                            last.then_inc(c["q_ps"].sem, 1)
                        if a is not None and layer == 0 and h in (3, 4):
                            t = h - 3
                            pe.wait_ge(ctx_in[0][a.parity], 16 * (a.half + 1))
                            if t == 0 and z is None:
                                wait(pe, c["qtm"], a.back(1), 1)
                            for d in range(DT):
                                last = pe.matmul(pM[:, 1 + t, :], ctx_s[a.parity][:, d, t * P:(t + 1) * P], wkv_s[:, d, :],
                                                 start=(d == 0), stop=(d == DT - 1))
                            last.then_inc(c["kv_ps"].sem, 1)
                        if h % 4 == 1 and h > 1 and b is not None:
                            values(b, h // 4 - 1)
                        if z is not None and h == 5:
                            wait(pe, c["xn2"], z, 1)
                            if layer == 0 and a is not None:
                                wait(pe, c["q32"], a)
                            else:
                                wait(pe, c["o"], z)
                            turn_in(pM[:, 0, :], xn_post, "x2T_ps")
                        if z is not None and layer == 0 and h == 7:
                            wait(pe, c["x2T"], z)
                            if a is not None:
                                wait(pe, c["v"], a, 0)
                            for t in range(TT):
                                for d in range(DT):
                                    last = pe.matmul(pM[:, 1, t * NE:(t + 1) * NE], xnT_post[:, d, t * P:(t + 1) * P],
                                                     gw0[:, d, :], start=(d == 0), stop=(d == DT - 1))
                            last.then_inc(c["lg_ps"].sem, 1)
                        if a is not None and 8 <= h < 12:
                            i = h - 8
                            if i == 0:
                                wait(pe, c["q3"], a)
                                wait(pe, c["x2"] if layer else c["v"], a, 1 - layer)
                            elif i == 1:
                                if z is not None:
                                    wait(pe, c["lg"] if layer == 0 else c["o"], z)
                                elif layer == 0:
                                    wait(pe, c["v"], a, 0)
                                else:
                                    wait(pe, c["qtm"], a.back(1), 1)
                            elif i == 2:
                                if z is not None:
                                    wait(pe, c["x2T"], z)
                                elif layer == 0:
                                    wait(pe, c["q32"], a)
                                else:
                                    wait(pe, c["qtm_a"], a.back(1), 1)
                            else:
                                wait(pe, c["qt"], a, 0)
                            turn_stack(q_nat, ROWS_A, i, (2, 1, 0, 2)[i], "qt_ps")
                        if a is not None and h >= 12:
                            i = h - 12
                            if i == 0:
                                wait(pe, c["kmask"] if layer == 0 else c["k3"], a)
                            if i < 3:
                                wait(pe, c["qt"], a, i + 1)
                            else:
                                wait(pe, c["kt"], a, 0)
                            turn_stack(k_nat, ROWS_B, i, (1, 0, 2, 1)[i], "kt_ps")
                    if b is not None:
                        values(b, 3)
                    if a is not None:
                        for h in range(NH):
                            scores_q(a, h)
                        wait(pe, c["m3"], a)
                        for i in range(4):
                            if i == 3:
                                wait(pe, c["qtm"], a, 0)
                            turn_stack(q_nat, ROWS_B, i, (0, 2, 1, 0)[i], "qtm_ps")
                return go

            slots(pe, slot_of(0))
            barrier(pe, 1)

            pe.wait_ge(route, 5)
            for t in range(TT):
                last = pe.transpose(pA[0:NB * NE, 0, t * P:(t + 1) * P], lg[:, t, :, :].rearrange("p b e -> p (b e)"), ident[:])
            last.then_inc(route_pe, 1)
            pe.wait_ge(route, 7 + CAP // 4)
            for t in range(TT):
                last = pe.transpose(pA[:, 1, 0:TT * NB * NE // 2].bitcast(BF16)[:, t * NB * NE:(t + 1) * NB * NE],
                                    selT[:, t * P:(t + 1) * P], identb[0:NB * NE, 0:NB * NE])
            last.then_inc(route_pe, 1)
            pe.wait_ge(route, 8 + CAP // 4)
            n = NB * NE
            pe.matmul(pB[:, 0, 0:n], upper[:], sel[:, 0, :], start=True, stop=True)
            pe.matmul(pB[:, 0, n:2 * n], onesb[:], sel[:, 0, :], start=True, stop=False)
            pe.matmul(pB[:, 0, n:2 * n], upper[:], sel[:, 1, :], start=False, stop=True).then_inc(route_pe, 1)

            def gather(b):
                for d, bank, free in ((0, pA, xin_ok), (1, pB, xin_act)):
                    wait(pe, free, b.back(2))
                    if d == 0:
                        wait(pe, onehot_ok, b, 1)
                    for t in range(TT):
                        for i in range(3):
                            last = pe.matmul(bank[:, b.parity, :],
                                             xn2s[:, bass.ds(b.n * TT + t, 1), i, d * P:(d + 1) * P].rearrange("p o d -> p (o d)"),
                                             onehot[:, t, bass.ds(b.n, 1), :].rearrange("p o s -> p (o s)"),
                                             start=(t == 0 and i == 0), stop=(t == TT - 1 and i == 2))
                    last.then_inc(gather_ps.sem, 1)

            pairs(pe, gather, NB)

            def expert(e):
                if e.turn is None and e.offset == 0:
                    pe.wait_ge(xin_ok.sem, NB)
                    pe.wait_ge(xin_act.sem, NB)
                for i in range(2):
                    pe.wait_ge(w_in[e.parity][i], 16 * (e.half + 1))
                for it in range(IT):
                    for w, bank, free, ps in ((wg_s, pA, silu_ok, g_ps), (wu_s, pB, h_ok, u_ps)):
                        wait(pe, free, e, it - 2)
                        for d in range(DT):
                            last = pe.matmul(bank[:, it % 2, :], w[e.parity][:, d, it * P:(it + 1) * P],
                                             xin[:, d, bass.ds(e.n, 1), :].rearrange("p o s -> p (o s)"),
                                             start=(d == 0), stop=(d == DT - 1))
                        last.then_inc(ps.sem, 1)
                for t in range(TT):
                    wait(pe, gated_ok, e, t)
                    wait(pe, gt_ok, e.back(1), t)
                    bank = pM[:, 2, :] if t == 0 else pO[:].rearrange("p a b -> p (a b)")
                    for q in range(NPAIR):
                        last = pe.transpose(bank[:, q * P:(q + 1) * P], gated[:, t, q * P:(q + 1) * P], ident[:])
                    last.then_inc(gt_ps.sem, 1)
                wait(pe, h_ok, e, IT - 1)
                pe.wait_ge(w_in[e.parity][2], 16 * (e.half + 1))
                for h in range(2):
                    wait(pe, y_ready, e.back(1), h)
                    for q in range(2):
                        tt = 2 * h + q
                        for it in range(IT):
                            last = pe.matmul(pM[:, h, q * D:(q + 1) * D], hT[:, it, tt * P:(tt + 1) * P], wd_s[e.parity][:, it, :],
                                             start=(it == 0), stop=(it == IT - 1))
                    last.then_inc(down_ps.sem, 1)

            pairs(pe, expert, NE)
            barrier(pe, 2)
            pe.wait_ge(const_l1, 4)
            pe.wait_ge(const_v1, 4)
            slots(pe, slot_of(1))
            barrier(pe, 3)

            for n in range(NT):
                for d in range(DT):
                    last = pe.matmul(pA[:, 0, n * NE1:(n + 1) * NE1], xnT_all[:, d, n * P:(n + 1) * P], gw1[:, d, :],
                                     start=(d == 0), stop=(d == DT - 1))
            last.then_inc(r1_pe, 1)
            pe.wait_ge(loaded["wl1"], 64)
            pe.wait_ge(r1, 1)

            def chunk(c):
                for i in range(4):
                    w, f = (wsi_s, i) if i < 2 else (w1_s, i - 2)
                    wait(pe, f1_act, c, i - 2)
                    wait(pe, f1_h, c, i - 2)
                    if i < 2:
                        wait(pe, o1_acc, c.back(1), 9 * (2 + i))
                    for k, bank in enumerate((pA, pB)):
                        for d in range(DT):
                            last = pe.matmul(bank[:, i % 2, :], w[:, d, k * H1 + f * P:k * H1 + (f + 1) * P],
                                             xnT_all[:, d, bass.ds(c.n * 512, 512)], start=(d == 0), stop=(d == DT - 1))
                        last.then_inc(f1_ps.sem, 1)
                for t in range(4):
                    wait(pe, f1_h, c, 3)
                    if t >= 2:
                        wait(pe, o1_acc, c, 9 * (t - 2))
                    for k in range(2):
                        last = pe.matmul(pA[:, t % 2, 0:D], hsT[:, k, t * P:(t + 1) * P], wso_s[:, k, :], start=(k == 0), stop=(k == 1))
                    last.then_inc(o1_ps.sem, 1)
                    for q in range(4):
                        wait(pe, o1_acc, c, 9 * (t - 1) + 2 * q + 2)
                        for k in range(2):
                            last = pe.matmul(out_bank(q), hrT[:, k, t * P:(t + 1) * P],
                                             w2_s[:, k, 2 * q:2 * q + 2, :].rearrange("p e d -> p (e d)"), start=(k == 0), stop=(k == 1))
                        last.then_inc(o1_ps.sem, 1)

            chunk(Batch(0))
            with pe.Fori(1, 4) as j:
                chunk(Batch(0, j, 1))


def kernel(x, ctx_1024, mask_BxS2_ik0, g_xattn, g_ffn, L0_xattn_Wq, L0_xattn_bq, L0_xattn_Wk, L0_xattn_bk,
           L0_xattn_Wv, L0_xattn_bv, L0_ffn_gate_w, L0_ffn_w_gate, L0_ffn_w_up, L0_ffn_w_down, L1_ffn_w_shared_in,
           L1_ffn_w_shared_out, L1_ffn_w1_shared, L1_ffn_w2, L1_ffn_w_gate, L1_ffn_gate_bias):
    import numpy as np
    import concourse.bacc as bacc
    from concourse.bass_utils import run_bass_kernel_spmd

    def rows(a):
        return np.ascontiguousarray(a.reshape(-1, P, a.shape[-1]).transpose(1, 0, 2))

    def turned_rows(a):
        return np.ascontiguousarray(a.reshape(a.shape[0], a.shape[1], -1, P).transpose(0, 3, 2, 1))

    a = {k: np.asarray(v) for k, v in locals().items() if k in INPUTS}
    arrays = {
        "x": rows(a["x"].reshape(NB * S, D)),
        "ctx": np.ascontiguousarray(a["ctx_1024"].reshape(NB, TT, P, D).transpose(0, 2, 1, 3)),
        "ctxT": turned_rows(a["ctx_1024"]),
        "mask": np.ascontiguousarray(a["mask_BxS2_ik0"].reshape(NT, P).T),
        "g_xattn": a["g_xattn"], "g_ffn": a["g_ffn"],
        "wq": rows(a["L0_xattn_Wq"].T),
        "wkv": rows(np.concatenate([a["L0_xattn_Wk"].T, a["L0_xattn_Wv"].T], axis=1)),
        "bq": a["L0_xattn_bq"], "bk": a["L0_xattn_bk"], "bv": a["L0_xattn_bv"],
        "gate0": rows(a["L0_ffn_gate_w"].T),
        "w_gate": turned_rows(a["L0_ffn_w_gate"]), "w_up": turned_rows(a["L0_ffn_w_up"]),
        "w_down": turned_rows(a["L0_ffn_w_down"]),
        "ws_in": rows(a["L1_ffn_w_shared_in"]), "ws_out": rows(a["L1_ffn_w_shared_out"]),
        "w1s": rows(a["L1_ffn_w1_shared"]),
        "w2": np.ascontiguousarray(a["L1_ffn_w2"].reshape(NE1, 2, P, D).transpose(2, 1, 0, 3)),
        "wg1": rows(a["L1_ffn_w_gate"]), "gbias": a["L1_ffn_gate_bias"],
    }
    nc = bacc.Bacc("TRN2", target_bir_lowering=False, num_devices=1)
    ins = {n: nc.dram_tensor(f"in_{n}", v.shape, mybir.dt.from_np(v.dtype), kind="ExternalInput").ap()
           for n, v in arrays.items()}
    out = nc.dram_tensor("out", (P, NT, D), F32, kind="ExternalOutput").ap()
    build_program(nc, out=out, **ins)
    r = run_bass_kernel_spmd(nc, [{f"in_{n}": v for n, v in arrays.items()}], core_ids=[0])
    got = np.asarray(r.results[0]["out"])
    return np.ascontiguousarray(got.transpose(1, 0, 2)).reshape(NB, S, D)


INPUTS = ("x", "ctx_1024", "mask_BxS2_ik0", "g_xattn", "g_ffn", "L0_xattn_Wq", "L0_xattn_bq", "L0_xattn_Wk",
          "L0_xattn_bk", "L0_xattn_Wv", "L0_xattn_bv", "L0_ffn_gate_w", "L0_ffn_w_gate", "L0_ffn_w_up",
          "L0_ffn_w_down", "L1_ffn_w_shared_in", "L1_ffn_w_shared_out", "L1_ffn_w1_shared", "L1_ffn_w2",
          "L1_ffn_w_gate", "L1_ffn_gate_bias")
```

```python
from contextlib import ExitStack

import concourse.bass as bass
from concourse import mybir

ALU = mybir.AluOpType
ACT = mybir.ActivationFunctionType
F32 = mybir.dt.float32
BF16 = mybir.dt.bfloat16
I32 = mybir.dt.int32
AX = mybir.AxisListType.X

P = 128
NB, S, D = 8, 256, 256
NH, W = 16, 16
TT = S // P
DT = D // P
NT = NB * TT
NE, I = 8, 1024
IT = I // P
CAP = S // NE * 2
SLOTS = NB * CAP
NPAIR = NE // 2
H1 = 256
NE1 = 8
EPS = 1e-5
SCALE = 0.25
NEG = -1.0e30

MASK0 = 6 * W
NMAX0 = MASK0 + 3
ROWS_A = NMAX0
ROWS_B = NMAX0 + 3
STACK = ROWS_B + 2


class Count:

    def __init__(self, sem, per, base=0):
        self.sem, self.per, self.base = sem, per, base

    def at(self, b, j=0):
        return b * self.per + (self.base + j + 1)


class Batch:

    def __init__(self, offset, turn=None, stride=2):
        self.offset, self.turn, self.stride = offset, turn, stride
        self.parity = offset % 2
        self.half = offset // 2 if turn is None else turn + offset // 2
        self.n = offset if turn is None else turn * stride + offset

    def back(self, n):
        return Batch(self.offset - n, self.turn, self.stride)


def wait(eng, count, b, j=0):
    if b.turn is not None or count.at(b.n, j) > 0:
        eng.wait_ge(count.sem, count.at(b.n, j))


def bcast(ap, dim, n):
    ap = ap.unsqueeze(dim)
    shape = list(ap.shape)
    shape[dim] = n
    return ap.broadcast_to(shape)


def build_program(nc, x, ctx, ctxT, mask, g_xattn, g_ffn, wq, wkv, bq, bk, bv, gate0, w_gate, w_up, w_down,
                  ws_in, ws_out, w1s, w2, wg1, gbias, out):
    with ExitStack() as keep:
        def sem(name):
            return keep.enter_context(nc.semaphore(name))

        def sb(name, shape, dt=F32, where=keep):
            return where.enter_context(nc.sbuf_tensor(name, shape, dt))

        xs = sb("xs", [P, NT, D])
        ident = sb("ident", [P, P])
        identb = sb("identb", [P, P], BF16)
        upper = sb("upper", [P, P], BF16)
        onesb = sb("onesb", [P, P], BF16)
        causal_q = sb("causal_q", [P, P], BF16)
        causal_k = sb("causal_k", [P, P], BF16)
        half = sb("half", [P, 3 * TT])
        zeros = sb("zeros", [P, TT, D])
        iota64 = sb("iota64", [P, CAP])
        tg = sb("tg", [P, 4])
        graw = sb("graw", [P, 4])
        gw0 = sb("gw0", [P, DT, NE])
        gw1 = sb("gw1", [P, DT, NE1])
        gb1 = sb("gb1", [P, NE1])
        maski = sb("maski", [P, NT], I32)
        maskr = sb("maskr", [P, 3, NT])
        maskp = sb("maskp", [P, NT, 3], BF16)
        lg = sb("lg", [P, TT, NB, NE])
        lgt = sb("lgt", [P, TT, NB, NE])
        lgs = sb("lgs", [P, TT * NB])
        sel = sb("sel", [P, TT, NB * NE], BF16)
        slot = sb("slot", [P, TT, NB * NE])

        ye = nc.dram_tensor("ye", [NB, NE * CAP, D], F32, kind="Internal").ap()
        gates = nc.dram_tensor("gates", [NB, P, NPAIR, S], F32, kind="Internal").ap()

        with ExitStack() as att:
            def ab(name, shape, dt=F32):
                return sb(name, shape, dt, att)

            xn2s = ab("xn2s", [P, NT, 3, D], BF16)
            xnT_all = xn2s[:, :, :, :].rearrange("p a b c -> p (a b c)")[:, 0:2 * DT * NB * S].bitcast(F32)\
                .rearrange("p (a b) -> p a b", a=DT)
            q_nat = [ab(f"q_nat{i}", [P, TT, NH, STACK], BF16) for i in range(2)]
            k_nat = [ab(f"k_nat{i}", [P, TT, NH, STACK], BF16) for i in range(2)]
            q_t = ab("q_t", [P, NH, S], BF16)
            q_tm = ab("q_tm", [P, NH, S], BF16)
            k_t = [ab(f"k_t{i}", [P, NH, S], BF16) for i in range(2)]
            v_aug = [ab(f"v_aug{i}", [P, TT, NH, 2 * W]) for i in range(2)]
            probs = [ab(f"probs{i}", [P, 4, TT * S]) for i in range(2)]
            o_t = ab("o_t", [P, 4, S])
            xn = ab("xn", [P, TT, D])
            xn_post = ab("xn_post", [P, TT, D])
            xnT = ab("xnT", [P, DT, S])
            xnT_post = ab("xnT_post", [P, DT, S])
            q32 = ab("q32", [P, TT, D])
            k32 = ab("k32", [P, TT, D])
            v32 = ab("v32", [P, TT, D])
            rq = ab("rq", [P, TT, D])
            rk = ab("rk", [P, TT, D])
            rx = ab("rx", [P, TT, D])
            o_nat = ab("o_nat", [P, TT, D])
            wq_s = ab("wq_s", [P, DT, D])
            wkv_s = ab("wkv_s", [P, DT, 2 * D])
            bq_s, bk_s, bv_s = (ab(n, [P, D]) for n in ("bq_s", "bk_s", "bv_s"))
            ctx_s = [ab(f"ctx_s{i}", [P, 2, 256]) for i in range(2)]
            ye_s = [ab(f"ye_s{i}", [P, NPAIR, D]) for i in range(2)]
            gates_s = [ab(f"gates_s{i}", [P, NPAIR, S]) for i in range(2)]
            st, st2 = ab("st", [P, TT, 6]), ab("st2", [P, TT, 6])
            mv, mv2 = ab("mv", [P, TT, 2]), ab("mv2", [P, TT, 2])
            rs, rs2 = ab("rs", [P, 2, TT]), ab("rs2", [P, 2, TT])
            mx = ab("mx", [P, TT, NH])
            mr = ab("mr", [P, TT, NH])
            rden = ab("rden", [P, 2, TT, NH])

        with ExitStack() as ffn:
            def fb(name, shape, dt=F32):
                return sb(name, shape, dt, ffn)

            fb("xn2s_place", [P, NT, 3, D], BF16)
            xin = fb("xin", [P, DT, NE, SLOTS])
            wg_s = [fb(f"wg_s{i}", [P, DT, I]) for i in range(2)]
            wu_s = [fb(f"wu_s{i}", [P, DT, I]) for i in range(2)]
            wd_s = [fb(f"wd_s{i}", [P, IT, D]) for i in range(2)]
            onehot = fb("onehot", [P, TT, NB, NE * CAP], BF16)
            silu = fb("silu", [P, 2, SLOTS])
            hT = fb("hT", [P, IT, SLOTS])
            y_s = fb("y_s", [P, 2, 2, D])
            gated = fb("gated", [P, TT, NE * CAP])
            gt_s = fb("gt_s", [P, TT, NPAIR, P])
            top = [fb(f"top{i}", [NB * NE, S]) for i in range(2)]
            top8 = fb("top8", [NB * NE, 8])
            selT = fb("selT", [NB * NE, S], BF16)

        with ExitStack() as last:
            def lb(name, shape, dt=F32):
                return sb(name, shape, dt, last)

            lb("xnT_all_place", [P, NT, 3, D], BF16)
            wsi_s = lb("wsi_s", [P, DT, 2 * H1])
            w1_s = lb("w1_s", [P, DT, 2 * H1])
            wso_s = lb("wso_s", [P, DT, D])
            w2_s = lb("w2_s", [P, DT, NE1, D])
            sact = lb("sact", [P, 2, 512])
            hsT = lb("hsT", [P, 2, 512])
            hrT = lb("hrT", [P, 2, 512])
            lg1 = lb("lg1", [P, NT, NE1])
            e1 = lb("e1", [P, NT, NE1])
            sm1 = lb("sm1", [P, NT])
            top1 = lb("tops_1", [P, NT, 2 * NE1])
            top1r = lb("tops_1r", [P, NT, 2 * NE1])
            best = lb("best", [P, NT, 8])
            find = lb("find", [P, NT, 8])
            wd1 = lb("wd1", [P, NT, NE1])

        pA, pB, pM = [keep.enter_context(nc.psum_tensor(n, [P, k, 512], F32)) for n, k in (("pA", 2), ("pB", 2), ("pM", 3))]
        pO = keep.enter_context(nc.psum_tensor("pO", [P, 2, S], F32))
        pMb = pM[:, :, :].bitcast(BF16)

        loaded = {n: sem(f"loaded_{n}") for n in ("x", "small", "wqkv", "wl1")}
        const_pool, const_dve, const_act = sem("const_pool"), sem("const_dve"), sem("const_act")
        const_l1 = sem("const_l1")
        settled = sem("settled")
        phase_end = sem("phase_end")
        ctx_in = [[sem(f"ctx_in{l}{i}") for i in range(2)] for l in range(2)]
        gates_in = [sem(f"gates_in{i}") for i in range(2)]
        ye_in = [sem(f"ye_in{i}") for i in range(2)]
        N_SMALL = 10
        N_CONST_POOL, N_CONST_DVE, N_CONST_ACT = 20, 11, 1

        both = dict(stat=2, mv=2, rs=2, xn=2, vc=1, q1=1, qr=1, q2=1, q3=1, k1=1, kr=1, k2=1, k3=1, qt_ps=4, qt=4,
                    kt_ps=4, kt=4, a_ps=NH, mx=NH, m1=4, mr=4, m2=4, m3=4, qtm_ps=4, qtm=4, b_ps=NH, p=NH,
                    pv=4, ot=4, ott=1, rden=2, o=1, xres=1, stat2=2, mv2=2, rs2=2, xn2=2, x2T_ps=1, x2T=1)
        only0 = dict(xnT_ps=1, xnT=1, q_ps=1, kv_ps=2, q32=1, k32=2, v=2, kmask=1, s1=1, sr=1, s2=1, s3=1, lg_ps=1, lg=1)
        only1 = dict(sc_ps=1, x2=1)
        C = [{n: Count(sem(n), per) for n, per in (both | only0).items()}, {}]
        C[1] = {n: Count(C[0][n].sem, per + (n == "rs"), NB * per) for n, per in both.items()}
        C[1] |= {n: Count(sem(n), per) for n, per in only1.items()}

        def barrier(eng, n):
            eng.drain().then_inc(phase_end, 1)
            eng.wait_ge(phase_end, 5 * n)

        def settle(eng):
            eng.sem_inc(settled, 1)

        def tile_of(n):
            return xs[:, bass.ds(n, 1), :].rearrange("p o d -> p (o d)")

        def stack(nat):
            return nat[:, :, :, 0:MASK0].rearrange("p t h (n w) -> p (t h) n w", w=W)

        def rep(nat, first, n):
            return stack(nat)[:, :, first:first + n, :]

        def rep_of(src, n):
            return bcast(src[:].rearrange("p t (h w) -> p (t h) w", w=W), 2, n)

        def part_of(nat, n):
            return nat[:, :, :, n * W:(n + 1) * W]

        def by_head(src):
            return src[:].rearrange("p t (h w) -> p t h w", w=W)

        def turned(bank, rows):
            return pMb[0:rows, bank, :].rearrange("p (h s) -> p h s", h=4)

        def out_bank(q):
            return pM[:, q, :] if q < 3 else pO[:].rearrange("p a b -> p (a b)")

        w_in = [[sem(f"w_in{p}{i}") for i in range(3)] for p in range(2)]
        y_ready = Count(sem("y_ready"), 2)
        gates_out = [sem("gates_out0"), sem("gates_out1")]
        y_out = [sem("y_out0"), sem("y_out1")]
        stored, out_ready = sem("stored"), sem("out_ready")
        g_ps, u_ps = Count(sem("g_ps"), IT), Count(sem("u_ps"), IT)
        silu_ok, h_ok = Count(sem("silu_ok"), IT), Count(sem("h_ok"), IT)
        down_ps = Count(sem("down_ps"), 2)
        gated_ok, gt_ps, gt_ok = Count(sem("gated_ok"), 2), Count(sem("gt_ps"), 2), Count(sem("gt_ok"), 2)
        onehot_ok, gather_ps = Count(sem("onehot_ok"), 2), Count(sem("gather_ps"), 2)
        route, route_act, route_pe = sem("route"), sem("route_act"), sem("route_pe")
        xin_ok, xin_act = Count(sem("xin_ok"), 1), Count(sem("xin_act"), 1)
        const_v1 = sem("const_v1")
        f1_ps, f1_act, f1_h = Count(sem("f1_ps"), 8), Count(sem("f1_act"), 4), Count(sem("f1_h"), 4)
        r1, r1_act, r1_pe = sem("r1"), sem("r1_act"), sem("r1_pe")
        o1_ps, o1_acc = Count(sem("o1_ps"), 20), Count(sem("o1_acc"), 36)

        block = keep.enter_context(nc.Block())

        def pairs(eng, body, n):
            body(Batch(0))
            body(Batch(1))
            with eng.Fori(1, n // 2) as j:
                body(Batch(0, j))
                body(Batch(1, j))

        def slots(eng, slot_of):
            slot_of(Batch(0), None, None, None)
            slot_of(Batch(1), Batch(0), None, None)
            slot_of(Batch(2), Batch(1), Batch(0), None)
            slot_of(Batch(3), Batch(2), Batch(1), Batch(0))
            with eng.Fori(0, 2) as j:
                slot_of(Batch(4, j), Batch(3, j), Batch(2, j), Batch(1, j))
                slot_of(Batch(5, j), Batch(4, j), Batch(3, j), Batch(2, j))
            slot_of(None, Batch(7), Batch(6), Batch(5))
            slot_of(None, None, Batch(7), Batch(6))
            slot_of(None, None, None, Batch(7))

        @block.sync
        def _(sp):
            for i, (dst, src) in enumerate(((maski[:], mask), (graw[:, 0:2], g_xattn.partition_broadcast(P)),
                                            (graw[:, 2:4], g_ffn.partition_broadcast(P)),
                                            (gw0[:], gate0), (gw1[:], wg1), (gb1[:], gbias.partition_broadcast(P)),
                                            (bq_s[:], bq.partition_broadcast(P)), (bk_s[:], bk.partition_broadcast(P)),
                                            (bv_s[:], bv.partition_broadcast(P)))):
                sp.dma_start(dst, src).then_inc(loaded["small"], 16)
            sp.dma_start(xs[:, 0:4, :], x[:, 0:4, :]).then_inc(loaded["small"], 16)
            sp.dma_start(wq_s[:], wq).then_inc(loaded["wqkv"], 16)
            sp.dma_start(ctx_s[0][:], ctxT[0]).then_inc(ctx_in[0][0], 16)
            sp.dma_start(wkv_s[:], wkv).then_inc(loaded["wqkv"], 16)
            sp.dma_start(ctx_s[1][:], ctxT[1]).then_inc(ctx_in[0][1], 16)
            sp.dma_start(xs[:, 4:NT, :], x[:, 4:NT, :]).then_inc(loaded["x"], 16)

            def ctx_loads(layer):
                src = (ctxT, ctx)[layer]
                c = C[layer]
                with sp.Fori(0, 3) as j:
                    for b in (Batch(2, j), Batch(3, j)):
                        if layer == 0:
                            wait(sp, c["kv_ps"], b.back(2), 1)
                        else:
                            wait(sp, c["vc"], b.back(2))
                            settle(sp)
                            wait(sp, c["sc_ps"], b.back(2))
                        settle(sp)
                        sp.dma_start(ctx_s[b.parity][:], src[bass.ds(b.n, 1)].rearrange("o p t d -> (o p) t d"))\
                          .then_inc(ctx_in[layer][b.parity], 16)
                        if layer == 1:
                            sp.dma_start(ye_s[b.parity][:], ye[bass.ds(b.n, 1)].rearrange("o (q p) d -> (o p) q d", p=P))\
                              .then_inc(ye_in[b.parity], 16)
                            sp.dma_start(gates_s[b.parity][:], gates[bass.ds(b.n, 1)].rearrange("o p q s -> (o p) q s"))\
                              .then_inc(gates_in[b.parity], 16)

            ctx_loads(0)
            barrier(sp, 1)

            def load_expert(e, n):
                for i, (dst, src) in enumerate(((wg_s, w_gate), (wu_s, w_up), (wd_s, w_down))):
                    s = src[bass.ds(n, 1)].rearrange("o p a b -> (o p) a b")
                    sp.dma_start(dst[e.parity][:], s).then_inc(w_in[e.parity][i], 16)

            load_expert(Batch(0), 0)
            load_expert(Batch(1), 1)

            def store_y(e):
                for t in range(TT):
                    wait(sp, gt_ok, e, t)
                    settle(sp)
                    sp.dma_start(gates[bass.ds(e.n, 1), :, :, t * P:(t + 1) * P].rearrange("o p q s -> (o p) q s"),
                                 gt_s[:, t, :, :]).then_inc(gates_out[t], 16)
                for h in range(2):
                    wait(sp, y_ready, e, h)
                    settle(sp)
                    for q in range(2):
                        tt = 2 * h + q
                        for b2 in range(2):
                            sp.dma_start(ye[2 * tt + b2, bass.ds(e.n * CAP, CAP), :],
                                         y_s[b2 * CAP:(b2 + 1) * CAP, h, q, :]).then_inc(y_out[h], 16)

            with sp.Fori(0, 3) as j:
                for e in (Batch(0, j), Batch(1, j)):
                    store_y(e)
                    wait(sp, down_ps, e, 1)
                    settle(sp)
                    load_expert(e, e.n + 2)
            for e in (Batch(6), Batch(7)):
                store_y(e)
            for h in range(2):
                sp.wait_ge(y_out[h], 16 * 4 * NE)
                sp.wait_ge(gates_out[h], 16 * NB)
            barrier(sp, 2)
            for b in range(2):
                sp.dma_start(ctx_s[b][:], ctx[b]).then_inc(ctx_in[1][b], 16)
                sp.dma_start(ye_s[b][:], ye[b].rearrange("(q p) d -> p q d", p=P)).then_inc(ye_in[b], 16)
                sp.dma_start(gates_s[b][:], gates[b]).then_inc(gates_in[b], 16)
            ctx_loads(1)
            barrier(sp, 3)
            for dst, src in ((wsi_s, ws_in), (w1_s, w1s), (wso_s, ws_out), (w2_s, w2)):
                sp.dma_start(dst[:], src).then_inc(loaded["wl1"], 16)
            with sp.Fori(0, NT) as n:
                sp.wait_ge(out_ready, n + 1)
                settle(sp)
                sp.dma_start(out[:, bass.ds(n, 1), :], xs[:, bass.ds(n, 1), :]).then_inc(stored, 16)
            sp.wait_ge(stored, 16 * NT)

        @block.gpsimd
        def _(pool):
            done = [0]

            def const(ins):
                done[0] += 1
                ins.then_inc(const_pool, 1)

            const(pool.memset(ident[:], 0.0))
            const(pool.memset(identb[:], 0.0))
            const(pool.memset(upper[:], 1.0))
            const(pool.memset(onesb[:], 1.0))
            const(pool.memset(causal_q[:], 0.0))
            const(pool.memset(causal_k[:], 0.0))
            const(pool.memset(half[:, 0:TT], -0.5))
            const(pool.memset(half[:, TT:2 * TT], EPS))
            const(pool.memset(half[:, 2 * TT:], SCALE))
            const(pool.memset(zeros[:], 0.0))
            const(pool.iota(iota64[:], pattern=[[1, CAP]], base=0, channel_multiplier=0,
                            allow_small_or_imprecise_dtypes=True))
            pool.wait_ge(const_pool, done[0])
            for m in (ident, identb):
                const(pool.affine_select(out=m[:], in_=m[:], compare_op=ALU.not_equal, fill=1.0, base=0,
                                         pattern=[[-1, P]], channel_multiplier=1))
            const(pool.affine_select(out=upper[:], in_=upper[:], compare_op=ALU.is_ge, fill=0.0, base=0,
                                     pattern=[[1, P]], channel_multiplier=-1))
            const(pool.affine_select(out=causal_q[:], in_=causal_q[:], compare_op=ALU.is_ge, fill=NEG, base=0,
                                     pattern=[[-1, P]], channel_multiplier=1))
            const(pool.affine_select(out=causal_k[:], in_=causal_k[:], compare_op=ALU.is_ge, fill=NEG, base=0,
                                     pattern=[[1, P]], channel_multiplier=-1))
            for i in range(2):
                const(pool.memset(q_nat[i][:, :, :, MASK0:NMAX0], 1.0))
                const(pool.memset(k_nat[i][:, :, :, NMAX0:ROWS_B], 1.0))
            assert done[0] == N_CONST_POOL

            def rstd(c, b, mvs, rss, mv_name, rs_name, used_name):
                wait(pool, c[mv_name], b, 1)
                wait(pool, c[used_name], b.back(1), 1)
                pool.tensor_tensor(rss[:, 0, :], mvs[:, :, 1], half[:, TT:2 * TT], ALU.add).then_inc(c[rs_name].sem, 1)
                wait(pool, c[rs_name], b, 0)
                pool.tensor_tensor(rss[:, 1, :], rss[:, 0, :], half[:, 0:TT], ALU.pow).then_inc(c[rs_name].sem, 1)

            def slot_of(layer):
                c = C[layer]

                def minus(out, in0, in1, name):
                    pool.tensor_tensor(out, in0, in1, ALU.subtract).then_inc(c[name].sem, 1)

                def go(n, a, b, z):
                    if a is not None:
                        if layer == 0:
                            wait(pool, c["v"], a, 1)
                        else:
                            pool.wait_ge(ctx_in[1][a.parity], 16 * (a.half + 1))
                        wait(pool, c["pv"], a.back(2), 3)
                        v = v32 if layer == 0 else ctx_s[a.parity]
                        pool.tensor_tensor(v_aug[a.parity][:, :, :, 0:W], by_head(v), by_head(zeros), ALU.add)\
                            .then_inc(c["vc"].sem, 1)
                    if n is not None and layer == 0:
                        rstd(c, n, mv, rs, "mv", "rs", "xn")
                    if z is not None:
                        x_z = xs[:, bass.ds(z.n * TT, TT), :]
                        wait(pool, c["o"], z)
                        settle(pool)
                        pool.tensor_tensor(x_z, x_z, o_nat[:], ALU.add).then_inc(c["xres"].sem, 1)
                        rstd(c, z, mv2, rs2, "mv2", "rs2", "xn2")
                    if n is not None and layer == 1:
                        rstd(c, n, mv, rs, "mv", "rs", "xn")
                        wait(pool, c["rs"], n, 1)
                        pool.tensor_tensor(rs[:, 1, :], rs[:, 1, :], half[:, 2 * TT:], ALU.mult).then_inc(c["rs"].sem, 1)
                    if n is not None:
                        qn, kn = q_nat[n.parity], k_nat[n.parity]
                        wait(pool, c["q1"], n)
                        minus(by_head(rq), by_head(q32), part_of(qn, 0), "qr")
                        wait(pool, c["q2"], n)
                        minus(part_of(qn, 3), by_head(rq), part_of(qn, 4), "q3")
                        wait(pool, c["k1"], n)
                        minus(by_head(rk), by_head(k32 if layer == 0 else ctx_s[n.parity]), part_of(kn, 2), "kr")
                        wait(pool, c["k2"], n)
                        minus(part_of(kn, 1), by_head(rk), part_of(kn, 0), "k3")
                    if z is not None and layer == 0:
                        part = [xn2s[:, bass.ds(z.n * TT, TT), i, :] for i in range(3)]
                        wait(pool, c["xn2"], z, 1)
                        settle(pool)
                        pool.tensor_tensor(part[0], xn_post[:], zeros[:], ALU.add).then_inc(c["s1"].sem, 1)
                        wait(pool, c["s1"], z)
                        settle(pool)
                        minus(rx[:], xn_post[:], part[0], "sr")
                        wait(pool, c["sr"], z)
                        settle(pool)
                        pool.tensor_tensor(part[1], rx[:], zeros[:], ALU.add).then_inc(c["s2"].sem, 1)
                        wait(pool, c["s2"], z)
                        settle(pool)
                        minus(part[2], rx[:], part[1], "s3")
                return go

            slots(pool, slot_of(0))
            barrier(pool, 1)
            barrier(pool, 2)
            for i in range(2):
                pool.memset(q_nat[i][:, :, :, MASK0:NMAX0], 1.0).then_inc(const_l1, 1)
                pool.memset(k_nat[i][:, :, :, NMAX0:ROWS_B], 1.0).then_inc(const_l1, 1)
                pool.memset(k_nat[i][:, :, :, MASK0:NMAX0], 0.0).then_inc(const_l1, 1)
            slots(pool, slot_of(1))
            barrier(pool, 3)

        @block.scalar
        def _(act):
            act.wait_ge(loaded["small"], 16 * N_SMALL)
            act.activation(tg[:], graw[:], ACT.Tanh).then_inc(const_act, 1)

            def slot_of(layer):
                c = C[layer]
                width = 2 * S if layer == 0 else S + P

                def take_q(a, i):
                    wait(act, c["qt_ps"], a, i)
                    wait(act, c["a_ps"], a.back(1), 4 * i + 3)
                    act.activation(q_t[0:ROWS_A, 4 * i:4 * i + 4, :], turned(2, ROWS_A), ACT.Copy).then_inc(c["qt"].sem, 1)

                def take_qm(a, i):
                    wait(act, c["qtm_ps"], a, i)
                    wait(act, c["b_ps"], a.back(1), 4 * i + 3)
                    act.activation(q_tm[0:ROWS_B, 4 * i:4 * i + 4, :], turned(2, ROWS_B), ACT.Copy).then_inc(c["qtm"].sem, 1)

                def go(n, a, b, z):
                    if a is not None:
                        take_q(a, 0)
                    for h in range(NH):
                        if b is not None:
                            wait(act, c["b_ps"], b, h)
                            wait(act, c["pv"], b, h // 4 - 2)
                            act.activation(probs[h // 4 % 2][:, h % 4, 0:width], pB[:, h % 2, 0:width], ACT.Exp)\
                               .then_inc(c["p"].sem, 1)
                        if a is not None:
                            if h in (1, 5, 9):
                                take_q(a, (h + 3) // 4)
                            if h in (7, 11, 15):
                                take_qm(a, h // 4 - 1)
                        if h == 11 and z is not None:
                            wait(act, c["x2T_ps"], z)
                            src = pM[:, 0, :].rearrange("p (a b) -> p a b", a=DT)
                            if layer == 0:
                                wait(act, c["lg_ps"], z, -1)
                                act.activation(xnT_post[:], src, ACT.Copy).then_inc(c["x2T"].sem, 1)
                            else:
                                settle(act)
                                act.activation(xnT_all[:, :, bass.ds(z.n * S, S)], src, ACT.Copy).then_inc(c["x2T"].sem, 1)
                        if n is None:
                            continue
                        qn, kn = q_nat[n.parity], k_nat[n.parity]
                        if h == 4 and layer == 0:
                            wait(act, c["xnT_ps"], n)
                            wait(act, c["q_ps"], n.back(1))
                            act.activation(xnT[:], pM[:, 0, :].rearrange("p (a b) -> p a b", a=DT), ACT.Copy)\
                               .then_inc(c["xnT"].sem, 1)
                        if h == 6:
                            wait(act, c["xn" if layer else "q32"], n, layer)
                            wait(act, c["qtm_ps"], n.back(2), 3)
                            act.activation(rep(qn, 0, 3), rep_of(q32, 3), ACT.Copy).then_inc(c["q1"].sem, 1)
                        if h == 8:
                            wait(act, c["qr"], n)
                            act.activation(rep(qn, 4, 2), rep_of(rq, 2), ACT.Copy).then_inc(c["q2"].sem, 1)
                        if h == 10:
                            if layer == 0:
                                wait(act, c["k32"], n, 1)
                                src = k32
                            else:
                                act.wait_ge(ctx_in[1][n.parity], 16 * (n.half + 1))
                                src = ctx_s[n.parity]
                            wait(act, c["kt_ps"], n.back(2), 3)
                            act.activation(rep(kn, 2, 3), rep_of(src, 3), ACT.Copy).then_inc(c["k1"].sem, 1)
                        if h == 13:
                            wait(act, c["kr"], n)
                            act.activation(stack(kn)[:, :, 0:6:5, :], rep_of(rk, 2), ACT.Copy).then_inc(c["k2"].sem, 1)
                    if a is not None:
                        take_qm(a, 3)
                return go

            slots(act, slot_of(0))
            barrier(act, 1)
            act.wait_ge(route, 2)
            act.activation(lg[:], lgt[:], ACT.Exp).then_inc(route_act, 1)

            def gather(b):
                wait(act, gather_ps, b, 1)
                settle(act)
                act.activation(xin[:, 1, :, bass.ds(b.n * CAP, CAP)], pB[:, b.parity, :].rearrange("p (e s) -> p e s", e=NE),
                               ACT.Copy).then_inc(xin_act.sem, 1)

            pairs(act, gather, NB)

            def expert(e):
                for it in range(IT):
                    wait(act, g_ps, e, it)
                    wait(act, h_ok, e, it - 2)
                    act.activation(silu[:, it % 2, :], pA[:, it % 2, :], ACT.Silu).then_inc(silu_ok.sem, 1)

            pairs(act, expert, NE)
            barrier(act, 2)
            slots(act, slot_of(1))
            barrier(act, 3)
            act.wait_ge(r1, 3)
            act.activation(e1[:], lg1[:], ACT.Exp).then_inc(r1_act, 1)

            def chunk(c):
                for i in range(4):
                    wait(act, f1_ps, c, 2 * i)
                    wait(act, f1_h, c, i - 2)
                    act.activation(sact[:, i % 2, :], pA[:, i % 2, :], ACT.Silu).then_inc(f1_act.sem, 1)

            chunk(Batch(0))
            with act.Fori(1, 4) as j:
                chunk(Batch(0, j, 1))

        @block.vector
        def _(dve):
            n_const = [0]

            def const(ins):
                n_const[0] += 1
                ins.then_inc(const_dve, 1)

            def v_const(count):
                for v in v_aug:
                    count(dve.memset(v[:, :, :, W:W + 1], 1.0))
                    count(dve.memset(v[:, :, :, W + 1:2 * W], 0.0))

            v_const(const)
            dve.wait_ge(loaded["small"], 16 * N_SMALL)
            const(dve.tensor_scalar(bq_s[:], bq_s[:], SCALE, None, ALU.mult))
            const(dve.tensor_copy(maskr[:, 0, :], maski[:]))
            dve.wait_ge(const_dve, n_const[0])
            const(dve.tensor_scalar(maskr[:, 1, :], maskr[:, 0, :], 10000.0, -10000.0, ALU.mult, ALU.add))
            dve.wait_ge(const_dve, n_const[0])
            const(dve.tensor_copy(maskp[:, :, 0], maskr[:, 1, :]))
            dve.wait_ge(const_dve, n_const[0])
            const(dve.tensor_tensor(maskr[:, 2, :], maskr[:, 1, :], maskp[:, :, 0], ALU.subtract))
            dve.wait_ge(const_dve, n_const[0])
            const(dve.tensor_copy(maskp[:, :, 1], maskr[:, 2, :]))
            dve.wait_ge(const_dve, n_const[0])
            const(dve.tensor_tensor(maskp[:, :, 2], maskr[:, 2, :], maskp[:, :, 1], ALU.subtract))
            assert n_const[0] == N_CONST_DVE
            dve.wait_ge(const_dve, N_CONST_DVE)
            dve.wait_ge(const_pool, N_CONST_POOL)
            dve.wait_ge(const_act, N_CONST_ACT)

            def slot_of(layer):
                c = C[layer]

                def inc(name):
                    return c[name].sem, 1

                def x_of(b):
                    return xs[:, bass.ds(b.n * TT, TT), :]

                def statistics(b, stt, mvv, stat, mv_name):
                    settle(dve)
                    for t in range(TT):
                        dve.bn_stats(stt[:, t, :], tile_of(b.n * TT + t)).then_inc(*inc(stat))
                    for t in range(TT):
                        wait(dve, c[stat], b, t)
                        settle(dve)
                        dve.bn_aggr(mvv[:, t, :], stt[:, t, :]).then_inc(*inc(mv_name))

                def normalise(b, dst, mvv, rss, name):
                    for t in range(TT):
                        dve.tensor_scalar(dst[:, t, :], tile_of(b.n * TT + t), mvv[:, t, 0:1],
                                          rss[:, 1, t:t + 1], ALU.subtract, ALU.mult).then_inc(*inc(name))

                def take_o(b, g):
                    wait(dve, c["pv"], b, g)
                    wait(dve, c["ott"], b.back(1))
                    dve.tensor_copy(o_t[:, g, :], pO[:, g % 2, :]).then_inc(*inc("ot"))

                def take_k(a, i):
                    wait(dve, c["kt_ps"], a, i)
                    wait(dve, c["b_ps"], a.back(2), 4 * i + 3)
                    dve.tensor_copy(k_t[a.parity][0:ROWS_B, 4 * i:4 * i + 4, :], turned(2, ROWS_B)).then_inc(*inc("kt"))

                def maximum(a, h):
                    wait(dve, c["a_ps"], a, h)
                    if layer == 0:
                        dve.tensor_reduce(mx[:, :, h], pA[:, h % 2, :].rearrange("p (t k) -> p t k", t=TT), AX, ALU.max)\
                           .then_inc(*inc("mx"))
                    else:
                        dve.tensor_reduce(mx[:, 0, h:h + 1], pA[:, h % 2, 0:P], AX, ALU.max)
                        dve.tensor_reduce(mx[:, 1, h:h + 1], pA[:, h % 2, P:P + S], AX, ALU.max).then_inc(*inc("mx"))

                def minus_maximum(a, i):
                    part = [q_nat[a.parity][:, :, 4 * i:4 * i + 4, NMAX0 + k] for k in range(3)]
                    m, rest = mx[:, :, 4 * i:4 * i + 4], mr[:, :, 4 * i:4 * i + 4]
                    wait(dve, c["mx"], a, 4 * i + 3)
                    dve.tensor_scalar(part[0], m, -1.0, None, ALU.mult).then_inc(*inc("m1"))
                    wait(dve, c["m1"], a, i)
                    dve.scalar_tensor_tensor(out=rest, in0=m, scalar=-1.0, in1=part[0], op0=ALU.mult, op1=ALU.subtract)\
                       .then_inc(*inc("mr"))
                    wait(dve, c["mr"], a, i)
                    dve.tensor_copy(part[1], rest).then_inc(*inc("m2"))
                    wait(dve, c["m2"], a, i)
                    dve.tensor_tensor(part[2], rest, part[1], ALU.subtract).then_inc(*inc("m3"))

                def output(z):
                    o_ps = pM[:, 0:TT, :].rearrange("p t (h w) -> p t h w", w=2 * W)
                    wait(dve, c["ott"], z)
                    dve.reciprocal(rden[:, 0, :, :], o_ps[:, :, :, W]).then_inc(*inc("rden"))
                    wait(dve, c["rden"], z, 0)
                    dve.tensor_scalar(rden[:, 1, :, :], rden[:, 0, :, :], tg[:, layer:layer + 1], None, ALU.mult)\
                       .then_inc(*inc("rden"))
                    wait(dve, c["rden"], z, 1)
                    wait(dve, c["xres"], z.back(1))
                    dve.tensor_tensor(by_head(o_nat), o_ps[:, :, :, 0:W], bcast(rden[:, 1, :, :], 3, W), ALU.mult)\
                       .then_inc(*inc("o"))

                def take_kv(n, t):
                    wait(dve, c["kv_ps"], n, t)
                    wait(dve, c["kr"], n.back(1))
                    dve.tensor_tensor(k32[:, t, :], pM[:, t, 0:D], bk_s[:], ALU.add).then_inc(*inc("k32"))
                    wait(dve, c["vc"], n.back(1))
                    dve.tensor_tensor(v32[:, t, :], pM[:, t, D:2 * D], bv_s[:], ALU.add).then_inc(*inc("v"))

                def go(n, a, b, z):
                    if a is not None:
                        take_k(a, 0)
                    if z is not None:
                        output(z)
                    for h in range(NH):
                        if a is not None:
                            maximum(a, h)
                            if h % 4 == 3:
                                minus_maximum(a, h // 4)
                            if h in (2, 6, 10):
                                take_k(a, (h + 2) // 4)
                        if b is not None and h in (6, 10, 14):
                            take_o(b, h // 4 - 1)
                        if z is not None:
                            if h == 1:
                                wait(dve, c["xres"], z)
                                statistics(z, st2, mv2, "stat2", "mv2")
                            if h == 7:
                                wait(dve, c["rs2"], z, 1)
                                wait(dve, c["x2T_ps"], z.back(1))
                                if layer == 0:
                                    wait(dve, c["sr"], z.back(1))
                                settle(dve)
                                normalise(z, xn_post, mv2, rs2, "xn2")
                            if h == 13 and layer == 0:
                                wait(dve, c["lg_ps"], z)
                                settle(dve)
                                dve.tensor_copy(lg[:, :, bass.ds(z.n, 1), :],
                                                pM[:, 1, 0:TT * NE].rearrange("p (t e) -> p t e", t=TT)).then_inc(*inc("lg"))
                        if n is None:
                            continue
                        if h == 0 and layer == 0:
                            if n.turn is None and n.offset == 1:
                                dve.wait_ge(loaded["x"], 16)
                            statistics(n, st, mv, "stat", "mv")
                        if h == 2 and layer == 1:
                            wait(dve, c["sc_ps"], n)
                            settle(dve)
                            x_n = xs[:, bass.ds(n.n * TT, TT), :]
                            dve.tensor_tensor(x_n, x_n, pM[:, 0, :].rearrange("p (t d) -> p t d", t=TT), ALU.add)\
                               .then_inc(*inc("x2"))
                            wait(dve, c["x2"], n)
                            statistics(n, st, mv, "stat", "mv")
                        if h == 2 + 2 * layer:
                            wait(dve, c["rs"], n, 1 + layer)
                            if layer == 0:
                                wait(dve, c["xnT_ps"], n.back(1))
                            else:
                                wait(dve, c["qr"], n.back(1))
                            normalise(n, (xn, q32)[layer], mv, rs, "xn")
                        if layer == 0:
                            if h == 5:
                                wait(dve, c["q_ps"], n)
                                wait(dve, c["qr"], n.back(1))
                                dve.scalar_tensor_tensor(out=q32[:], in0=pM[:, 1, :].rearrange("p (t d) -> p t d", t=TT),
                                                         scalar=SCALE, in1=bcast(bq_s[:], 1, TT), op0=ALU.mult, op1=ALU.add)\
                                   .then_inc(*inc("q32"))
                            if h in (7, 9):
                                take_kv(n, h // 2 - 3)
                            if h == 12:
                                wait(dve, c["kt_ps"], n.back(2), 3)
                                settle(dve)
                                dve.tensor_copy(k_nat[n.parity][:, :, :, MASK0:NMAX0],
                                                bcast(maskp[:, bass.ds(n.n * TT, TT), :], 2, NH)).then_inc(*inc("kmask"))
                    if b is not None:
                        take_o(b, 3)
                return go

            slots(dve, slot_of(0))
            barrier(dve, 1)

            step = [0]

            def then(ins, sem_=route):
                step[0] += 1
                ins.then_inc(sem_, 1)
                dve.wait_ge(sem_, step[0])

            lg3 = lg[:].rearrange("p t b e -> p (t b) e")
            lgt3 = lgt[:].rearrange("p t b e -> p (t b) e")
            then(dve.tensor_reduce(lgs[:], lg3, AX, ALU.max))
            then(dve.tensor_tensor(lgt3, lg3, bcast(lgs[:], 2, NE), ALU.subtract))
            dve.wait_ge(route_act, 1)
            then(dve.tensor_reduce(lgs[:], lg3, AX, ALU.add))
            then(dve.reciprocal(lgs[:], lgs[:]))
            then(dve.tensor_tensor(lg3, lg3, bcast(lgs[:], 2, NE), ALU.mult))
            assert step[0] == 5
            dve.wait_ge(route_pe, 1)
            then(dve.tensor_copy(top[0][:], pA[0:NB * NE, 0, 0:S]))
            for r in range(CAP // 8):
                then(dve.max(top8[:], top[r % 2][:]))
                then(dve.match_replace(top[1 - r % 2][:], top8[:], top[r % 2][:], -1.0))
            then(dve.tensor_scalar(selT[:], top[0][:], 0.0, None, ALU.is_lt))
            assert step[0] == 7 + CAP // 4
            dve.wait_ge(route_pe, 2)
            then(dve.tensor_copy(sel[:], pA[:, 1, 0:TT * NB * NE // 2].bitcast(BF16).rearrange("p (t n) -> p t n", t=TT)))
            dve.wait_ge(route_pe, 3)
            then(dve.tensor_tensor(slot[:], pB[:, 0, 0:TT * NB * NE].rearrange("p (t n) -> p t n", t=TT), sel[:], ALU.mult))
            then(dve.tensor_scalar(slot[:], slot[:], -1.0, None, ALU.add))
            then(dve.tensor_scalar(lg3, lg3, tg[:, 2:3], None, ALU.mult))

            def gather(b):
                for t in range(TT):
                    dve.tensor_tensor(onehot[:, t, bass.ds(b.n, 1), :].rearrange("p o (e s) -> p (o e) s", e=NE),
                                      bcast(iota64[:], 1, NE), bcast(slot[:, t, bass.ds(b.n * NE, NE)], 2, CAP),
                                      ALU.is_equal).then_inc(onehot_ok.sem, 1)
                wait(dve, gather_ps, b, 0)
                settle(dve)
                dve.tensor_copy(xin[:, 0, :, bass.ds(b.n * CAP, CAP)], pA[:, b.parity, :].rearrange("p (e s) -> p e s", e=NE))\
                   .then_inc(xin_ok.sem, 1)

            pairs(dve, gather, NB)

            def expert(e):
                for t in range(TT):
                    wait(dve, gt_ps, e.back(1), t)
                    settle(dve)
                    dve.tensor_tensor(gated[:, t, :].rearrange("p (e s) -> p e s", e=NE),
                                      onehot[:, t, bass.ds(e.n, 1), :].rearrange("p o (e s) -> p (o e) s", e=NE),
                                      bcast(lg[:, t, bass.ds(e.n, 1), :].rearrange("p o e -> p (o e)"), 2, CAP),
                                      ALU.mult).then_inc(gated_ok.sem, 1)
                for it in range(IT):
                    wait(dve, silu_ok, e, it)
                    wait(dve, u_ps, e, it)
                    if it == 0:
                        wait(dve, down_ps, e.back(1), 1)
                    dve.tensor_tensor(hT[:, it, :], silu[:, it % 2, :], pB[:, it % 2, :], ALU.mult).then_inc(h_ok.sem, 1)
                for t in range(TT):
                    wait(dve, gt_ps, e, t)
                    settle(dve)
                    bank = pM[:, 2, :] if t == 0 else pO[:].rearrange("p a b -> p (a b)")
                    if e.turn is not None or e.offset > 0:
                        dve.wait_ge(gates_out[t], e.n * 16)
                    dve.tensor_copy(gt_s[:, t, :, :], bank.rearrange("p (q s) -> p q s", q=NPAIR)).then_inc(gt_ok.sem, 1)
                for h in range(2):
                    wait(dve, down_ps, e, h)
                    if e.turn is not None or e.offset > 0:
                        dve.wait_ge(y_out[h], e.n * 64)
                    dve.tensor_copy(y_s[:, h, :, :], pM[:, h, :].rearrange("p (q d) -> p q d", q=2)).then_inc(y_ready.sem, 1)

            pairs(dve, expert, NE)
            barrier(dve, 2)
            v_const(lambda ins: ins.then_inc(const_v1, 1))
            dve.wait_ge(const_v1, 4)
            slots(dve, slot_of(1))
            barrier(dve, 3)

            step[0] = 0

            def then1(ins):
                then(ins, r1)

            dve.wait_ge(r1_pe, 1)
            then1(dve.tensor_tensor(lg1[:], pA[:, 0, 0:NT * NE1].rearrange("p (n e) -> p n e", n=NT), bcast(gb1[:], 1, NT), ALU.add))
            then1(dve.tensor_reduce(sm1[:], lg1[:], AX, ALU.max))
            then1(dve.tensor_tensor(lg1[:], lg1[:], bcast(sm1[:], 2, NE1), ALU.subtract))
            dve.wait_ge(r1_act, 1)
            then1(dve.tensor_reduce(sm1[:], e1[:], AX, ALU.add))
            then1(dve.reciprocal(sm1[:], sm1[:]))
            then1(dve.tensor_tensor(top1[:, :, 0:NE1], e1[:], bcast(sm1[:], 2, NE1), ALU.mult))
            then1(dve.memset(top1[:, :, NE1:2 * NE1], -2.0))
            then1(dve.memset(find[:, :, 2:8], -2.0))
            for n in range(NT):
                then1(dve.max(best[:, n, :], top1[:, n, 0:NE1]))
            then1(dve.tensor_copy(find[:, :, 0:2], best[:, :, 0:2]))
            for n in range(NT):
                then1(dve.match_replace(top1r[:, n, :], find[:, n, :], top1[:, n, :], -2.0))
            then1(dve.scalar_tensor_tensor(out=wd1[:], in0=top1r[:, :, 0:NE1], scalar=-1.0, in1=top1[:, :, 0:NE1],
                                           op0=ALU.is_lt, op1=ALU.mult))
            then1(dve.tensor_scalar(wd1[:], wd1[:], tg[:, 3:4], None, ALU.mult))

            def chunk(c):
                for i in range(4):
                    wait(dve, f1_act, c, i)
                    wait(dve, f1_ps, c, 2 * i + 1)
                    dst = hsT[:, i, :] if i < 2 else hrT[:, i - 2, :]
                    dve.tensor_tensor(dst, sact[:, i % 2, :], pB[:, i % 2, :], ALU.mult).then_inc(f1_h.sem, 1)
                for t in range(4):
                    n = c.n * 4 + t
                    x_n = tile_of(n)
                    wait(dve, o1_ps, c, 5 * t)
                    settle(dve)
                    dve.scalar_tensor_tensor(out=x_n, in0=pA[:, t % 2, 0:D], scalar=tg[:, 3:4], in1=x_n, op0=ALU.mult, op1=ALU.add)\
                       .then_inc(o1_acc.sem, 1)
                    for e in range(NE1):
                        if e % 2 == 0:
                            wait(dve, o1_ps, c, 5 * t + 1 + e // 2)
                        wait(dve, o1_acc, c, 9 * t + e)
                        settle(dve)
                        ins = dve.scalar_tensor_tensor(out=x_n, in0=out_bank(e // 2)[:, e % 2 * D:(e % 2 + 1) * D],
                                                       scalar=wd1[:, bass.ds(n, 1), e:e + 1].rearrange("p o e -> p (o e)"), in1=x_n,
                                                       op0=ALU.mult, op1=ALU.add)
                        ins.then_inc(o1_acc.sem, 1)
                    wait(dve, o1_acc, c, 9 * t + 8)
                    dve.sem_inc(out_ready, 1)

            chunk(Batch(0))
            with dve.Fori(1, 4) as j:
                chunk(Batch(0, j, 1))

        @block.tensor
        def _(pe):
            pe.wait_ge(const_pool, N_CONST_POOL)

            def slot_of(layer):
                c = C[layer]

                def turn_in(dst, src, ps_name):
                    for t in range(TT):
                        for d in range(DT):
                            last = pe.transpose(dst[:, d * S + t * P:d * S + (t + 1) * P], src[:, t, d * P:(d + 1) * P], ident[:])
                    last.then_inc(c[ps_name].sem, 1)

                def turn_stack(src, rows, i, ps_name):
                    for hh in range(4):
                        for t in range(TT):
                            last = pe.transpose(pMb[0:rows, 2, hh * S + t * P:hh * S + (t + 1) * P],
                                                src[:, t, 4 * i + hh, 0:rows], identb[:])
                    last.then_inc(c[ps_name].sem, 1)

                def scores_q(a, h):
                    if h % 4 == 0:
                        wait(pe, c["qt"], a, h // 4)
                        wait(pe, c["kt"], a, h // 4)
                    wait(pe, c["mx"], a, h - 2)
                    kt = k_t[a.parity][0:ROWS_A, h, :]
                    if layer == 0:
                        for t in range(TT):
                            last = pe.matmul(pA[:, h % 2, t * S:(t + 1) * S], q_t[0:ROWS_A, h, t * P:(t + 1) * P], kt,
                                             start=True, stop=True)
                    else:
                        for t, lo in ((0, 0), (1, P)):
                            pe.matmul(pA[:, h % 2, lo:lo + (t + 1) * P], q_t[0:ROWS_A, h, t * P:(t + 1) * P],
                                      kt[:, 0:(t + 1) * P], start=True, stop=False, skip_group_check=True)
                            last = pe.matmul(pA[:, h % 2, lo + t * P:lo + (t + 1) * P], identb[:], causal_q[:],
                                             start=False, stop=True, skip_group_check=True)
                    last.then_inc(c["a_ps"].sem, 1)

                def scores_k(b, h):
                    if h % 4 == 0:
                        wait(pe, c["qtm"], b, h // 4)
                    wait(pe, c["p"], b, h - 2)
                    q = q_tm[0:ROWS_B, h, :]
                    if layer == 0:
                        for t in range(TT):
                            last = pe.matmul(pB[:, h % 2, t * S:(t + 1) * S], k_t[b.parity][0:ROWS_B, h, t * P:(t + 1) * P], q,
                                             start=True, stop=True)
                    else:
                        for t, lo in ((0, 0), (1, S)):
                            pe.matmul(pB[:, h % 2, lo:lo + S - t * P], k_t[b.parity][0:ROWS_B, h, t * P:(t + 1) * P],
                                      q[:, t * P:S], start=True, stop=False, skip_group_check=True)
                            last = pe.matmul(pB[:, h % 2, lo:lo + P], identb[:], causal_k[:],
                                             start=False, stop=True, skip_group_check=True)
                    last.then_inc(c["b_ps"].sem, 1)

                def values(b, g):
                    if g == 0:
                        wait(pe, c["vc"], b)
                    wait(pe, c["p"], b, 4 * g + 3)
                    wait(pe, c["ot"], b, g - 1)
                    for t in range(TT):
                        lo = 0 if layer == 0 else t * P
                        for hh in range(4):
                            last = pe.matmul(pO[32 * hh:32 * hh + 32, g % 2, lo:S], v_aug[b.parity][:, t, 4 * g + hh, :],
                                             probs[g % 2][:, hh, t * S:t * S + S - lo], start=(t == 0), stop=(t == TT - 1),
                                             skip_group_check=True)
                    last.then_inc(c["pv"].sem, 1)

                def turn_q(a, i):
                    if i == 0:
                        wait(pe, c["q3"], a)
                        wait(pe, c["qtm"], a, -1)
                    elif i < 3:
                        wait(pe, c["kt"], a, i - 1)
                    else:
                        wait(pe, c["qtm"], a, 0)
                    turn_stack(q_nat[a.parity], ROWS_A, i, "qt_ps")

                def turn_k(a, i):
                    if i == 0:
                        wait(pe, c["k3"], a)
                        if layer == 0:
                            wait(pe, c["kmask"], a)
                    wait(pe, c["qt"], a, i)
                    turn_stack(k_nat[a.parity], ROWS_B, i, "kt_ps")

                def turn_qm(a, i):
                    wait(pe, c["m3"], a, i)
                    if i < 2:
                        wait(pe, c["kt"], a, 2 + i)
                    else:
                        wait(pe, c["qtm"], a, i - 1)
                    turn_stack(q_nat[a.parity], ROWS_B, i, "qtm_ps")

                def go(n, a, b, z):
                    if a is not None:
                        turn_q(a, 0)
                        turn_k(a, 0)
                    if z is not None:
                        wait(pe, c["ot"], z, 3)
                        if b is not None and z.offset + 2 < NB:
                            if layer == 0:
                                wait(pe, c["v"], Batch(z.offset + 2, z.turn), 1)
                            elif z.turn is not None or z.offset == 0:
                                wait(pe, c["x2"], Batch(z.offset + 2, z.turn))
                        wait(pe, c["x2T"], z.back(1))
                        if layer == 0:
                            wait(pe, c["lg"], z.back(1))
                        for t in range(TT):
                            for g in range(4):
                                last = pe.transpose(pM[:, t, g * P:(g + 1) * P], o_t[:, g, t * P:(t + 1) * P], ident[:])
                        last.then_inc(c["ott"].sem, 1)
                    for h in range(NH):
                        if b is not None:
                            scores_k(b, h)
                        if a is not None:
                            scores_q(a, h)
                            if h in (1, 5, 9):
                                turn_q(a, (h + 3) // 4)
                            if h in (2, 6, 10):
                                turn_k(a, (h + 2) // 4)
                            if h in (7, 11, 15):
                                turn_qm(a, h // 4 - 1)
                        if h in (5, 9, 13) and b is not None:
                            values(b, h // 4 - 1)
                        if n is not None and layer == 1 and h == 1:
                            if z is not None:
                                wait(pe, c["o"], z)
                            else:
                                wait(pe, c["x2"], n.back(1))
                            pe.wait_ge(ye_in[n.parity], 16 * (n.half + 1))
                            pe.wait_ge(gates_in[n.parity], 16 * (n.half + 1))
                            for t in range(TT):
                                for q in range(NPAIR):
                                    last = pe.matmul(pM[:, 0, t * D:(t + 1) * D], gates_s[n.parity][:, q, t * P:(t + 1) * P],
                                                     ye_s[n.parity][:, q, :], start=(q == 0), stop=(q == NPAIR - 1))
                            last.then_inc(c["sc_ps"].sem, 1)
                        if n is not None and layer == 0:
                            if h == 3:
                                wait(pe, c["xn"], n, 1)
                                if z is not None:
                                    wait(pe, c["o"], z)
                                else:
                                    wait(pe, c["v"], n, -1)
                                turn_in(pM[:, 0, :], xn, "xnT_ps")
                            if h == 5:
                                if n.turn is None and n.offset == 0:
                                    pe.wait_ge(loaded["wqkv"], 32)
                                wait(pe, c["xnT"], n)
                                for t in range(TT):
                                    for d in range(DT):
                                        last = pe.matmul(pM[:, 1, t * D:(t + 1) * D], xnT[:, d, t * P:(t + 1) * P], wq_s[:, d, :],
                                                         start=(d == 0), stop=(d == DT - 1))
                                last.then_inc(c["q_ps"].sem, 1)
                            if h in (6, 8):
                                t = h // 2 - 3
                                if t == 0:
                                    pe.wait_ge(ctx_in[0][n.parity], 16 * (n.half + 1))
                                else:
                                    wait(pe, c["q32"], n)
                                for d in range(DT):
                                    last = pe.matmul(pM[:, t, :], ctx_s[n.parity][:, d, t * P:(t + 1) * P], wkv_s[:, d, :],
                                                     start=(d == 0), stop=(d == DT - 1))
                                last.then_inc(c["kv_ps"].sem, 1)
                        if z is not None and h == 10:
                            wait(pe, c["xn2"], z, 1)
                            if n is not None:
                                wait(pe, c["x2"] if layer else c["v"], n, 0)
                            else:
                                wait(pe, c["o"], z)
                            turn_in(pM[:, 0, :], xn_post, "x2T_ps")
                        if z is not None and layer == 0 and h == 12:
                            wait(pe, c["x2T"], z)
                            if n is not None:
                                wait(pe, c["v"], n, 1)
                            for t in range(TT):
                                for d in range(DT):
                                    last = pe.matmul(pM[:, 1, t * NE:(t + 1) * NE], xnT_post[:, d, t * P:(t + 1) * P],
                                                     gw0[:, d, :], start=(d == 0), stop=(d == DT - 1))
                            last.then_inc(c["lg_ps"].sem, 1)
                    if b is not None:
                        values(b, 3)
                    if a is not None:
                        turn_qm(a, 3)
                return go

            slots(pe, slot_of(0))
            barrier(pe, 1)

            pe.wait_ge(route, 5)
            for t in range(TT):
                last = pe.transpose(pA[0:NB * NE, 0, t * P:(t + 1) * P], lg[:, t, :, :].rearrange("p b e -> p (b e)"), ident[:])
            last.then_inc(route_pe, 1)
            pe.wait_ge(route, 7 + CAP // 4)
            for t in range(TT):
                last = pe.transpose(pA[:, 1, 0:TT * NB * NE // 2].bitcast(BF16)[:, t * NB * NE:(t + 1) * NB * NE],
                                    selT[:, t * P:(t + 1) * P], identb[0:NB * NE, 0:NB * NE])
            last.then_inc(route_pe, 1)
            pe.wait_ge(route, 8 + CAP // 4)
            n = NB * NE
            pe.matmul(pB[:, 0, 0:n], upper[:], sel[:, 0, :], start=True, stop=True)
            pe.matmul(pB[:, 0, n:2 * n], onesb[:], sel[:, 0, :], start=True, stop=False)
            pe.matmul(pB[:, 0, n:2 * n], upper[:], sel[:, 1, :], start=False, stop=True).then_inc(route_pe, 1)

            def gather(b):
                for d, bank, free in ((0, pA, xin_ok), (1, pB, xin_act)):
                    wait(pe, free, b.back(2))
                    if d == 0:
                        wait(pe, onehot_ok, b, 1)
                    for t in range(TT):
                        for i in range(3):
                            last = pe.matmul(bank[:, b.parity, :],
                                             xn2s[:, bass.ds(b.n * TT + t, 1), i, d * P:(d + 1) * P].rearrange("p o d -> p (o d)"),
                                             onehot[:, t, bass.ds(b.n, 1), :].rearrange("p o s -> p (o s)"),
                                             start=(t == 0 and i == 0), stop=(t == TT - 1 and i == 2))
                    last.then_inc(gather_ps.sem, 1)

            pairs(pe, gather, NB)

            def expert(e):
                if e.turn is None and e.offset == 0:
                    pe.wait_ge(xin_ok.sem, NB)
                    pe.wait_ge(xin_act.sem, NB)
                for i in range(2):
                    pe.wait_ge(w_in[e.parity][i], 16 * (e.half + 1))
                for it in range(IT):
                    for w, bank, free, ps in ((wg_s, pA, silu_ok, g_ps), (wu_s, pB, h_ok, u_ps)):
                        wait(pe, free, e, it - 2)
                        for d in range(DT):
                            last = pe.matmul(bank[:, it % 2, :], w[e.parity][:, d, it * P:(it + 1) * P],
                                             xin[:, d, bass.ds(e.n, 1), :].rearrange("p o s -> p (o s)"),
                                             start=(d == 0), stop=(d == DT - 1))
                        last.then_inc(ps.sem, 1)
                for t in range(TT):
                    wait(pe, gated_ok, e, t)
                    wait(pe, gt_ok, e.back(1), t)
                    bank = pM[:, 2, :] if t == 0 else pO[:].rearrange("p a b -> p (a b)")
                    for q in range(NPAIR):
                        last = pe.transpose(bank[:, q * P:(q + 1) * P], gated[:, t, q * P:(q + 1) * P], ident[:])
                    last.then_inc(gt_ps.sem, 1)
                wait(pe, h_ok, e, IT - 1)
                pe.wait_ge(w_in[e.parity][2], 16 * (e.half + 1))
                for h in range(2):
                    wait(pe, y_ready, e.back(1), h)
                    for q in range(2):
                        tt = 2 * h + q
                        for it in range(IT):
                            last = pe.matmul(pM[:, h, q * D:(q + 1) * D], hT[:, it, tt * P:(tt + 1) * P], wd_s[e.parity][:, it, :],
                                             start=(it == 0), stop=(it == IT - 1))
                    last.then_inc(down_ps.sem, 1)

            pairs(pe, expert, NE)
            barrier(pe, 2)
            pe.wait_ge(const_l1, 6)
            pe.wait_ge(const_v1, 4)
            slots(pe, slot_of(1))
            barrier(pe, 3)

            for n in range(NT):
                for d in range(DT):
                    last = pe.matmul(pA[:, 0, n * NE1:(n + 1) * NE1], xnT_all[:, d, n * P:(n + 1) * P], gw1[:, d, :],
                                     start=(d == 0), stop=(d == DT - 1))
            last.then_inc(r1_pe, 1)
            pe.wait_ge(loaded["wl1"], 64)
            pe.wait_ge(r1, 1)

            def chunk(c):
                for i in range(4):
                    w, f = (wsi_s, i) if i < 2 else (w1_s, i - 2)
                    wait(pe, f1_act, c, i - 2)
                    wait(pe, f1_h, c, i - 2)
                    if i < 2:
                        wait(pe, o1_acc, c.back(1), 9 * (2 + i))
                    for k, bank in enumerate((pA, pB)):
                        for d in range(DT):
                            last = pe.matmul(bank[:, i % 2, :], w[:, d, k * H1 + f * P:k * H1 + (f + 1) * P],
                                             xnT_all[:, d, bass.ds(c.n * 512, 512)], start=(d == 0), stop=(d == DT - 1))
                        last.then_inc(f1_ps.sem, 1)
                for t in range(4):
                    wait(pe, f1_h, c, 3)
                    if t >= 2:
                        wait(pe, o1_acc, c, 9 * (t - 2))
                    for k in range(2):
                        last = pe.matmul(pA[:, t % 2, 0:D], hsT[:, k, t * P:(t + 1) * P], wso_s[:, k, :], start=(k == 0), stop=(k == 1))
                    last.then_inc(o1_ps.sem, 1)
                    for q in range(4):
                        wait(pe, o1_acc, c, 9 * (t - 1) + 2 * q + 2)
                        for k in range(2):
                            last = pe.matmul(out_bank(q), hrT[:, k, t * P:(t + 1) * P],
                                             w2_s[:, k, 2 * q:2 * q + 2, :].rearrange("p e d -> p (e d)"), start=(k == 0), stop=(k == 1))
                        last.then_inc(o1_ps.sem, 1)

            chunk(Batch(0))
            with pe.Fori(1, 4) as j:
                chunk(Batch(0, j, 1))


def kernel(x, ctx_1024, mask_BxS2_ik0, g_xattn, g_ffn, L0_xattn_Wq, L0_xattn_bq, L0_xattn_Wk, L0_xattn_bk,
           L0_xattn_Wv, L0_xattn_bv, L0_ffn_gate_w, L0_ffn_w_gate, L0_ffn_w_up, L0_ffn_w_down, L1_ffn_w_shared_in,
           L1_ffn_w_shared_out, L1_ffn_w1_shared, L1_ffn_w2, L1_ffn_w_gate, L1_ffn_gate_bias):
    import numpy as np
    import concourse.bacc as bacc
    from concourse.bass_utils import run_bass_kernel_spmd

    def rows(a):
        return np.ascontiguousarray(a.reshape(-1, P, a.shape[-1]).transpose(1, 0, 2))

    def turned_rows(a):
        return np.ascontiguousarray(a.reshape(a.shape[0], a.shape[1], -1, P).transpose(0, 3, 2, 1))

    a = {k: np.asarray(v) for k, v in locals().items() if k in INPUTS}
    arrays = {
        "x": rows(a["x"].reshape(NB * S, D)),
        "ctx": np.ascontiguousarray(a["ctx_1024"].reshape(NB, TT, P, D).transpose(0, 2, 1, 3)),
        "ctxT": turned_rows(a["ctx_1024"]),
        "mask": np.ascontiguousarray(a["mask_BxS2_ik0"].reshape(NT, P).T),
        "g_xattn": a["g_xattn"], "g_ffn": a["g_ffn"],
        "wq": rows(a["L0_xattn_Wq"].T),
        "wkv": rows(np.concatenate([a["L0_xattn_Wk"].T, a["L0_xattn_Wv"].T], axis=1)),
        "bq": a["L0_xattn_bq"], "bk": a["L0_xattn_bk"], "bv": a["L0_xattn_bv"],
        "gate0": rows(a["L0_ffn_gate_w"].T),
        "w_gate": turned_rows(a["L0_ffn_w_gate"]), "w_up": turned_rows(a["L0_ffn_w_up"]),
        "w_down": turned_rows(a["L0_ffn_w_down"]),
        "ws_in": rows(a["L1_ffn_w_shared_in"]), "ws_out": rows(a["L1_ffn_w_shared_out"]),
        "w1s": rows(a["L1_ffn_w1_shared"]),
        "w2": np.ascontiguousarray(a["L1_ffn_w2"].reshape(NE1, 2, P, D).transpose(2, 1, 0, 3)),
        "wg1": rows(a["L1_ffn_w_gate"]), "gbias": a["L1_ffn_gate_bias"],
    }
    nc = bacc.Bacc("TRN2", target_bir_lowering=False, num_devices=1)
    ins = {n: nc.dram_tensor(f"in_{n}", v.shape, mybir.dt.from_np(v.dtype), kind="ExternalInput").ap()
           for n, v in arrays.items()}
    out = nc.dram_tensor("out", (P, NT, D), F32, kind="ExternalOutput").ap()
    build_program(nc, out=out, **ins)
    r = run_bass_kernel_spmd(nc, [{f"in_{n}": v for n, v in arrays.items()}], core_ids=[0])
    got = np.asarray(r.results[0]["out"])
    return np.ascontiguousarray(got.transpose(1, 0, 2)).reshape(NB, S, D)


INPUTS = ("x", "ctx_1024", "mask_BxS2_ik0", "g_xattn", "g_ffn", "L0_xattn_Wq", "L0_xattn_bq", "L0_xattn_Wk",
          "L0_xattn_bk", "L0_xattn_Wv", "L0_xattn_bv", "L0_ffn_gate_w", "L0_ffn_w_gate", "L0_ffn_w_up",
          "L0_ffn_w_down", "L1_ffn_w_shared_in", "L1_ffn_w_shared_out", "L1_ffn_w1_shared", "L1_ffn_w2",
          "L1_ffn_w_gate", "L1_ffn_gate_bias")
```

```python
from contextlib import ExitStack

import concourse.bass as bass
from concourse import mybir

ALU = mybir.AluOpType
ACT = mybir.ActivationFunctionType
F32 = mybir.dt.float32
F32R = mybir.dt.float32r
BF16 = mybir.dt.bfloat16
I32 = mybir.dt.int32
AX = mybir.AxisListType.X

P = 128
NB, S, D = 8, 256, 256
NH, W = 16, 16
TT = S // P
DT = D // P
NT = NB * TT
NE, I = 8, 1024
IT = I // P
CAP = S // NE * 2
SLOTS = NB * CAP
NPAIR = NE // 2
H1 = 256
NE1 = 8
EPS = 1e-5
SCALE = 0.25
NEG = -1.0e30

MASK0 = 6 * W
NMAX0 = MASK0 + 3
ROWS_A = NMAX0
ROWS_B = NMAX0 + 3
STACK = ROWS_B + 2


HI, LO = 0, 1
PRODUCTS = ((HI, HI), (HI, LO), (LO, HI))


class Count:

    def __init__(self, sem, per, base=0):
        self.sem, self.per, self.base = sem, per, base

    def at(self, b, j=0):
        return b * self.per + (self.base + j + 1)


class Batch:

    def __init__(self, offset, turn=None, stride=2):
        self.offset, self.turn, self.stride = offset, turn, stride
        self.parity = offset % 2
        self.half = offset // 2 if turn is None else turn + offset // 2
        self.n = offset if turn is None else turn * stride + offset

    def back(self, n):
        return Batch(self.offset - n, self.turn, self.stride)


def wait(eng, count, b, j=0):
    if b.turn is not None or count.at(b.n, j) > 0:
        eng.wait_ge(count.sem, count.at(b.n, j))


def bcast(ap, dim, n):
    ap = ap.unsqueeze(dim)
    shape = list(ap.shape)
    shape[dim] = n
    return ap.broadcast_to(shape)


def build_program(nc, x, ctx, ctxT, mask, g_xattn, g_ffn, wq, wkv, bq, bk, bv, gate0, w_gate, w_up, w_down,
                  ws_in, ws_out, w1s, w2, wg1, gbias, out):
    with ExitStack() as keep:
        def sem(name):
            return keep.enter_context(nc.semaphore(name))

        def sb(name, shape, dt=F32, where=keep):
            return where.enter_context(nc.sbuf_tensor(name, shape, dt))

        xs = sb("xs", [P, NT, D])
        ident = sb("ident", [P, P])
        identb = sb("identb", [P, P], BF16)
        upper = sb("upper", [P, P], BF16)
        onesb = sb("onesb", [P, P], BF16)
        causal_q = sb("causal_q", [P, P], BF16)
        causal_k = sb("causal_k", [P, P], BF16)
        half = sb("half", [P, TT])
        zeros = sb("zeros", [P, TT, D])
        iota64 = sb("iota64", [P, CAP])
        tg = sb("tg", [P, 4])
        graw = sb("graw", [P, 4])
        gw0 = sb("gw0", [P, DT, NE])
        gw1 = sb("gw1", [P, DT, NE1])
        gb1 = sb("gb1", [P, NE1])
        maski = sb("maski", [P, NT], I32)
        maskr = sb("maskr", [P, 3, NT])
        maskp = sb("maskp", [P, NT, 3], BF16)
        lg = sb("lg", [P, TT, NB, NE])
        lgt = sb("lgt", [P, TT, NB, NE])
        lgs = sb("lgs", [P, TT * NB])
        sel = sb("sel", [P, TT, NB * NE], BF16)
        slot = sb("slot", [P, TT, NB * NE])

        ye = nc.dram_tensor("ye", [NB // 2, P, NE, D], F32, kind="Internal").ap()
        gates = nc.dram_tensor("gates", [NB, P, NPAIR, S], F32, kind="Internal").ap()

        with ExitStack() as att:
            def ab(name, shape, dt=F32):
                return sb(name, shape, dt, att)

            xn2s = ab("xn2s", [P, NT, 3, D], BF16)
            xnT_all = xn2s[:, :, :, :].rearrange("p a b c -> p (a b c)")[:, 0:2 * DT * NB * S].bitcast(F32)\
                .rearrange("p (a b) -> p a b", a=DT)
            with ExitStack() as first:
                def zb(name, shape):
                    return sb(name, shape, F32, first)

                xn = zb("xn", [P, TT, D])
                xnT = zb("xnT", [P, DT, S])
                xnT_post = zb("xnT_post", [P, DT, S])
                k32 = zb("k32", [P, TT, D])
                v32 = zb("v32", [P, TT, D])
                rx = zb("rx", [P, TT, D])
                wq_s = zb("wq_s", [P, DT, D])
                wkv_s = zb("wkv_s", [P, DT, 2 * D])
                bq_s, bk_s, bv_s = (zb(n, [P, D]) for n in ("bq_s", "bk_s", "bv_s"))
            wsi_s = ab("wsi_s", [P, DT, 2 * H1])
            w1_s = ab("w1_s", [P, DT, 2 * H1])
            wso_s = ab("wso_s", [P, DT, D])
            w2_s = ab("w2_s", [P, DT, NE1, D])
            lgT = ab("lgT", [NE1, NB * S])
            ctx_s = [ab(f"ctx_s{i}", [P, 2, 256]) for i in range(2)]
            ye_s = [ab(f"ye_s{i}", [P, NPAIR, D]) for i in range(2)]
            gates_s = [ab(f"gates_s{i}", [P, NPAIR, S]) for i in range(2)]
            q_nat = [ab(f"q_nat{i}", [P, TT, NH, STACK], BF16) for i in range(2)]
            k_nat = [ab(f"k_nat{i}", [P, TT, NH, STACK], BF16) for i in range(2)]
            q_t = ab("q_t", [P, NH, S], BF16)
            q_tm = ab("q_tm", [P, NH, S], BF16)
            k_t = [ab(f"k_t{i}", [P, NH, S], BF16) for i in range(2)]
            v_aug = [ab(f"v_aug{i}", [P, TT, NH, 2 * W]) for i in range(2)]
            probs = [ab(f"probs{i}", [P, 4, TT * S]) for i in range(2)]
            o_t = ab("o_t", [P, 4, S])
            xn_post = ab("xn_post", [P, TT, D])
            q32 = ab("q32", [P, TT, D])
            rq = ab("rq", [P, TT, D])
            rk = ab("rk", [P, TT, D])
            o_nat = ab("o_nat", [P, TT, D])
            st, st2 = ab("st", [P, TT, 6]), ab("st2", [P, TT, 6])
            mv, mv2 = ab("mv", [P, TT, 2]), ab("mv2", [P, TT, 2])
            rs, rs2 = ab("rs", [P, 2, TT]), ab("rs2", [P, 2, TT])
            mx = ab("mx", [P, TT, NH])
            mr = ab("mr", [P, TT, NH])
            rden = ab("rden", [P, 2, TT, NH])

        with ExitStack() as ffn:
            def fb(name, shape, dt=F32):
                return sb(name, shape, dt, ffn)

            hT = [fb("hT_hi", [P, IT, SLOTS], F32R)]
            gated = fb("gated", [P, TT, NE * CAP])
            gt_s = fb("gt_s", [P, TT, NPAIR, P])
            assert IT * SLOTS + 2 * TT * NE * CAP >= NT * 3 * D // 2
            xin = [fb(f"xin_{part}", [P, DT, NE, SLOTS], F32R) for part in ("hi", "lo")]
            wg_s = fb("wg_s", [P, DT, I])
            wu_s = fb("wu_s", [P, DT, I])
            wd_s = fb("wd_s", [P, IT // 2, D])
            wg_p = [fb(f"wg_{part}", [P, DT, I], F32R) for part in ("hi", "lo")]
            wu_p = [fb(f"wu_{part}", [P, DT, I], F32R) for part in ("hi", "lo")]
            wd_p = [fb(f"wd_{part}", [P, IT, D], F32R) for part in ("hi", "lo")]
            pieces = [(w[:, :, k * 512:(k + 1) * 512], [q[:, :, k * 512:(k + 1) * 512] for q in parts])
                      for k in range(2) for w, parts in ((wg_s, wg_p), (wu_s, wu_p))]
            pieces += [(wd_s[:], [q[:, 4 * k:4 * k + 4, :] for q in wd_p]) for k in range(2)]
            onehot = fb("onehot", [P, 2, TT, NE * CAP], BF16)
            silu = fb("silu", [P, 2, SLOTS])
            hT.append(fb("hT_lo", [P, IT, SLOTS], F32R))
            y_s = fb("y_s", [P, 2, 2, D])
            work = silu[0:NB * NE, :, :].rearrange("p a b -> p (a b)")
            top = [work[:, i * S:(i + 1) * S] for i in range(2)]
            top8 = work[:, 2 * S:2 * S + 8]
            selT = work[:, 3 * S:4 * S].bitcast(BF16)[:, 0:S]
        with ExitStack() as last:
            def lb(name, shape, dt=F32):
                return sb(name, shape, dt, last)

            lb("xnT_all_place", [P, NT, 3, D], BF16)
            lb("weights_place", [P, DT * (4 * H1 + D + NE1 * D)])
            lb("lgT_place", [NE1, NB * S])
            wsi_p = [lb(f"wsi_{part}", [P, DT, 2 * H1], F32R) for part in ("hi", "lo")]
            w1_p = [lb(f"w1_{part}", [P, DT, 2 * H1], F32R) for part in ("hi", "lo")]
            wso_p = [lb(f"wso_{part}", [P, DT, D], F32R) for part in ("hi", "lo")]
            w2_p = [lb(f"w2_{part}", [P, DT, NE1, D], F32R) for part in ("hi", "lo")]
            pieces1 = [(w[:], [q[:] for q in parts]) for w, parts in ((wsi_s, wsi_p), (w1_s, w1_p), (wso_s, wso_p))]
            pieces1 += [(w2_s[:, :, 2 * k:2 * k + 2, :], [q[:, :, 2 * k:2 * k + 2, :] for q in w2_p]) for k in range(NE1 // 2)]
            xc = [lb(f"xc_{part}", [P, DT, 512], F32R) for part in ("hi", "lo")]
            sact = lb("sact", [P, 2, 512])
            hsT = [lb(f"hsT_{part}", [P, 2, 512], F32R) for part in ("hi", "lo")]
            hrT = [lb(f"hrT_{part}", [P, 2, 512], F32R) for part in ("hi", "lo")]
            lg1 = lb("lg1", [P, NT, NE1])
            e1 = lb("e1", [P, NT, NE1])
            sm1 = lb("sm1", [P, NT])
            top1 = lb("tops_1", [P, NT, 2 * NE1])
            top1r = lb("tops_1r", [P, NT, 2 * NE1])
            best = lb("best", [P, NT, 8])
            find = lb("find", [P, NT, 8])
            wd1 = lb("wd1", [P, NT, NE1])
            wdc = lb("wdc", [P, 4, NE1])
            acc = [lb(f"acc{i}", [P, D]) for i in range(2)]

        pA, pB, pM = [keep.enter_context(nc.psum_tensor(n, [P, k, 512], F32)) for n, k in (("pA", 2), ("pB", 2), ("pM", 3))]
        pO = keep.enter_context(nc.psum_tensor("pO", [P, 2, S], F32))
        pMb = pM[:, :, :].bitcast(BF16)

        loaded = {n: sem(f"loaded_{n}") for n in ("x0", "x", "gains", "small", "wqkv", "wl1")}
        const_pool, const_dve, const_act = sem("const_pool"), sem("const_dve"), sem("const_act")
        const_l1 = sem("const_l1")
        settled = sem("settled")
        phase_end = sem("phase_end")
        ctx_in = [[sem(f"ctx_in{l}{i}") for i in range(2)] for l in range(2)]
        gates_in = [sem(f"gates_in{i}") for i in range(2)]
        ye_in = [sem(f"ye_in{i}") for i in range(2)]
        N_SMALL = 7
        N_CONST_POOL, N_CONST_DVE, N_CONST_ACT = 18, 11, 1

        both = dict(stat=2, mv=2, rs=2, xn=2, vc=1, q1=1, qr=1, q2=1, q3=1, k1=1, kr=1, k2=1, k3=1, qt_ps=4, qt=4,
                    kt_ps=4, kt=4, a_ps=NH, mx=NH, m1=4, mr=4, m2=4, m3=4, qtm_ps=4, qtm=4, b_ps=NH, p=NH,
                    pv=4, ot=4, ott=1, rden=2, o=1, xres=1, stat2=2, mv2=2, rs2=2, xn2=2, x2T_ps=1, x2T=1, lg_ps=1, lg=1)
        only0 = dict(xnT_ps=1, xnT=1, q_ps=1, kv_ps=2, q32=1, k32=2, v=2, kmask=1, s1=1, sr=1, s2=1, s3=1)
        only1 = dict(sc_ps=1, x2=1)
        C = [{n: Count(sem(n), per) for n, per in (both | only0).items()}, {}]
        C[1] = {n: Count(C[0][n].sem, per, NB * per) for n, per in both.items()}
        C[1] |= {n: Count(sem(n), per) for n, per in only1.items()}

        def arrive(eng):
            eng.drain().then_inc(phase_end, 1)

        def barrier(eng, n):
            arrive(eng)
            eng.wait_ge(phase_end, 5 * n)

        def settle(eng):
            eng.sem_inc(settled, 1)

        def tile_of(n):
            return xs[:, bass.ds(n, 1), :].rearrange("p o d -> p (o d)")

        def stack(nat):
            return nat[:, :, :, 0:MASK0].rearrange("p t h (n w) -> p (t h) n w", w=W)

        def rep(nat, first, n):
            return stack(nat)[:, :, first:first + n, :]

        def rep_of(src, n):
            return bcast(src[:].rearrange("p t (h w) -> p (t h) w", w=W), 2, n)

        def part_of(nat, n):
            return nat[:, :, :, n * W:(n + 1) * W]

        def by_head(src):
            return src[:].rearrange("p t (h w) -> p t h w", w=W)

        def turned(bank, rows):
            return pMb[0:rows, bank, :].rearrange("p (h s) -> p h s", h=4)

        def out_bank(q):
            return pM[:, q, :] if q < 3 else pO[:].rearrange("p a b -> p (a b)")

        w_in = [sem(f"w_in{i}") for i in range(3)]
        w_hi, w_lo = Count(sem("w_hi"), 6), Count(sem("w_lo"), 6)
        y_ready = Count(sem("y_ready"), 2)
        gates_out = [sem("gates_out0"), sem("gates_out1")]
        y_out = [sem("y_out0"), sem("y_out1")]
        stored, out_ready = sem("stored"), sem("out_ready")
        g_ps, u_ps = Count(sem("g_ps"), IT), Count(sem("u_ps"), IT)
        silu_ok, h_ok = Count(sem("silu_ok"), IT), Count(sem("h_ok"), IT)
        h_hi, h_lo = Count(sem("h_hi"), IT), Count(sem("h_lo"), IT)
        down_ps = Count(sem("down_ps"), 2)
        gated_ok, gt_ps, gt_ok = Count(sem("gated_ok"), 4), Count(sem("gt_ps"), 2), Count(sem("gt_ok"), 2)
        onehot_ok, gather_ps = Count(sem("onehot_ok"), 2), Count(sem("gather_ps"), 2)
        route, route_act, route_pe = sem("route"), sem("route_act"), sem("route_pe")
        xin_hi, xin_lo = Count(sem("xin_hi"), 2), Count(sem("xin_lo"), 2)
        const_v1 = sem("const_v1")
        f1_ps, f1_act, f1_h = Count(sem("f1_ps"), 8), Count(sem("f1_act"), 4), Count(sem("f1_h"), 4)
        f1_hi, f1_lo = Count(sem("f1_hi"), 4), Count(sem("f1_lo"), 4)
        xc_hi, xc_lo = Count(sem("xc_hi"), 1), Count(sem("xc_lo"), 1)
        wdc_ok = Count(sem("wdc_ok"), 1)
        w1_hi, w1_lo = sem("w1_hi"), sem("w1_lo")
        r1, r1_act, r1_pe = sem("r1"), sem("r1_act"), sem("r1_pe")
        o1_ps, o1_acc = Count(sem("o1_ps"), 20), Count(sem("o1_acc"), 36)

        block = keep.enter_context(nc.Block())

        def pairs(eng, body, n):
            body(Batch(0))
            body(Batch(1))
            with eng.Fori(1, n // 2) as j:
                body(Batch(0, j))
                body(Batch(1, j))

        def quartet(eng, body):
            body(Batch(0), Batch(1))
            with eng.Fori(1, 3) as j:
                body(Batch(0, j, 1), Batch(1, j, 1))
            body(Batch(3), None)

        def octet(eng, body):
            for i in range(2):
                body(Batch(i), Batch(i + 1))
            with eng.Fori(1, 3) as j:
                for i in range(2):
                    body(Batch(i, j), Batch(i + 1, j))
            body(Batch(6), Batch(7))
            body(Batch(7), None)

        def slots(eng, slot_of):
            slot_of(Batch(0), None, None, None)
            slot_of(Batch(1), Batch(0), None, None)
            slot_of(Batch(2), Batch(1), Batch(0), None)
            slot_of(Batch(3), Batch(2), Batch(1), Batch(0))
            with eng.Fori(0, 2) as j:
                slot_of(Batch(4, j), Batch(3, j), Batch(2, j), Batch(1, j))
                slot_of(Batch(5, j), Batch(4, j), Batch(3, j), Batch(2, j))
            slot_of(None, Batch(7), Batch(6), Batch(5))
            slot_of(None, None, Batch(7), Batch(6))
            slot_of(None, None, None, Batch(7))

        TURN_ORDER = (("q", 1), ("k", 1), ("q", 2), ("k", 2), ("m", 0), ("q", 3), ("k", 3), ("m", 1), ("m", 2))
        TURN_AFTER = ((0, 2, 3, 5, 7, 8, 10, 11, 13), (1, 2, 4, 5, 7, 8, 10, 11, 13))
        TURNS = [dict(zip(after, TURN_ORDER)) for after in TURN_AFTER]
        NEXT = (15, 15)
        COPIED = {"q": "qt", "k": "kt", "m": "qtm"}
        FIRST, SECOND = ("q", "k"), ("k", "q")
        TURN_BANK = [{item: 2 - n % 2 * i for n, item in enumerate(((SECOND[i], 0), *TURN_ORDER, (FIRST[i], 0), ("m", 3)))}
                     for i in range(2)]

        WHEN = {
            "pe": {"values": ((5, 10, 14), (6, 9, 13)), "xnT": (1,), "q": ((2, 4),), "kv": ((4, 6, 7, 8),),
                   "scatter": ((), (1, 1, 2, 2)), "x2T": (12, 11), "lg": (15, 15), "output": (-1, -1)},
            "act": {"xnT": (1,), "q1": (5, 9), "q2": (7, 15),
                    "k1": (9, 0), "k2": (12, 4), "x2T": (13, 12)},
            "dve": {"o": ((5, 10, 14), (6, 11, 13)), "stat2": (2, 2), "xn2": (6, 9),
                    "lg": (15, 15), "output": (-1, -1), "x2": (None, 2), "stat": (None, 5), "xn": (None, 8),
                    "q32": (4,), "kv": ((7, 8),), "kmask": (13,)},
        }
        POOL_STEPS = (("rstd", "vc", "xres", "rstd2", "qr", "q3", "kr", "parts", "k3"),
                      ("xres", "vc", "rstd2", "kr", "rstd", "k3", "qr", "q3"))

        @block.sync
        def _(sp):
            sp.dma_start(xs[:, 0:TT, :], x[:, 0:TT, :]).then_inc(loaded["x0"], 16)
            sp.dma_start(wq_s[:], wq).then_inc(loaded["wqkv"], 16)
            sp.dma_start(ctx_s[0][:], ctxT[0]).then_inc(ctx_in[0][0], 16)
            for dst, src in ((graw[:, 0:2], g_xattn.partition_broadcast(P)), (graw[:, 2:4], g_ffn.partition_broadcast(P))):
                sp.dma_start(dst, src).then_inc(loaded["gains"], 16)
            sp.dma_start(wkv_s[:], wkv).then_inc(loaded["wqkv"], 16)
            for dst, src in ((bq_s[:], bq.partition_broadcast(P)), (bk_s[:], bk.partition_broadcast(P)),
                             (bv_s[:], bv.partition_broadcast(P)), (maski[:], mask),
                             (gw0[:], gate0), (gw1[:], wg1), (gb1[:], gbias.partition_broadcast(P))):
                sp.dma_start(dst, src).then_inc(loaded["small"], 16)
            sp.dma_start(ctx_s[1][:], ctxT[1]).then_inc(ctx_in[0][1], 16)
            sp.dma_start(xs[:, TT:NT, :], x[:, TT:NT, :]).then_inc(loaded["x"], 16)

            def load_ye(b):
                for i in range(2):
                    src = ye[bass.ds(b.half, 1), b.parity * CAP:(b.parity + 1) * CAP, i:NE:2, :]
                    sp.dma_start(ye_s[b.parity][i * CAP:(i + 1) * CAP, :, :], src.rearrange("o p q d -> (o p) q d"))\
                      .then_inc(ye_in[b.parity], 16)

            def ctx_loads(layer):
                src = (ctxT, ctx)[layer]
                c = C[layer]
                with sp.Fori(0, 3) as j:
                    for b in (Batch(2, j), Batch(3, j)):
                        if layer == 0:
                            wait(sp, c["kv_ps"], b.back(2), 1)
                        else:
                            wait(sp, c["vc"], b.back(2))
                            settle(sp)
                            wait(sp, c["sc_ps"], b.back(2))
                        settle(sp)
                        sp.dma_start(ctx_s[b.parity][:], src[bass.ds(b.n, 1)].rearrange("o p t d -> (o p) t d"))\
                          .then_inc(ctx_in[layer][b.parity], 16)
                        if layer == 1:
                            load_ye(b)
                            sp.dma_start(gates_s[b.parity][:], gates[bass.ds(b.n, 1)].rearrange("o p q s -> (o p) q s"))\
                              .then_inc(gates_in[b.parity], 16)

            ctx_loads(0)
            barrier(sp, 1)

            def load_gate_up(e):
                for i, (dst, src) in enumerate(((wg_s, w_gate), (wu_s, w_up))):
                    sp.dma_start(dst[:], src[bass.ds(e, 1)].rearrange("o p a b -> (o p) a b")).then_inc(w_in[i], 16)

            def load_down(e, k):
                src = w_down[bass.ds(e, 1), :, k * IT // 2:(k + 1) * IT // 2, :]
                sp.dma_start(wd_s[:], src.rearrange("o p a b -> (o p) a b")).then_inc(w_in[2], 16)

            load_gate_up(0)
            load_down(0, 0)

            def store_y(e, h):
                wait(sp, y_ready, e, h)
                settle(sp)
                sp.dma_start(ye[2 * h:2 * h + 2, :, bass.ds(e.n, 1), :].rearrange("t p o d -> (o p) t d"), y_s[:, h, :, :])\
                  .then_inc(y_out[h], 16)

            def traffic(e, e_next):
                if e_next is not None:
                    wait(sp, w_lo, e, 3)
                    settle(sp)
                    load_gate_up(e_next.n)
                wait(sp, w_lo, e, 4)
                settle(sp)
                load_down(e.n, 1)
                if e_next is not None:
                    wait(sp, w_lo, e, 5)
                    settle(sp)
                    load_down(e_next.n, 0)
                for t in range(TT):
                    wait(sp, gt_ok, e, t)
                    settle(sp)
                    sp.dma_start(gates[bass.ds(e.n, 1), :, :, t * P:(t + 1) * P].rearrange("o p q s -> (o p) q s"),
                                 gt_s[:, t, :, :]).then_inc(gates_out[t], 16)
                if e_next is not None:
                    for h in range(2):
                        store_y(e, h)

            octet(sp, traffic)
            wait(sp, u_ps, Batch(NE - 1), IT - 1)
            for b in range(2):
                sp.dma_start(ctx_s[b][:], ctx[b]).then_inc(ctx_in[1][b], 16)
            store_y(Batch(NE - 1), 0)
            for h in range(2):
                sp.wait_ge(gates_out[h], 16 * NB)
            for b in range(2):
                sp.dma_start(gates_s[b][:], gates[b]).then_inc(gates_in[b], 16)
            sp.wait_ge(y_out[0], 16 * NE)
            load_ye(Batch(0))
            store_y(Batch(NE - 1), 1)
            arrive(sp)
            load_ye(Batch(1))
            sp.wait_ge(phase_end, 10)
            sp.wait_ge(y_out[1], 16 * NE)
            for dst, src in ((wsi_s, ws_in), (w1_s, w1s), (wso_s, ws_out), (w2_s, w2)):
                sp.dma_start(dst[:], src).then_inc(loaded["wl1"], 16)
            ctx_loads(1)
            barrier(sp, 3)
            with sp.Fori(0, NT) as n:
                sp.wait_ge(out_ready, n + 1)
                settle(sp)
                sp.dma_start(out[:, bass.ds(n, 1), :], xs[:, bass.ds(n, 1), :]).then_inc(stored, 16)
            sp.wait_ge(stored, 16 * NT)

        @block.gpsimd
        def _(pool):
            done = [0]

            def const(ins):
                done[0] += 1
                ins.then_inc(const_pool, 1)

            const(pool.memset(ident[:], 0.0))
            const(pool.memset(identb[:], 0.0))
            const(pool.memset(upper[:], 1.0))
            const(pool.memset(onesb[:], 1.0))
            const(pool.memset(causal_q[:], 0.0))
            const(pool.memset(causal_k[:], 0.0))
            const(pool.memset(half[:], -0.5))
            const(pool.memset(zeros[:], 0.0))
            const(pool.iota(iota64[:], pattern=[[1, CAP]], base=1, channel_multiplier=0,
                            allow_small_or_imprecise_dtypes=True))
            pool.wait_ge(const_pool, done[0])
            for m in (ident, identb):
                const(pool.affine_select(out=m[:], in_=m[:], compare_op=ALU.not_equal, fill=1.0, base=0,
                                         pattern=[[-1, P]], channel_multiplier=1))
            const(pool.affine_select(out=upper[:], in_=upper[:], compare_op=ALU.is_ge, fill=0.0, base=0,
                                     pattern=[[1, P]], channel_multiplier=-1))
            const(pool.affine_select(out=causal_q[:], in_=causal_q[:], compare_op=ALU.is_ge, fill=NEG, base=0,
                                     pattern=[[-1, P]], channel_multiplier=1))
            const(pool.affine_select(out=causal_k[:], in_=causal_k[:], compare_op=ALU.is_ge, fill=NEG, base=0,
                                     pattern=[[1, P]], channel_multiplier=-1))
            for i in range(2):
                const(pool.memset(q_nat[i][:, :, :, MASK0:NMAX0], 1.0))
                const(pool.memset(k_nat[i][:, :, :, NMAX0:ROWS_B], 1.0))
            assert done[0] == N_CONST_POOL

            def rstd(c, b, mvs, rss, mv_name, rs_name, used_name, factor=1.0):
                wait(pool, c[mv_name], b, 1)
                wait(pool, c[used_name], b.back(1), 1)
                settle(pool)
                pool.tensor_scalar(rss[:, 0, :], mvs[:, :, 1], EPS, factor, ALU.add, ALU.mult).then_inc(c[rs_name].sem, 1)
                wait(pool, c[rs_name], b, 0)
                pool.tensor_tensor(rss[:, 1, :], rss[:, 0, :], half[:], ALU.pow).then_inc(c[rs_name].sem, 1)

            def slot_of(layer):
                c = C[layer]

                def minus(out, in0, in1, name):
                    pool.tensor_tensor(out, in0, in1, ALU.subtract).then_inc(c[name].sem, 1)

                def go(n, a, b, z):
                    steps = {}
                    if a is not None:
                        def vc():
                            if layer == 0:
                                wait(pool, c["v"], a, 1)
                            else:
                                pool.wait_ge(ctx_in[1][a.parity], 16 * (a.half + 1))
                            wait(pool, c["pv"], a.back(2), 3)
                            v = v32 if layer == 0 else ctx_s[a.parity]
                            pool.tensor_tensor(v_aug[a.parity][:, :, :, 0:W], by_head(v), by_head(zeros), ALU.add)\
                                .then_inc(c["vc"].sem, 1)

                        steps |= {"vc": vc}
                    if z is not None:
                        def xres():
                            x_z = xs[:, bass.ds(z.n * TT, TT), :]
                            wait(pool, c["o"], z)
                            settle(pool)
                            pool.tensor_tensor(x_z, x_z, o_nat[:], ALU.add).then_inc(c["xres"].sem, 1)

                        def rstd2():
                            rstd(c, z, mv2, rs2, "mv2", "rs2", "xn2")

                        def parts():
                            part = [xn2s[:, bass.ds(z.n * TT, TT), i, :] for i in range(3)]
                            wait(pool, c["xn2"], z, 1)
                            settle(pool)
                            pool.tensor_tensor(part[0], xn_post[:], zeros[:], ALU.add).then_inc(c["s1"].sem, 1)
                            wait(pool, c["s1"], z)
                            settle(pool)
                            minus(rx[:], xn_post[:], part[0], "sr")
                            wait(pool, c["sr"], z)
                            settle(pool)
                            pool.tensor_tensor(part[1], rx[:], zeros[:], ALU.add).then_inc(c["s2"].sem, 1)
                            wait(pool, c["s2"], z)
                            settle(pool)
                            minus(part[2], rx[:], part[1], "s3")

                        steps |= {"xres": xres, "rstd2": rstd2, "parts": parts}
                    if n is not None:
                        qn, kn = q_nat[n.parity], k_nat[n.parity]

                        def rstd_n():
                            rstd(c, n, mv, rs, "mv", "rs", "xn", (1.0, SCALE ** -2)[layer])

                        def qr():
                            wait(pool, c["q1"], n)
                            minus(by_head(rq), by_head(q32), part_of(qn, 0), "qr")

                        def q3():
                            wait(pool, c["q2"], n)
                            minus(part_of(qn, 3), by_head(rq), part_of(qn, 4), "q3")

                        def kr():
                            wait(pool, c["k1"], n)
                            minus(by_head(rk), by_head(k32 if layer == 0 else ctx_s[n.parity]), part_of(kn, 2), "kr")

                        def k3():
                            wait(pool, c["k2"], n)
                            minus(part_of(kn, 1), by_head(rk), part_of(kn, 0), "k3")

                        steps |= {"rstd": rstd_n, "qr": qr, "q3": q3, "kr": kr, "k3": k3}
                    for name in POOL_STEPS[layer]:
                        if name in steps:
                            steps[name]()
                return go

            slots(pool, slot_of(0))
            barrier(pool, 1)

            def weight_lo(e, k):
                raw, parts = pieces[k]
                wait(pool, w_hi, e, k)
                pool.tensor_tensor(parts[LO], raw, parts[HI], ALU.subtract).then_inc(w_lo.sem, 1)

            def expert(e, e_next):
                for k in (4, 5):
                    weight_lo(e, k)
                if e_next is not None:
                    for k in range(4):
                        weight_lo(e_next, k)

            for k in range(4):
                weight_lo(Batch(0), k)
            octet(pool, expert)
            barrier(pool, 2)
            for i in range(2):
                pool.memset(q_nat[i][:, :, :, MASK0:NMAX0], 1.0).then_inc(const_l1, 1)
                pool.memset(k_nat[i][:, :, :, NMAX0:ROWS_B], 1.0).then_inc(const_l1, 1)
                pool.memset(k_nat[i][:, :, :, MASK0:NMAX0], 0.0).then_inc(const_l1, 1)
            slots(pool, slot_of(1))
            barrier(pool, 3)
            for k, (raw, parts) in enumerate(pieces1):
                pool.wait_ge(w1_hi, k + 1)
                pool.tensor_tensor(parts[LO], raw, parts[HI], ALU.subtract).then_inc(w1_lo, 1)

        @block.scalar
        def _(act):
            act.wait_ge(loaded["gains"], 32)
            act.activation(tg[:], graw[:], ACT.Tanh).then_inc(const_act, 1)

            def slot_of(layer):
                c = C[layer]
                when = WHEN["act"]
                width = 2 * S if layer == 0 else S + P

                def take_q(a, i):
                    wait(act, c["qt_ps"], a, i)
                    wait(act, c["a_ps"], a.back(1), 4 * i + 3)
                    act.activation(q_t[0:ROWS_A, 4 * i:4 * i + 4, :], turned(TURN_BANK[layer]["q", i], ROWS_A), ACT.Copy).then_inc(c["qt"].sem, 1)

                def take_qm(a, i):
                    wait(act, c["qtm_ps"], a, i)
                    wait(act, c["b_ps"], a.back(1), 4 * i + 3)
                    act.activation(q_tm[0:ROWS_B, 4 * i:4 * i + 4, :], turned(TURN_BANK[layer]["m", i], ROWS_B), ACT.Copy).then_inc(c["qtm"].sem, 1)

                def go(n, a, b, z):
                    if a is not None and SECOND[layer] == "q":
                        take_q(a, 0)
                    for h in range(NH):
                        if b is not None:
                            wait(act, c["b_ps"], b, h)
                            wait(act, c["pv"], b, h // 4 - 2)
                            act.activation(probs[h // 4 % 2][:, h % 4, 0:width], pB[:, h % 2, 0:width], ACT.Exp)\
                               .then_inc(c["p"].sem, 1)
                        if a is not None and h in TURNS[layer]:
                            kind, i = TURNS[layer][h]
                            if kind == "q":
                                take_q(a, i)
                            elif kind == "m":
                                take_qm(a, i)
                        if h == when["x2T"][layer] and z is not None:
                            wait(act, c["x2T_ps"], z)
                            src = pM[:, 0, :].rearrange("p (a b) -> p a b", a=DT)
                            wait(act, c["lg_ps"], z, -1)
                            if layer == 0:
                                act.activation(xnT_post[:], src, ACT.Copy).then_inc(c["x2T"].sem, 1)
                            else:
                                settle(act)
                                act.activation(xnT_all[:, :, bass.ds(z.n * S, S)], src, ACT.Copy).then_inc(c["x2T"].sem, 1)
                        if n is None:
                            continue
                        qn, kn = q_nat[n.parity], k_nat[n.parity]
                        if layer == 0 and h == when["xnT"][0]:
                            wait(act, c["xnT_ps"], n)
                            wait(act, c["q_ps"], n.back(1))
                            act.activation(xnT[:], pM[:, 0, :].rearrange("p (a b) -> p a b", a=DT), ACT.Copy)\
                               .then_inc(c["xnT"].sem, 1)
                        if h == when["q1"][layer]:
                            wait(act, c["xn" if layer else "q32"], n, layer)
                            wait(act, c["qtm_ps"], n.back(2), 3)
                            act.activation(rep(qn, 0, 3), rep_of(q32, 3), ACT.Copy).then_inc(c["q1"].sem, 1)
                        if h == when["q2"][layer]:
                            wait(act, c["qr"], n)
                            act.activation(rep(qn, 4, 2), rep_of(rq, 2), ACT.Copy).then_inc(c["q2"].sem, 1)
                        if h == when["k1"][layer]:
                            if layer == 0:
                                wait(act, c["k32"], n, 1)
                                src = k32
                            else:
                                act.wait_ge(ctx_in[1][n.parity], 16 * (n.half + 1))
                                src = ctx_s[n.parity]
                            wait(act, c["kt_ps"], n.back(2), 3)
                            act.activation(rep(kn, 2, 3), rep_of(src, 3), ACT.Copy).then_inc(c["k1"].sem, 1)
                        if h == when["k2"][layer]:
                            wait(act, c["kr"], n)
                            act.activation(stack(kn)[:, :, 0:6:5, :], rep_of(rk, 2), ACT.Copy).then_inc(c["k2"].sem, 1)
                        if h == NEXT[layer] and FIRST[layer] == "q":
                            take_q(n, 0)
                    if a is not None:
                        take_qm(a, 3)
                return go

            slots(act, slot_of(0))
            arrive(act)
            act.wait_ge(route, 2)
            act.activation(lg[:], lgt[:], ACT.Exp).then_inc(route_act, 1)
            act.wait_ge(phase_end, 5)

            def weight_hi(e, k):
                raw, parts = pieces[k]
                if k < 4:
                    act.wait_ge(w_in[k % 2], 16 * (e.n + 1))
                else:
                    act.wait_ge(w_in[2], 16 * (2 * e.n + k - 3))
                if k < 4:
                    wait(act, u_ps, e.back(1), 4 * (k // 2) + 3)
                else:
                    wait(act, down_ps, e.back(1), 1)
                act.activation(parts[HI], raw, ACT.Copy).then_inc(w_hi.sem, 1)

            for k in range(4):
                weight_hi(Batch(0), k)

            def gather(b):
                for d, bank in enumerate((pA, pB)):
                    wait(act, gather_ps, b, d)
                    settle(act)
                    act.activation(xin[HI][:, d, :, bass.ds(b.n * CAP, CAP)], bank[:, b.parity, :].rearrange("p (e s) -> p e s", e=NE),
                                   ACT.Copy).then_inc(xin_hi.sem, 1)

            pairs(act, gather, NB)

            def expert(e, e_next):
                for it in range(IT + 1):
                    if it < IT:
                        wait(act, g_ps, e, it)
                        wait(act, h_lo, e, it - 2)
                        act.activation(silu[:, it % 2, :], pA[:, it % 2, :], ACT.Silu).then_inc(silu_ok.sem, 1)
                    if it > 0:
                        wait(act, h_ok, e, it - 1)
                        act.activation(hT[HI][:, it - 1, :], silu[:, (it - 1) % 2, :], ACT.Copy).then_inc(h_hi.sem, 1)
                    if it in (1, 4):
                        weight_hi(e, 4 + it // 4)
                    if it in (5, 6) and e_next is not None:
                        weight_hi(e_next, it - 5)
                if e_next is not None:
                    weight_hi(e_next, 2)
                    weight_hi(e_next, 3)

            octet(act, expert)
            barrier(act, 2)
            slots(act, slot_of(1))
            barrier(act, 3)

            def weight1_hi(k):
                raw, parts = pieces1[k]
                act.activation(parts[HI], raw, ACT.Copy).then_inc(w1_hi, 1)

            def chunk_hi(c):
                act.activation(xc[HI][:], xnT_all[:, :, bass.ds(c.n * 512, 512)], ACT.Copy).then_inc(xc_hi.sem, 1)

            act.wait_ge(loaded["wl1"], 64)
            weight1_hi(0)
            chunk_hi(Batch(0))
            weight1_hi(1)
            act.wait_ge(r1, 3)
            act.activation(e1[:], lg1[:], ACT.Exp).then_inc(r1_act, 1)
            weight1_hi(2)

            def chunk(c, c_next):
                for i in range(5):
                    if i < 4:
                        wait(act, f1_ps, c, 2 * i)
                        wait(act, f1_lo, c, i - 2)
                        act.activation(sact[:, i % 2, :], pA[:, i % 2, :], ACT.Silu).then_inc(f1_act.sem, 1)
                        if c.turn is None and c.offset == 0:
                            weight1_hi(3 + i)
                    if i > 0:
                        wait(act, f1_h, c, i - 1)
                        dst = (hsT if i <= 2 else hrT)[HI][:, (i - 1) % 2, :]
                        wait(act, o1_ps, c.back(1), 19)
                        act.activation(dst, sact[:, (i - 1) % 2, :], ACT.Copy).then_inc(f1_hi.sem, 1)
                if c_next is not None:
                    wait(act, f1_ps, c, 7)
                    settle(act)
                    chunk_hi(c_next)

            quartet(act, chunk)

        @block.vector
        def _(dve):
            n_const = [0]

            def const(ins):
                n_const[0] += 1
                ins.then_inc(const_dve, 1)

            def v_const(count):
                for v in v_aug:
                    count(dve.memset(v[:, :, :, W:W + 1], 1.0))
                    count(dve.memset(v[:, :, :, W + 1:2 * W], 0.0))

            v_const(const)
            def mask_and_bias():
                dve.wait_ge(loaded["small"], 16 * N_SMALL)
                const(dve.tensor_scalar(bq_s[:], bq_s[:], SCALE, None, ALU.mult))
                const(dve.tensor_copy(maskr[:, 0, :], maski[:]))
                dve.wait_ge(const_dve, n_const[0])
                const(dve.tensor_scalar(maskr[:, 1, :], maskr[:, 0, :], 10000.0, -10000.0, ALU.mult, ALU.add))
                dve.wait_ge(const_dve, n_const[0])
                const(dve.tensor_copy(maskp[:, :, 0], maskr[:, 1, :]))
                dve.wait_ge(const_dve, n_const[0])
                const(dve.tensor_tensor(maskr[:, 2, :], maskr[:, 1, :], maskp[:, :, 0], ALU.subtract))
                dve.wait_ge(const_dve, n_const[0])
                const(dve.tensor_copy(maskp[:, :, 1], maskr[:, 2, :]))
                dve.wait_ge(const_dve, n_const[0])
                const(dve.tensor_tensor(maskp[:, :, 2], maskr[:, 2, :], maskp[:, :, 1], ALU.subtract))
                assert n_const[0] == N_CONST_DVE
                dve.wait_ge(const_dve, N_CONST_DVE)
                dve.wait_ge(const_pool, N_CONST_POOL)
                dve.wait_ge(const_act, N_CONST_ACT)

            def slot_of(layer):
                c = C[layer]

                when = WHEN["dve"]

                def inc(name):
                    return c[name].sem, 1

                def x_of(b):
                    return xs[:, bass.ds(b.n * TT, TT), :]

                def statistics(b, stt, mvv, stat, mv_name):
                    settle(dve)
                    for t in range(TT):
                        dve.bn_stats(stt[:, t, :], tile_of(b.n * TT + t)).then_inc(*inc(stat))
                    for t in range(TT):
                        wait(dve, c[stat], b, t)
                        settle(dve)
                        dve.bn_aggr(mvv[:, t, :], stt[:, t, :]).then_inc(*inc(mv_name))

                def normalise(b, dst, mvv, rss, name):
                    for t in range(TT):
                        dve.tensor_scalar(dst[:, t, :], tile_of(b.n * TT + t), mvv[:, t, 0:1],
                                          rss[:, 1, t:t + 1], ALU.subtract, ALU.mult).then_inc(*inc(name))

                def take_o(b, g):
                    wait(dve, c["pv"], b, g)
                    wait(dve, c["ott"], b.back(1))
                    dve.tensor_copy(o_t[:, g, :], pO[:, g % 2, :]).then_inc(*inc("ot"))

                def take_k(a, i):
                    wait(dve, c["kt_ps"], a, i)
                    wait(dve, c["b_ps"], a.back(2), 4 * i + 3)
                    dve.tensor_copy(k_t[a.parity][0:ROWS_B, 4 * i:4 * i + 4, :], turned(TURN_BANK[layer]["k", i], ROWS_B)).then_inc(*inc("kt"))

                def maximum(a, h):
                    wait(dve, c["a_ps"], a, h)
                    if layer == 0:
                        dve.tensor_reduce(mx[:, :, h], pA[:, h % 2, :].rearrange("p (t k) -> p t k", t=TT), AX, ALU.max)\
                           .then_inc(*inc("mx"))
                    else:
                        dve.tensor_reduce(mx[:, 0, h:h + 1], pA[:, h % 2, 0:P], AX, ALU.max)
                        dve.tensor_reduce(mx[:, 1, h:h + 1], pA[:, h % 2, P:P + S], AX, ALU.max).then_inc(*inc("mx"))

                def minus_maximum(a, i):
                    part = [q_nat[a.parity][:, :, 4 * i:4 * i + 4, NMAX0 + k] for k in range(3)]
                    m, rest = mx[:, :, 4 * i:4 * i + 4], mr[:, :, 4 * i:4 * i + 4]
                    wait(dve, c["mx"], a, 4 * i + 3)
                    dve.tensor_scalar(part[0], m, -1.0, None, ALU.mult).then_inc(*inc("m1"))
                    wait(dve, c["m1"], a, i)
                    dve.scalar_tensor_tensor(out=rest, in0=m, scalar=-1.0, in1=part[0], op0=ALU.mult, op1=ALU.subtract)\
                       .then_inc(*inc("mr"))
                    dve.scalar_tensor_tensor(out=part[1], in0=m, scalar=-1.0, in1=part[0], op0=ALU.mult, op1=ALU.subtract)\
                       .then_inc(*inc("m2"))
                    wait(dve, c["mr"], a, i)
                    wait(dve, c["m2"], a, i)
                    dve.tensor_tensor(part[2], rest, part[1], ALU.subtract).then_inc(*inc("m3"))

                def output(z):
                    o_ps = pM[:, 0:TT, :].rearrange("p t (h w) -> p t h w", w=2 * W)
                    wait(dve, c["ott"], z)
                    dve.reciprocal(rden[:, 0, :, :], o_ps[:, :, :, W]).then_inc(*inc("rden"))
                    wait(dve, c["rden"], z, 0)
                    dve.tensor_scalar(rden[:, 1, :, :], rden[:, 0, :, :], tg[:, layer:layer + 1], None, ALU.mult)\
                       .then_inc(*inc("rden"))
                    wait(dve, c["rden"], z, 1)
                    wait(dve, c["xres"], z.back(1))
                    dve.tensor_tensor(by_head(o_nat), o_ps[:, :, :, 0:W], bcast(rden[:, 1, :, :], 3, W), ALU.mult)\
                       .then_inc(*inc("o"))

                def take_kv(n, t):
                    wait(dve, c["kv_ps"], n, t)
                    wait(dve, c["kr"], n.back(1))
                    dve.tensor_tensor(k32[:, t, :], pM[:, t, 0:D], bk_s[:], ALU.add).then_inc(*inc("k32"))
                    wait(dve, c["vc"], n.back(1))
                    dve.tensor_tensor(v32[:, t, :], pM[:, t, D:2 * D], bv_s[:], ALU.add).then_inc(*inc("v"))

                def normalise_n(n, dst, used):
                    wait(dve, c["rs"], n, 1)
                    wait(dve, c[used], n.back(1))
                    normalise(n, dst, mv, rs, "xn")

                def go(n, a, b, z):
                    if n is not None and layer == 0:
                        if n.turn is None and n.offset < 2:
                            dve.wait_ge(loaded["x0"] if n.offset == 0 else loaded["x"], 16)
                        statistics(n, st, mv, "stat", "mv")
                    if a is not None and SECOND[layer] == "k":
                        take_k(a, 0)
                    if n is not None and layer == 0:
                        normalise_n(n, xn, "xnT_ps")
                        if n.turn is None and n.offset == 0:
                            mask_and_bias()
                    if z is not None and when["output"][layer] < 0:
                        output(z)
                    for h in range(NH):
                        if a is not None:
                            maximum(a, h)
                            if h % 4 == 3:
                                minus_maximum(a, h // 4)
                            if h in TURNS[layer] and TURNS[layer][h][0] == "k":
                                take_k(a, TURNS[layer][h][1])
                        if b is not None and h in when["o"][layer]:
                            take_o(b, when["o"][layer].index(h))
                        if z is not None:
                            if h == when["output"][layer]:
                                output(z)
                            if h == when["stat2"][layer]:
                                wait(dve, c["xres"], z)
                                statistics(z, st2, mv2, "stat2", "mv2")
                            if h == when["xn2"][layer]:
                                wait(dve, c["rs2"], z, 1)
                                wait(dve, c["x2T_ps"], z.back(1))
                                if layer == 0:
                                    wait(dve, c["sr"], z.back(1))
                                settle(dve)
                                normalise(z, xn_post, mv2, rs2, "xn2")
                            if h == when["lg"][layer]:
                                wait(dve, c["lg_ps"], z)
                                settle(dve)
                                if layer == 0:
                                    dst, src = lg[:, :, bass.ds(z.n, 1), :], pM[:, 1, 0:TT * NE].rearrange("p (t e) -> p t e", t=TT)
                                else:
                                    dst, src = lgT[:, bass.ds(z.n * S, S)], pM[0:NE1, 0, 0:S]
                                dve.tensor_copy(dst, src).then_inc(*inc("lg"))
                        if n is None:
                            continue
                        if layer == 1 and h == when["x2"][1]:
                            wait(dve, c["sc_ps"], n)
                            settle(dve)
                            x_n = xs[:, bass.ds(n.n * TT, TT), :]
                            dve.tensor_tensor(x_n, x_n, pM[:, 0, :].rearrange("p (t d) -> p t d", t=TT), ALU.add)\
                               .then_inc(*inc("x2"))
                        if layer == 1 and h == when["stat"][1]:
                            wait(dve, c["x2"], n)
                            statistics(n, st, mv, "stat", "mv")
                        if layer == 1 and h == when["xn"][1]:
                            normalise_n(n, q32, "qr")
                        if layer == 0:
                            if h == when["q32"][0]:
                                wait(dve, c["q_ps"], n)
                                wait(dve, c["qr"], n.back(1))
                                dve.scalar_tensor_tensor(out=q32[:], in0=pM[:, 1, :].rearrange("p (t d) -> p t d", t=TT),
                                                         scalar=SCALE, in1=bcast(bq_s[:], 1, TT), op0=ALU.mult, op1=ALU.add)\
                                   .then_inc(*inc("q32"))
                            if h in when["kv"][0]:
                                take_kv(n, when["kv"][0].index(h))
                            if h == when["kmask"][0]:
                                wait(dve, c["kt_ps"], n.back(2), 3)
                                settle(dve)
                                dve.tensor_copy(k_nat[n.parity][:, :, :, MASK0:NMAX0],
                                                bcast(maskp[:, bass.ds(n.n * TT, TT), :], 2, NH)).then_inc(*inc("kmask"))
                        if h == NEXT[layer] and FIRST[layer] == "k":
                            take_k(n, 0)
                    if b is not None:
                        take_o(b, 3)
                return go

            slots(dve, slot_of(0))
            arrive(dve)

            step = [0]

            def then(ins, sem_=route):
                step[0] += 1
                ins.then_inc(sem_, 1)
                dve.wait_ge(sem_, step[0])

            lg3 = lg[:].rearrange("p t b e -> p (t b) e")
            lgt3 = lgt[:].rearrange("p t b e -> p (t b) e")
            then(dve.tensor_reduce(lgs[:], lg3, AX, ALU.max))
            then(dve.tensor_tensor(lgt3, lg3, bcast(lgs[:], 2, NE), ALU.subtract))
            dve.wait_ge(route_act, 1)
            then(dve.tensor_reduce(lgs[:], lg3, AX, ALU.add))
            then(dve.reciprocal(lgs[:], lgs[:]))
            then(dve.tensor_tensor(lg3, lg3, bcast(lgs[:], 2, NE), ALU.mult))
            assert step[0] == 5
            dve.wait_ge(phase_end, 5)
            dve.wait_ge(route_pe, 1)
            then(dve.tensor_copy(top[0], pA[0:NB * NE, 0, 0:S]))
            for r in range(CAP // 8):
                then(dve.max(top8, top[r % 2]))
                then(dve.match_replace(top[1 - r % 2], top8, top[r % 2], -1.0))
            then(dve.tensor_scalar(selT, top[0], 0.0, None, ALU.is_lt))
            assert step[0] == 7 + CAP // 4
            dve.wait_ge(route_pe, 2)
            then(dve.tensor_copy(sel[:], pA[:, 1, 0:TT * NB * NE // 2].bitcast(BF16).rearrange("p (t n) -> p t n", t=TT)))
            dve.wait_ge(route_pe, 3)
            then(dve.tensor_tensor(slot[:], pB[:, 0, 0:TT * NB * NE].rearrange("p (t n) -> p t n", t=TT), sel[:], ALU.mult))

            def one_hot(b):
                for t in range(TT):
                    wait(dve, gather_ps, b.back(2), 1)
                    settle(dve)
                    dve.tensor_tensor(onehot[:, b.parity, t, :].rearrange("p (e s) -> p e s", e=NE),
                                      bcast(iota64[:], 1, NE), bcast(slot[:, t, bass.ds(b.n * NE, NE)], 2, CAP),
                                      ALU.is_equal).then_inc(onehot_ok.sem, 1)

            def gather(b, b_next):
                if b_next is not None:
                    one_hot(b_next)
                for d, bank in enumerate((pA, pB)):
                    wait(dve, xin_hi, b, d)
                    settle(dve)
                    at = bass.ds(b.n * CAP, CAP)
                    dve.tensor_tensor(xin[LO][:, d, :, at], bank[:, b.parity, :].rearrange("p (e s) -> p e s", e=NE),
                                      xin[HI][:, d, :, at], ALU.subtract).then_inc(xin_lo.sem, 1)

            one_hot(Batch(0))
            then(dve.tensor_scalar(lg3, lg3, tg[:, 2:3], None, ALU.mult))
            octet(dve, gather)

            def expert(e):
                for t in range(TT):
                    rows = gated[:, t, :].rearrange("p (e s) -> p e s", e=NE)
                    wait(dve, gt_ps, e.back(1), t)
                    settle(dve)
                    dve.tensor_tensor(rows, bcast(iota64[:], 1, NE), bcast(slot[:, t, bass.ds(e.n * NE, NE)], 2, CAP),
                                      ALU.is_equal).then_inc(gated_ok.sem, 1)
                    wait(dve, gated_ok, e, 2 * t)
                    settle(dve)
                    dve.tensor_tensor(rows, rows, bcast(lg[:, t, bass.ds(e.n, 1), :].rearrange("p o e -> p (o e)"), 2, CAP),
                                      ALU.mult).then_inc(gated_ok.sem, 1)
                for it in range(IT + 1):
                    if it < IT:
                        wait(dve, silu_ok, e, it)
                        wait(dve, u_ps, e, it)
                        dve.tensor_tensor(silu[:, it % 2, :], silu[:, it % 2, :], pB[:, it % 2, :], ALU.mult).then_inc(h_ok.sem, 1)
                    if it > 0:
                        wait(dve, h_hi, e, it - 1)
                        dve.tensor_tensor(hT[LO][:, it - 1, :], silu[:, (it - 1) % 2, :], hT[HI][:, it - 1, :], ALU.subtract)\
                           .then_inc(h_lo.sem, 1)
                for t in range(TT):
                    wait(dve, gt_ps, e, t)
                    settle(dve)
                    bank = pM[:, 2, :] if t == 0 else pO[:].rearrange("p a b -> p (a b)")
                    if e.turn is not None or e.offset > 0:
                        dve.wait_ge(gates_out[t], e.n * 16)
                    dve.tensor_copy(gt_s[:, t, :, :], bank.rearrange("p (q s) -> p q s", q=NPAIR)).then_inc(gt_ok.sem, 1)
                for h in range(2):
                    wait(dve, down_ps, e, h)
                    if e.turn is not None or e.offset > 0:
                        dve.wait_ge(y_out[h], e.n * 16)
                    dve.tensor_copy(y_s[:, h, :, :], pM[:, h, :].rearrange("p (q d) -> p q d", q=2)).then_inc(y_ready.sem, 1)

            pairs(dve, expert, NE)
            barrier(dve, 2)
            v_const(lambda ins: ins.then_inc(const_v1, 1))
            dve.wait_ge(const_v1, 4)
            slots(dve, slot_of(1))
            barrier(dve, 3)

            step[0] = 0

            def then1(ins):
                then(ins, r1)

            def chunk_lo(c):
                dve.tensor_tensor(xc[LO][:], xnT_all[:, :, bass.ds(c.n * 512, 512)], xc[HI][:], ALU.subtract).then_inc(xc_lo.sem, 1)

            dve.wait_ge(xc_hi.sem, 1)
            chunk_lo(Batch(0))
            dve.wait_ge(r1_pe, 1)
            then1(dve.tensor_tensor(lg1[:], pO[:, 0, 0:NT * NE1].rearrange("p (n e) -> p n e", n=NT), bcast(gb1[:], 1, NT), ALU.add))
            then1(dve.tensor_reduce(sm1[:], lg1[:], AX, ALU.max))
            then1(dve.tensor_tensor(lg1[:], lg1[:], bcast(sm1[:], 2, NE1), ALU.subtract))
            dve.wait_ge(r1_act, 1)
            then1(dve.tensor_reduce(sm1[:], e1[:], AX, ALU.add))
            then1(dve.reciprocal(sm1[:], sm1[:]))
            then1(dve.tensor_tensor(top1[:, :, 0:NE1], e1[:], bcast(sm1[:], 2, NE1), ALU.mult))
            then1(dve.memset(top1[:, :, NE1:2 * NE1], -2.0))
            then1(dve.memset(find[:, :, 2:8], -2.0))
            for n in range(NT):
                dve.max(best[:, n, :], top1[:, n, 0:NE1]).then_inc(r1, 1)
            step[0] += NT
            dve.wait_ge(r1, step[0])
            then1(dve.tensor_copy(find[:, :, 0:2], best[:, :, 0:2]))
            for n in range(NT):
                dve.match_replace(top1r[:, n, :], find[:, n, :], top1[:, n, :], -2.0).then_inc(r1, 1)
            step[0] += NT
            dve.wait_ge(r1, step[0])
            then1(dve.scalar_tensor_tensor(out=wd1[:], in0=top1r[:, :, 0:NE1], scalar=-1.0, in1=top1[:, :, 0:NE1],
                                           op0=ALU.is_lt, op1=ALU.mult))
            then1(dve.tensor_scalar(wd1[:], wd1[:], tg[:, 3:4], None, ALU.mult))

            def chunk(c, c_next):
                for i in range(5):
                    if i < 4:
                        wait(dve, f1_act, c, i)
                        wait(dve, f1_ps, c, 2 * i + 1)
                        dve.tensor_tensor(sact[:, i % 2, :], sact[:, i % 2, :], pB[:, i % 2, :], ALU.mult).then_inc(f1_h.sem, 1)
                    if i > 0:
                        parts = [q[:, (i - 1) % 2, :] for q in (hsT if i <= 2 else hrT)]
                        wait(dve, f1_hi, c, i - 1)
                        dve.tensor_tensor(parts[LO], sact[:, (i - 1) % 2, :], parts[HI], ALU.subtract).then_inc(f1_lo.sem, 1)
                if c_next is not None:
                    wait(dve, xc_hi, c_next)
                    settle(dve)
                    chunk_lo(c_next)
                settle(dve)
                dve.tensor_copy(wdc[:], wd1[:, bass.ds(c.n * 4, 4), :]).then_inc(wdc_ok.sem, 1)
                for t in range(4):
                    x_n, sum_t = tile_of(c.n * 4 + t), acc[t % 2][:]
                    wait(dve, o1_ps, c, (0, 1, 6, 11)[t])
                    settle(dve)
                    dve.scalar_tensor_tensor(out=sum_t, in0=pA[:, t % 2, 0:D], scalar=tg[:, 3:4], in1=x_n, op0=ALU.mult, op1=ALU.add)\
                       .then_inc(o1_acc.sem, 1)
                    if t == 0:
                        wait(dve, wdc_ok, c)
                    for e in range(NE1):
                        if e % 2 == 0:
                            wait(dve, o1_ps, c, (2, 7, 12, 16)[t] + e // 2)
                        wait(dve, o1_acc, c, 9 * t + e)
                        last = e == NE1 - 1
                        if last:
                            settle(dve)
                        dve.scalar_tensor_tensor(out=x_n if last else sum_t, in0=out_bank(e // 2)[:, e % 2 * D:(e % 2 + 1) * D],
                                                 scalar=wdc[:, t, e:e + 1], in1=sum_t, op0=ALU.mult, op1=ALU.add)\
                           .then_inc(o1_acc.sem, 1)
                    wait(dve, o1_acc, c, 9 * t + 8)
                    dve.sem_inc(out_ready, 1)

            quartet(dve, chunk)

        @block.tensor
        def _(pe):
            pe.wait_ge(const_pool, N_CONST_POOL)

            def slot_of(layer):
                c = C[layer]

                when = WHEN["pe"]

                def steps_at(name, h):
                    return [i for i, after in enumerate(when[name][layer]) if after == h]

                def turn_in(dst, src, ps_name):
                    for t in range(TT):
                        for d in range(DT):
                            last = pe.transpose(dst[:, d * S + t * P:d * S + (t + 1) * P], src[:, t, d * P:(d + 1) * P], ident[:])
                    last.then_inc(c[ps_name].sem, 1)

                def turn_stack(src, rows, i, bank, ps_name):
                    for hh in range(4):
                        for t in range(TT):
                            last = pe.transpose(pMb[0:rows, bank, hh * S + t * P:hh * S + (t + 1) * P],
                                                src[:, t, 4 * i + hh, 0:rows], identb[:])
                    last.then_inc(c[ps_name].sem, 1)

                def scores_q(a, h):
                    if h % 4 == 0:
                        wait(pe, c["qt"], a, h // 4)
                        wait(pe, c["kt"], a, h // 4)
                    wait(pe, c["mx"], a, h - 2)
                    kt = k_t[a.parity][0:ROWS_A, h, :]
                    if layer == 0:
                        for t in range(TT):
                            last = pe.matmul(pA[:, h % 2, t * S:(t + 1) * S], q_t[0:ROWS_A, h, t * P:(t + 1) * P], kt,
                                             start=True, stop=True)
                    else:
                        for t, lo in ((0, 0), (1, P)):
                            pe.matmul(pA[:, h % 2, lo:lo + (t + 1) * P], q_t[0:ROWS_A, h, t * P:(t + 1) * P],
                                      kt[:, 0:(t + 1) * P], start=True, stop=False, skip_group_check=True)
                            last = pe.matmul(pA[:, h % 2, lo + t * P:lo + (t + 1) * P], identb[:], causal_q[:],
                                             start=False, stop=True, skip_group_check=True)
                    last.then_inc(c["a_ps"].sem, 1)

                def scores_k(b, h):
                    if h % 4 == 0:
                        wait(pe, c["qtm"], b, h // 4)
                    wait(pe, c["p"], b, h - 2)
                    q = q_tm[0:ROWS_B, h, :]
                    if layer == 0:
                        for t in range(TT):
                            last = pe.matmul(pB[:, h % 2, t * S:(t + 1) * S], k_t[b.parity][0:ROWS_B, h, t * P:(t + 1) * P], q,
                                             start=True, stop=True)
                    else:
                        for t, lo in ((0, 0), (1, S)):
                            pe.matmul(pB[:, h % 2, lo:lo + S - t * P], k_t[b.parity][0:ROWS_B, h, t * P:(t + 1) * P],
                                      q[:, t * P:S], start=True, stop=False, skip_group_check=True)
                            last = pe.matmul(pB[:, h % 2, lo:lo + P], identb[:], causal_k[:],
                                             start=False, stop=True, skip_group_check=True)
                    last.then_inc(c["b_ps"].sem, 1)

                def values(b, g):
                    if g == 0:
                        wait(pe, c["vc"], b)
                    wait(pe, c["p"], b, 4 * g + 3)
                    wait(pe, c["ot"], b, g - 1)
                    for t in range(TT):
                        lo = 0 if layer == 0 else t * P
                        for hh in range(4):
                            last = pe.matmul(pO[32 * hh:32 * hh + 32, g % 2, lo:S], v_aug[b.parity][:, t, 4 * g + hh, :],
                                             probs[g % 2][:, hh, t * S:t * S + S - lo], start=(t == 0), stop=(t == TT - 1),
                                             skip_group_check=True)
                    last.then_inc(c["pv"].sem, 1)

                def turn(kind, a, i, free):
                    bank = TURN_BANK[layer][kind, i]
                    if bank in free:
                        name, a_before, i_before = free[bank]
                        wait(pe, c[name], a_before, i_before)
                    free[bank] = COPIED[kind], a, i
                    if kind == "m":
                        wait(pe, c["m3"], a, i)
                    elif i == 0:
                        wait(pe, c[kind + "3"], a)
                        if kind == "k" and layer == 0:
                            wait(pe, c["kmask"], a)
                    stacks = k_nat if kind == "k" else q_nat
                    turn_stack(stacks[a.parity], ROWS_A if kind == "q" else ROWS_B, i, bank, COPIED[kind] + "_ps")

                def go(n, a, b, z):
                    free = {}
                    if a is not None:
                        free[2] = COPIED[FIRST[layer]], a, 0
                    if b is not None:
                        free[2 - layer] = "qtm", b, 3
                    elif z is not None:
                        free[1] = "o", z.back(1), 0
                    if b is not None:
                        scores_k(b, 0)
                    if a is not None:
                        turn(SECOND[layer], a, 0, free)
                    if b is not None:
                        scores_k(b, 1)
                    def turn_output():
                        wait(pe, c["ot"], z, 3)
                        if layer == 1:
                            name, b_before, i_before = free[1]
                            wait(pe, c[name], b_before, i_before)
                            free[1] = "o", z, 0
                        if b is not None and z.offset + 2 < NB:
                            if layer == 0:
                                wait(pe, c["v"], Batch(z.offset + 2, z.turn), 1)
                            elif z.turn is not None or z.offset == 0:
                                wait(pe, c["x2"], Batch(z.offset + 2, z.turn))
                        wait(pe, c["x2T"], z.back(1))
                        wait(pe, c["lg"], z.back(1))
                        for t in range(TT):
                            for g in range(4):
                                last = pe.transpose(pM[:, t, g * P:(g + 1) * P], o_t[:, g, t * P:(t + 1) * P], ident[:])
                        last.then_inc(c["ott"].sem, 1)

                    if z is not None and when["output"][layer] < 0:
                        turn_output()
                    for h in range(NH):
                        if b is not None and h > 1:
                            scores_k(b, h)
                        if a is not None:
                            scores_q(a, h)
                            if h in TURNS[layer]:
                                kind, i = TURNS[layer][h]
                                turn(kind, a, i, free)
                        if h == NEXT[layer] and n is not None:
                            if layer == 1 and n.turn is None and n.offset == 0:
                                pe.wait_ge(const_l1, 6)
                                pe.wait_ge(const_v1, 4)
                            turn(FIRST[layer], n, 0, free)
                        if h in when["values"][layer] and b is not None:
                            values(b, when["values"][layer].index(h))
                        if z is not None and h == when["output"][layer]:
                            turn_output()
                        for i in steps_at("scatter", h) if n is not None else ():
                            t = i // 2
                            if i == 0:
                                if z is not None:
                                    wait(pe, c["o"], z)
                                else:
                                    wait(pe, c["x2"], n.back(1))
                                pe.wait_ge(ye_in[n.parity], 32 * (n.half + 1))
                                pe.wait_ge(gates_in[n.parity], 16 * (n.half + 1))
                            for q in range(i % 2 * NPAIR // 2, (i % 2 + 1) * NPAIR // 2):
                                last = pe.matmul(pM[:, 0, t * D:(t + 1) * D], gates_s[n.parity][:, q, t * P:(t + 1) * P],
                                                 ye_s[n.parity][:, q, :], start=(q == 0), stop=(q == NPAIR - 1))
                            if i == 3:
                                last.then_inc(c["sc_ps"].sem, 1)
                        if n is not None and layer == 0:
                            if h == when["xnT"][0]:
                                wait(pe, c["xn"], n, 1)
                                if z is not None:
                                    wait(pe, c["o"], z)
                                else:
                                    wait(pe, c["v"], n, -1)
                                turn_in(pM[:, 0, :], xn, "xnT_ps")
                            for t in steps_at("q", h):
                                if t == 0:
                                    if n.turn is None and n.offset == 0:
                                        pe.wait_ge(loaded["wqkv"], 32)
                                    wait(pe, c["xnT"], n)
                                for d in range(DT):
                                    last = pe.matmul(pM[:, 1, t * D:(t + 1) * D], xnT[:, d, t * P:(t + 1) * P], wq_s[:, d, :],
                                                     start=(d == 0), stop=(d == DT - 1))
                                if t == 1:
                                    last.then_inc(c["q_ps"].sem, 1)
                            for i in steps_at("kv", h):
                                t, d = i // DT, i % DT
                                if i == 0:
                                    pe.wait_ge(ctx_in[0][n.parity], 16 * (n.half + 1))
                                elif i == DT:
                                    wait(pe, c["q32"], n)
                                last = pe.matmul(pM[:, t, :], ctx_s[n.parity][:, d, t * P:(t + 1) * P], wkv_s[:, d, :],
                                                 start=(d == 0), stop=(d == DT - 1))
                                if d == DT - 1:
                                    last.then_inc(c["kv_ps"].sem, 1)
                        if z is not None and h == when["x2T"][layer]:
                            wait(pe, c["xn2"], z, 1)
                            if n is not None:
                                wait(pe, c["x2"] if layer else c["v"], n, 0)
                            else:
                                wait(pe, c["o"], z)
                            turn_in(pM[:, 0, :], xn_post, "x2T_ps")
                        if z is not None and layer == 1 and h == when["lg"][1]:
                            wait(pe, c["x2T"], z)
                            for d in range(DT):
                                last = pe.matmul(pM[0:NE1, 0, 0:S], gw1[:, d, :], xnT_all[:, d, bass.ds(z.n * S, S)],
                                                 start=(d == 0), stop=(d == DT - 1))
                            last.then_inc(c["lg_ps"].sem, 1)
                        if z is not None and layer == 0 and h == when["lg"][0]:
                            wait(pe, c["x2T"], z)
                            if n is not None:
                                wait(pe, c["v"], n, 1)
                            for t in range(TT):
                                for d in range(DT):
                                    last = pe.matmul(pM[:, 1, t * NE:(t + 1) * NE], xnT_post[:, d, t * P:(t + 1) * P],
                                                     gw0[:, d, :], start=(d == 0), stop=(d == DT - 1))
                            last.then_inc(c["lg_ps"].sem, 1)
                    if b is not None:
                        values(b, 3)
                    if a is not None:
                        turn("m", a, 3, free)
                return go

            slots(pe, slot_of(0))
            arrive(pe)

            pe.wait_ge(route, 5)
            for t in range(TT):
                last = pe.transpose(pA[0:NB * NE, 0, t * P:(t + 1) * P], lg[:, t, :, :].rearrange("p b e -> p (b e)"), ident[:])
            last.then_inc(route_pe, 1)
            pe.wait_ge(phase_end, 5)
            pe.wait_ge(route, 7 + CAP // 4)
            for t in range(TT):
                last = pe.transpose(pA[:, 1, 0:TT * NB * NE // 2].bitcast(BF16)[:, t * NB * NE:(t + 1) * NB * NE],
                                    selT[:, t * P:(t + 1) * P], identb[0:NB * NE, 0:NB * NE])
            last.then_inc(route_pe, 1)
            pe.wait_ge(route, 8 + CAP // 4)
            n = NB * NE
            pe.matmul(pB[:, 0, 0:n], upper[:], sel[:, 0, :], start=True, stop=True)
            pe.matmul(pB[:, 0, n:2 * n], onesb[:], sel[:, 0, :], start=True, stop=False)
            pe.matmul(pB[:, 0, n:2 * n], upper[:], sel[:, 1, :], start=False, stop=True).then_inc(route_pe, 1)

            def gather(b):
                for d, bank in enumerate((pA, pB)):
                    wait(pe, xin_lo, b.back(2), d)
                    for t in range(TT):
                        if d == 0:
                            wait(pe, onehot_ok, b, t)
                        for i in range(3):
                            last = pe.matmul(bank[:, b.parity, :],
                                             xn2s[:, bass.ds(b.n * TT + t, 1), i, d * P:(d + 1) * P].rearrange("p o d -> p (o d)"),
                                             onehot[:, b.parity, t, :],
                                             start=(t == 0 and i == 0), stop=(t == TT - 1 and i == 2))
                    last.then_inc(gather_ps.sem, 1)

            pairs(pe, gather, NB)

            def expert(e):
                if e.turn is None and e.offset == 0:
                    pe.wait_ge(xin_lo.sem, 2 * NB)
                for it in range(IT):
                    if it in (0, 4):
                        wait(pe, w_lo, e, it // 2 + 1)
                    for w, bank, free, ps in ((wg_p, pA, silu_ok, g_ps), (wu_p, pB, h_ok, u_ps)):
                        wait(pe, free, e, it - 2)
                        for d in range(DT):
                            for i, (ws, xm) in enumerate(PRODUCTS):
                                last = pe.matmul(bank[:, it % 2, :], w[ws][:, d, it * P:(it + 1) * P],
                                                 xin[xm][:, d, bass.ds(e.n, 1), :].rearrange("p o s -> p (o s)"),
                                                 start=(d == 0 and i == 0), stop=(d == DT - 1 and i == 2))
                        last.then_inc(ps.sem, 1)
                for t in range(TT):
                    wait(pe, gated_ok, e, 2 * t + 1)
                    wait(pe, gt_ok, e.back(1), t)
                    bank = pM[:, 2, :] if t == 0 else pO[:].rearrange("p a b -> p (a b)")
                    for q in range(NPAIR):
                        last = pe.transpose(bank[:, q * P:(q + 1) * P], gated[:, t, q * P:(q + 1) * P], ident[:])
                    last.then_inc(gt_ps.sem, 1)
                wait(pe, w_lo, e, 5)
                for h in range(2):
                    wait(pe, y_ready, e.back(1), h)
                    for q in range(2):
                        tt = 2 * h + q
                        for it in range(IT):
                            if tt == 0 and it in (0, IT - 2, IT - 1):
                                wait(pe, h_lo, e, max(it, IT - 3))
                            for i, (hs, wm) in enumerate(PRODUCTS):
                                last = pe.matmul(pM[:, h, q * D:(q + 1) * D], hT[hs][:, it, tt * P:(tt + 1) * P], wd_p[wm][:, it, :],
                                                 start=(it == 0 and i == 0), stop=(it == IT - 1 and i == 2))
                    last.then_inc(down_ps.sem, 1)

            pairs(pe, expert, NE)
            barrier(pe, 2)
            slots(pe, slot_of(1))
            barrier(pe, 3)

            for n in range(NT):
                last = pe.transpose(pO[:, 0, n * NE1:(n + 1) * NE1], lgT[:, n * P:(n + 1) * P], ident[0:NE1, 0:NE1])
            last.then_inc(r1_pe, 1)

            def product(dst, stationary, moving, inner):
                for k in range(inner):
                    for i, (a, b) in enumerate(PRODUCTS):
                        last = pe.matmul(dst, stationary(a, k), moving(b, k), start=(k == 0 and i == 0), stop=(k == inner - 1 and i == 2))
                return last

            def chunk(c, c_next):
                first = c.turn is None and c.offset == 0
                wait(pe, xc_lo, c)
                for i in range(4):
                    w, f = (wsi_p, i) if i < 2 else (w1_p, i - 2)
                    if first and i in (0, 2):
                        pe.wait_ge(w1_lo, 1 + i // 2)
                    wait(pe, f1_act, c, i - 2)
                    wait(pe, f1_h, c, i - 2)
                    if i < 2:
                        wait(pe, o1_acc, c.back(1), 9 * (2 + i))
                    for k, bank in enumerate((pA, pB)):
                        lo = k * H1 + f * P
                        product(bank[:, i % 2, :], lambda a, d: w[a][:, d, lo:lo + P], lambda b, d: xc[b][:, d, :], DT)\
                            .then_inc(f1_ps.sem, 1)
                def shared(t):
                    if t < 2:
                        wait(pe, f1_act, c, 2 + t)
                    if t == 0:
                        wait(pe, f1_lo, c, 1)
                        if first:
                            pe.wait_ge(w1_lo, 3)
                    else:
                        wait(pe, o1_acc, c, 9 * (t - 2))
                    product(pA[:, t % 2, 0:D], lambda a, k: hsT[a][:, k, t * P:(t + 1) * P], lambda b, k: wso_p[b][:, k, :], 2)\
                        .then_inc(o1_ps.sem, 1)

                def experts(t):
                    if t == 0:
                        wait(pe, f1_lo, c, 3)
                    for q in range(4):
                        if first and t == 0:
                            pe.wait_ge(w1_lo, 4 + q)
                            if q == 3:
                                pe.wait_ge(r1, 1)
                        wait(pe, o1_acc, c, 9 * (t - 1) + 2 * q + 2)
                        product(out_bank(q), lambda a, k: hrT[a][:, k, t * P:(t + 1) * P],
                                lambda b, k: w2_p[b][:, k, 2 * q:2 * q + 2, :].rearrange("p e d -> p (e d)"), 2)\
                            .then_inc(o1_ps.sem, 1)

                shared(0)
                shared(1)
                for t in range(4):
                    experts(t)
                    if t < 2:
                        shared(t + 2)

            quartet(pe, chunk)


def kernel(x, ctx_1024, mask_BxS2_ik0, g_xattn, g_ffn, L0_xattn_Wq, L0_xattn_bq, L0_xattn_Wk, L0_xattn_bk,
           L0_xattn_Wv, L0_xattn_bv, L0_ffn_gate_w, L0_ffn_w_gate, L0_ffn_w_up, L0_ffn_w_down, L1_ffn_w_shared_in,
           L1_ffn_w_shared_out, L1_ffn_w1_shared, L1_ffn_w2, L1_ffn_w_gate, L1_ffn_gate_bias):
    import numpy as np
    import concourse.bacc as bacc
    from concourse.bass_utils import run_bass_kernel_spmd

    def rows(a):
        return np.ascontiguousarray(a.reshape(-1, P, a.shape[-1]).transpose(1, 0, 2))

    def turned_rows(a):
        return np.ascontiguousarray(a.reshape(a.shape[0], a.shape[1], -1, P).transpose(0, 3, 2, 1))

    a = {k: np.asarray(v) for k, v in locals().items() if k in INPUTS}
    arrays = {
        "x": rows(a["x"].reshape(NB * S, D)),
        "ctx": np.ascontiguousarray(a["ctx_1024"].reshape(NB, TT, P, D).transpose(0, 2, 1, 3)),
        "ctxT": turned_rows(a["ctx_1024"]),
        "mask": np.ascontiguousarray(a["mask_BxS2_ik0"].reshape(NT, P).T),
        "g_xattn": a["g_xattn"], "g_ffn": a["g_ffn"],
        "wq": rows(a["L0_xattn_Wq"].T),
        "wkv": rows(np.concatenate([a["L0_xattn_Wk"].T, a["L0_xattn_Wv"].T], axis=1)),
        "bq": a["L0_xattn_bq"], "bk": a["L0_xattn_bk"], "bv": a["L0_xattn_bv"],
        "gate0": rows(a["L0_ffn_gate_w"].T),
        "w_gate": turned_rows(a["L0_ffn_w_gate"]), "w_up": turned_rows(a["L0_ffn_w_up"]),
        "w_down": turned_rows(a["L0_ffn_w_down"]),
        "ws_in": rows(a["L1_ffn_w_shared_in"]), "ws_out": rows(a["L1_ffn_w_shared_out"]),
        "w1s": rows(a["L1_ffn_w1_shared"]),
        "w2": np.ascontiguousarray(a["L1_ffn_w2"].reshape(NE1, 2, P, D).transpose(2, 1, 0, 3)),
        "wg1": rows(a["L1_ffn_w_gate"]), "gbias": a["L1_ffn_gate_bias"],
    }
    nc = bacc.Bacc("TRN2", target_bir_lowering=False, num_devices=1)
    ins = {n: nc.dram_tensor(f"in_{n}", v.shape, mybir.dt.from_np(v.dtype), kind="ExternalInput").ap()
           for n, v in arrays.items()}
    out = nc.dram_tensor("out", (P, NT, D), F32, kind="ExternalOutput").ap()
    build_program(nc, out=out, **ins)
    r = run_bass_kernel_spmd(nc, [{f"in_{n}": v for n, v in arrays.items()}], core_ids=[0])
    got = np.asarray(r.results[0]["out"])
    return np.ascontiguousarray(got.transpose(1, 0, 2)).reshape(NB, S, D)


INPUTS = ("x", "ctx_1024", "mask_BxS2_ik0", "g_xattn", "g_ffn", "L0_xattn_Wq", "L0_xattn_bq", "L0_xattn_Wk",
          "L0_xattn_bk", "L0_xattn_Wv", "L0_xattn_bv", "L0_ffn_gate_w", "L0_ffn_w_gate", "L0_ffn_w_up",
          "L0_ffn_w_down", "L1_ffn_w_shared_in", "L1_ffn_w_shared_out", "L1_ffn_w1_shared", "L1_ffn_w2",
          "L1_ffn_w_gate", "L1_ffn_gate_bias")
```
